# Optimizing a Trainium2 kernel written in Bass

```python
import numpy as np
import jax
import jax.numpy as jnp

def _softmax(x, axis=-1):
    return jax.nn.softmax(x, axis=axis)

def _gelu(x):
    return jax.nn.gelu(x, approximate=True)

def _silu(x):
    return jax.nn.silu(x)

def _sigmoid(x):
    return jax.nn.sigmoid(x)

def _layernorm(x, axis=-1, eps=1e-05):
    m = jnp.mean(x, axis=axis, keepdims=True)
    v = jnp.var(x, axis=axis, keepdims=True)
    return (x - m) / jnp.sqrt(v + eps)

def _scatter_add(tgt, idx, src, axis=0):
    return tgt.at[idx].add(src)

def _segment_sum(src, seg, n):
    return jax.ops.segment_sum(src, seg, n)
kernel_name = 'mk_hybrid_d2_jaxref_r8_569aa2'

def setup_inputs(seed: int=0):
    np.random.seed(seed)
    _w = jnp.asarray

    def _L0_attn_a_setup():
        import jax, jax.numpy as jnp
        import numpy as np
        from jax import lax
        EPS = 1e-05

        def layer_norm(x, w, b):
            mu = x.mean(-1, keepdims=True)
            var = ((x - mu) ** 2).mean(-1, keepdims=True)
            return (x - mu) * lax.rsqrt(var + EPS) * w + b

        def causal_dw_conv(x, w, b):
            B, L, D = x.shape
            K = w.shape[1]
            xt = jnp.pad(x.transpose(0, 2, 1), ((0, 0), (0, 0), (K - 1, 0)))
            y = lax.conv_general_dilated(xt, w[:, None, :], (1,), 'VALID', dimension_numbers=('NCH', 'OIH', 'NCH'), feature_group_count=D)
            return (y + b[:, None]).transpose(0, 2, 1)

        def mamba_block(x, ln_w, ln_b, W_in, b_in, conv_w, conv_b, W_xproj, W_dt, b_dt, A_log, Dp, W_out, b_out):
            res = x
            x = layer_norm(x, ln_w, ln_b)
            xz = x @ W_in + b_in
            Di = xz.shape[-1] // 2
            xp, z = (xz[..., :Di], xz[..., Di:])
            xp = jax.nn.silu(causal_dw_conv(xp, conv_w, conv_b))
            dbl = xp @ W_xproj
            N = A_log.shape[-1]
            R = dbl.shape[-1] - 2 * N
            dt, Bm, Cm = (dbl[..., :R], dbl[..., R:R + N], dbl[..., R + N:])
            delta = jax.nn.softplus(dt @ W_dt + b_dt)
            A = -jnp.exp(A_log)
            dA = jnp.exp(delta[..., None] * A)
            dBx = delta[..., None] * Bm[:, :, None, :] * xp[..., None]

            def step(h, inp):
                dAt, dBxt, ct = inp
                h = dAt * h + dBxt
                return (h, jnp.einsum('bdn,bn->bd', h, ct))
            h0 = jnp.zeros((x.shape[0], Di, N), x.dtype)
            _, ys = lax.scan(step, h0, (dA.transpose(1, 0, 2, 3), dBx.transpose(1, 0, 2, 3), Cm.transpose(1, 0, 2)))
            y = ys.transpose(1, 0, 2) + xp * Dp
            y = y * jax.nn.silu(z)
            return res + y @ W_out + b_out
        B, L, Dm = (2, 128, 128)
        Di, N, R, K = (256, 16, 64, 4)
        key = jax.random.key(seed)
        ks = jax.random.split(key, 12)
        s_in = 1.0 / np.sqrt(Dm)
        s_di = 1.0 / np.sqrt(Di)
        A = jnp.broadcast_to(jnp.arange(1, N + 1, dtype=jnp.float32), (Di, N))
        return {'x': jax.random.normal(ks[0], (B, L, Dm), jnp.float32), 'ln_w': jnp.ones((2, Dm), jnp.float32), 'ln_b': jnp.zeros((2, Dm), jnp.float32), 'W_in': jax.random.normal(ks[1], (2, Dm, 2 * Di), jnp.float32) * s_in, 'b_in': jnp.zeros((2, 2 * Di), jnp.float32), 'conv_w': jax.random.normal(ks[2], (2, Di, K), jnp.float32) * 0.5, 'conv_b': jnp.zeros((2, Di), jnp.float32), 'W_xproj': jax.random.normal(ks[3], (2, Di, R + 2 * N), jnp.float32) * s_di, 'W_dt': jax.random.normal(ks[4], (2, R, Di), jnp.float32) * 0.02, 'b_dt': jnp.full((2, Di), -4.6, jnp.float32) + 0.1 * jax.random.normal(ks[5], (2, Di), jnp.float32), 'A_log': jnp.log(jnp.stack([A, A])), 'D': jnp.ones((2, Di), jnp.float32), 'W_out': jax.random.normal(ks[6], (2, Di, Dm), jnp.float32) * s_di, 'b_out': jnp.zeros((2, Dm), jnp.float32), 'Wg': jax.random.normal(ks[7], (2 * Dm, Dm), jnp.float32) / np.sqrt(2 * Dm), 'bg': jnp.zeros((Dm,), jnp.float32), 'Wv': jax.random.normal(ks[8], (2 * Dm, Dm), jnp.float32) / np.sqrt(2 * Dm), 'bv': jnp.zeros((Dm,), jnp.float32)}
    _L0_attn_a_in = _L0_attn_a_setup()

    def _L0_attn_b_setup():
        import jax, jax.numpy as jnp
        import numpy as np
        NUM_HEADS = 16
        EPS = 1e-06

        def elu_plus_one(x):
            return jax.nn.elu(x) + 1.0
        key = jax.random.key(seed)
        ks = jax.random.split(key, 9)
        B, L, E = (4, 512, 128)
        s = 1.0 / np.sqrt(E)
        return {'query': jax.random.normal(ks[0], (B, L, E), jnp.float32), 'Wq': jax.random.normal(ks[1], (E, E), jnp.float32) * s, 'bq': jax.random.normal(ks[2], (E,), jnp.float32) * 0.01, 'Wk': jax.random.normal(ks[3], (E, E), jnp.float32) * s, 'bk': jax.random.normal(ks[4], (E,), jnp.float32) * 0.01, 'Wv': jax.random.normal(ks[5], (E, E), jnp.float32) * s, 'bv': jax.random.normal(ks[6], (E,), jnp.float32) * 0.01, 'Wo': jax.random.normal(ks[7], (E, E), jnp.float32) * s, 'bo': jax.random.normal(ks[8], (E,), jnp.float32) * 0.01}
    _L0_attn_b_in = _L0_attn_b_setup()

    def _L0_ffn_setup():
        import jax, jax.numpy as jnp
        import numpy as np
        DIM = 128
        E = 8
        K = 2
        EPS = 1e-05

        def _ln(x, g, b):
            mu = jnp.mean(x, axis=-1, keepdims=True)
            var = jnp.mean(jnp.square(x - mu), axis=-1, keepdims=True)
            return (x - mu) * jax.lax.rsqrt(var + EPS) * g + b
        key = jax.random.key(seed)
        ks = jax.random.split(key, 8)
        H = 2 * DIM
        s_in = 1.0 / np.sqrt(DIM)
        s_h = 1.0 / np.sqrt(H)
        return {'x': jax.random.normal(ks[0], (2, 256, DIM), dtype=jnp.float32), 'gate_w': jax.random.uniform(ks[1], (DIM, E), minval=-s_in, maxval=s_in, dtype=jnp.float32), 'w1': jax.random.uniform(ks[2], (E, DIM, H), minval=-s_in, maxval=s_in, dtype=jnp.float32), 'b1': jax.random.uniform(ks[3], (E, H), minval=-s_in, maxval=s_in, dtype=jnp.float32), 'ln1_g': jnp.ones((E, H), dtype=jnp.float32), 'ln1_b': jnp.zeros((E, H), dtype=jnp.float32), 'w2': jax.random.uniform(ks[4], (E, H, DIM), minval=-s_h, maxval=s_h, dtype=jnp.float32), 'b2': jax.random.uniform(ks[5], (E, DIM), minval=-s_h, maxval=s_h, dtype=jnp.float32), 'ln_g': jnp.ones((DIM,), dtype=jnp.float32), 'ln_b': jnp.zeros((DIM,), dtype=jnp.float32)}
    _L0_ffn_in = _L0_ffn_setup()

    def _L1_attn_a_setup():
        import jax, jax.numpy as jnp
        import numpy as np
        EMBED_DIM = 128
        NUM_HEADS = 16
        HEAD_DIM = EMBED_DIM // NUM_HEADS
        SCALING = HEAD_DIM ** (-0.5)
        EPS = 1e-05

        def _rope(seq_len):
            inv_freq = 1.0 / 10000.0 ** (jnp.arange(0, HEAD_DIM, 2, dtype=jnp.float32) / HEAD_DIM)
            freqs = jnp.arange(seq_len, dtype=jnp.float32)[:, None] * inv_freq[None, :]
            emb = jnp.concatenate([freqs, freqs], axis=-1)
            return (jnp.cos(emb), jnp.sin(emb))

        def _rotate(x, cos, sin):
            d = x.shape[-1]
            x1, x2 = (x[..., :d // 2], x[..., d // 2:])
            rotated = jnp.concatenate([-x2, x1], axis=-1)
            return x * cos + rotated * sin
        key = jax.random.key(seed)
        ks = jax.random.split(key, 6)
        B, S, D = (2, 256, EMBED_DIM)
        scale = D ** (-0.5)
        return {'x': jax.random.normal(ks[0], (B, S, D), jnp.float32), 'Wq': jax.random.normal(ks[1], (D, D), jnp.float32) * scale, 'Wk': jax.random.normal(ks[2], (D, D), jnp.float32) * scale, 'Wv': jax.random.normal(ks[3], (D, D), jnp.float32) * scale, 'Wg': jax.random.normal(ks[4], (D, D), jnp.float32) * scale, 'Wo': jax.random.normal(ks[5], (D, D), jnp.float32) * scale, 'gn_w': jnp.ones((D,), jnp.float32), 'gn_b': jnp.zeros((D,), jnp.float32)}
    _L1_attn_a_in = _L1_attn_a_setup()

    def _L1_attn_b_setup():
        import jax, jax.numpy as jnp
        import numpy as np
        import math
        B, S, E = (2, 256, 128)
        H, DC, DR = (16, 32, 128)
        HD = E // H

        def _linear_params(key, din, dout):
            k1, k2 = jax.random.split(key)
            bound = 1.0 / math.sqrt(din)
            w = jax.random.uniform(k1, (din, dout), minval=-bound, maxval=bound, dtype=jnp.float32)
            b = jax.random.uniform(k2, (dout,), minval=-bound, maxval=bound, dtype=jnp.float32)
            return (w, b)

        def _gelu(x):
            return jax.nn.gelu(x, approximate=False)

        def _rope_cos_sin(seq_len, d_rope):
            inv_freq = 1.0 / 10000.0 ** (jnp.arange(0, d_rope, 2, dtype=jnp.float32) / d_rope)
            t = jnp.arange(seq_len, dtype=jnp.float32)
            freqs = t[:, None] * inv_freq[None, :]
            emb = jnp.concatenate([freqs, freqs], axis=-1)
            return (jnp.cos(emb), jnp.sin(emb))

        def _apply_rope(x, cos, sin):
            d = x.shape[-1]
            x1, x2 = (x[..., :d // 2], x[..., d // 2:])
            rot = jnp.concatenate([-x2, x1], axis=-1)
            return x * cos + rot * sin
        key = jax.random.key(seed)
        ks = jax.random.split(key, 10)
        x = jax.random.normal(ks[0], (B, S, E), dtype=jnp.float32)
        wq, bq = _linear_params(ks[1], E, DC)
        wqc, bqc = _linear_params(ks[2], DC, E - DR)
        wqr, bqr = _linear_params(ks[3], E, DR)
        wkv, bkv = _linear_params(ks[4], E, DC)
        wkr, bkr = _linear_params(ks[5], E, DR)
        wkc, bkc = _linear_params(ks[6], DC, E - DR)
        wv, bv = _linear_params(ks[7], DC, E)
        wo, bo = _linear_params(ks[8], E, E)
        return dict(x=x, wq=wq, bq=bq, wqc=wqc, bqc=bqc, wqr=wqr, bqr=bqr, wkv=wkv, bkv=bkv, wkr=wkr, bkr=bkr, wkc=wkc, bkc=bkc, wv=wv, bv=bv, wo=wo, bo=bo)
    _L1_attn_b_in = _L1_attn_b_setup()

    def _L1_ffn_setup():
        import jax, jax.numpy as jnp
        import numpy as np
        B, S, D, H, F, E = (2, 128, 128, 16, 512, 8)
        HD = D // H
        EPS = 1e-06

        def _layernorm(x, g, b):
            m = jnp.mean(x, axis=-1, keepdims=True)
            v = jnp.var(x, axis=-1, keepdims=True)
            return (x - m) / jnp.sqrt(v + EPS) * g + b
        key = jax.random.key(seed)
        ks = jax.random.split(key, 10)
        sc = 0.02
        x = jax.random.normal(ks[0], (B, S, D), jnp.float32)
        Wq = jax.random.normal(ks[1], (D, D), jnp.float32) * sc
        Wk = jax.random.normal(ks[2], (D, D), jnp.float32) * sc
        Wv = jax.random.normal(ks[3], (D, D), jnp.float32) * sc
        Wo = jax.random.normal(ks[4], (D, D), jnp.float32) * sc
        bo = jnp.zeros((D,), jnp.float32)
        Wr = jax.random.normal(ks[5], (D, E), jnp.float32) * sc
        We1 = jax.random.normal(ks[6], (E, D, F), jnp.float32) * sc
        be1 = jnp.zeros((E, F), jnp.float32)
        We2 = jax.random.normal(ks[7], (E, F, D), jnp.float32) * sc
        be2 = jnp.zeros((E, D), jnp.float32)
        ln1_g = jnp.ones((D,), jnp.float32)
        ln1_b = jnp.zeros((D,), jnp.float32)
        ln2_g = jnp.ones((D,), jnp.float32)
        ln2_b = jnp.zeros((D,), jnp.float32)
        return {'x': x, 'Wq': Wq, 'Wk': Wk, 'Wv': Wv, 'Wo': Wo, 'bo': bo, 'Wr': Wr, 'We1': We1, 'be1': be1, 'We2': We2, 'be2': be2, 'ln1_g': ln1_g, 'ln1_b': ln1_b, 'ln2_g': ln2_g, 'ln2_b': ln2_b}
    _L1_ffn_in = _L1_ffn_setup()
    _d = {'L0_attn_a_x': _L0_attn_a_in['x'], 'L0_attn_a_ln_w': _L0_attn_a_in['ln_w'], 'L0_attn_a_ln_b': _L0_attn_a_in['ln_b'], 'L0_attn_a_W_in': _L0_attn_a_in['W_in'], 'L0_attn_a_b_in': _L0_attn_a_in['b_in'], 'L0_attn_a_conv_w': _L0_attn_a_in['conv_w'], 'L0_attn_a_conv_b': _L0_attn_a_in['conv_b'], 'L0_attn_a_W_xproj': _L0_attn_a_in['W_xproj'], 'L0_attn_a_W_dt': _L0_attn_a_in['W_dt'], 'L0_attn_a_b_dt': _L0_attn_a_in['b_dt'], 'L0_attn_a_A_log': _L0_attn_a_in['A_log'], 'L0_attn_a_D': _L0_attn_a_in['D'], 'L0_attn_a_W_out': _L0_attn_a_in['W_out'], 'L0_attn_a_b_out': _L0_attn_a_in['b_out'], 'L0_attn_a_Wg': _L0_attn_a_in['Wg'], 'L0_attn_a_bg': _L0_attn_a_in['bg'], 'L0_attn_a_Wv': _L0_attn_a_in['Wv'], 'L0_attn_a_bv': _L0_attn_a_in['bv'], 'L0_attn_b_Wq': _L0_attn_b_in['Wq'], 'L0_attn_b_bq': _L0_attn_b_in['bq'], 'L0_attn_b_Wk': _L0_attn_b_in['Wk'], 'L0_attn_b_bk': _L0_attn_b_in['bk'], 'L0_attn_b_Wv': _L0_attn_b_in['Wv'], 'L0_attn_b_bv': _L0_attn_b_in['bv'], 'L0_attn_b_Wo': _L0_attn_b_in['Wo'], 'L0_attn_b_bo': _L0_attn_b_in['bo'], 'L0_ffn_gate_w': _L0_ffn_in['gate_w'], 'L0_ffn_w1': _L0_ffn_in['w1'], 'L0_ffn_b1': _L0_ffn_in['b1'], 'L0_ffn_ln1_g': _L0_ffn_in['ln1_g'], 'L0_ffn_ln1_b': _L0_ffn_in['ln1_b'], 'L0_ffn_w2': _L0_ffn_in['w2'], 'L0_ffn_b2': _L0_ffn_in['b2'], 'L0_ffn_ln_g': _L0_ffn_in['ln_g'], 'L0_ffn_ln_b': _L0_ffn_in['ln_b'], 'L1_attn_a_Wq': _L1_attn_a_in['Wq'], 'L1_attn_a_Wk': _L1_attn_a_in['Wk'], 'L1_attn_a_Wv': _L1_attn_a_in['Wv'], 'L1_attn_a_Wg': _L1_attn_a_in['Wg'], 'L1_attn_a_Wo': _L1_attn_a_in['Wo'], 'L1_attn_a_gn_w': _L1_attn_a_in['gn_w'], 'L1_attn_a_gn_b': _L1_attn_a_in['gn_b'], 'L1_attn_b_wq': _L1_attn_b_in['wq'], 'L1_attn_b_bq': _L1_attn_b_in['bq'], 'L1_attn_b_wqc': _L1_attn_b_in['wqc'], 'L1_attn_b_bqc': _L1_attn_b_in['bqc'], 'L1_attn_b_wqr': _L1_attn_b_in['wqr'], 'L1_attn_b_bqr': _L1_attn_b_in['bqr'], 'L1_attn_b_wkv': _L1_attn_b_in['wkv'], 'L1_attn_b_bkv': _L1_attn_b_in['bkv'], 'L1_attn_b_wkr': _L1_attn_b_in['wkr'], 'L1_attn_b_bkr': _L1_attn_b_in['bkr'], 'L1_attn_b_wkc': _L1_attn_b_in['wkc'], 'L1_attn_b_bkc': _L1_attn_b_in['bkc'], 'L1_attn_b_wv': _L1_attn_b_in['wv'], 'L1_attn_b_bv': _L1_attn_b_in['bv'], 'L1_attn_b_wo': _L1_attn_b_in['wo'], 'L1_attn_b_bo': _L1_attn_b_in['bo'], 'L1_ffn_Wq': _L1_ffn_in['Wq'], 'L1_ffn_Wk': _L1_ffn_in['Wk'], 'L1_ffn_Wv': _L1_ffn_in['Wv'], 'L1_ffn_Wo': _L1_ffn_in['Wo'], 'L1_ffn_bo': _L1_ffn_in['bo'], 'L1_ffn_Wr': _L1_ffn_in['Wr'], 'L1_ffn_We1': _L1_ffn_in['We1'], 'L1_ffn_be1': _L1_ffn_in['be1'], 'L1_ffn_We2': _L1_ffn_in['We2'], 'L1_ffn_be2': _L1_ffn_in['be2'], 'L1_ffn_ln1_g': _L1_ffn_in['ln1_g'], 'L1_ffn_ln1_b': _L1_ffn_in['ln1_b'], 'L1_ffn_ln2_g': _L1_ffn_in['ln2_g'], 'L1_ffn_ln2_b': _L1_ffn_in['ln2_b']}
    _x0 = _d['L0_attn_a_x']
    _d['L0_attn_a_x'] = jax.random.normal(jax.random.fold_in(jax.random.key(seed), 1), (8, 512, 128), dtype=_x0.dtype)
    del _x0
    return _d

def reference(L0_attn_a_x, L0_attn_a_ln_w, L0_attn_a_ln_b, L0_attn_a_W_in, L0_attn_a_b_in, L0_attn_a_conv_w, L0_attn_a_conv_b, L0_attn_a_W_xproj, L0_attn_a_W_dt, L0_attn_a_b_dt, L0_attn_a_A_log, L0_attn_a_D, L0_attn_a_W_out, L0_attn_a_b_out, L0_attn_a_Wg, L0_attn_a_bg, L0_attn_a_Wv, L0_attn_a_bv, L0_attn_b_Wq, L0_attn_b_bq, L0_attn_b_Wk, L0_attn_b_bk, L0_attn_b_Wv, L0_attn_b_bv, L0_attn_b_Wo, L0_attn_b_bo, L0_ffn_gate_w, L0_ffn_w1, L0_ffn_b1, L0_ffn_ln1_g, L0_ffn_ln1_b, L0_ffn_w2, L0_ffn_b2, L0_ffn_ln_g, L0_ffn_ln_b, L1_attn_a_Wq, L1_attn_a_Wk, L1_attn_a_Wv, L1_attn_a_Wg, L1_attn_a_Wo, L1_attn_a_gn_w, L1_attn_a_gn_b, L1_attn_b_wq, L1_attn_b_bq, L1_attn_b_wqc, L1_attn_b_bqc, L1_attn_b_wqr, L1_attn_b_bqr, L1_attn_b_wkv, L1_attn_b_bkv, L1_attn_b_wkr, L1_attn_b_bkr, L1_attn_b_wkc, L1_attn_b_bkc, L1_attn_b_wv, L1_attn_b_bv, L1_attn_b_wo, L1_attn_b_bo, L1_ffn_Wq, L1_ffn_Wk, L1_ffn_Wv, L1_ffn_Wo, L1_ffn_bo, L1_ffn_Wr, L1_ffn_We1, L1_ffn_be1, L1_ffn_We2, L1_ffn_be2, L1_ffn_ln1_g, L1_ffn_ln1_b, L1_ffn_ln2_g, L1_ffn_ln2_b):

    def _L0_attn_a_ref(x, ln_w, ln_b, W_in, b_in, conv_w, conv_b, W_xproj, W_dt, b_dt, A_log, D, W_out, b_out, Wg, bg, Wv, bv):
        import jax, jax.numpy as jnp
        import numpy as np
        from jax import lax
        EPS = 1e-05

        def layer_norm(x, w, b):
            mu = x.mean(-1, keepdims=True)
            var = ((x - mu) ** 2).mean(-1, keepdims=True)
            return (x - mu) * lax.rsqrt(var + EPS) * w + b

        def causal_dw_conv(x, w, b):
            B, L, D = x.shape
            K = w.shape[1]
            xt = jnp.pad(x.transpose(0, 2, 1), ((0, 0), (0, 0), (K - 1, 0)))
            y = lax.conv_general_dilated(xt, w[:, None, :], (1,), 'VALID', dimension_numbers=('NCH', 'OIH', 'NCH'), feature_group_count=D)
            return (y + b[:, None]).transpose(0, 2, 1)

        def mamba_block(x, ln_w, ln_b, W_in, b_in, conv_w, conv_b, W_xproj, W_dt, b_dt, A_log, Dp, W_out, b_out):
            res = x
            x = layer_norm(x, ln_w, ln_b)
            xz = x @ W_in + b_in
            Di = xz.shape[-1] // 2
            xp, z = (xz[..., :Di], xz[..., Di:])
            xp = jax.nn.silu(causal_dw_conv(xp, conv_w, conv_b))
            dbl = xp @ W_xproj
            N = A_log.shape[-1]
            R = dbl.shape[-1] - 2 * N
            dt, Bm, Cm = (dbl[..., :R], dbl[..., R:R + N], dbl[..., R + N:])
            delta = jax.nn.softplus(dt @ W_dt + b_dt)
            A = -jnp.exp(A_log)
            dA = jnp.exp(delta[..., None] * A)
            dBx = delta[..., None] * Bm[:, :, None, :] * xp[..., None]

            def step(h, inp):
                dAt, dBxt, ct = inp
                h = dAt * h + dBxt
                return (h, jnp.einsum('bdn,bn->bd', h, ct))
            h0 = jnp.zeros((x.shape[0], Di, N), x.dtype)
            _, ys = lax.scan(step, h0, (dA.transpose(1, 0, 2, 3), dBx.transpose(1, 0, 2, 3), Cm.transpose(1, 0, 2)))
            y = ys.transpose(1, 0, 2) + xp * Dp
            y = y * jax.nn.silu(z)
            return res + y @ W_out + b_out
        fwd = mamba_block(x, ln_w[0], ln_b[0], W_in[0], b_in[0], conv_w[0], conv_b[0], W_xproj[0], W_dt[0], b_dt[0], A_log[0], D[0], W_out[0], b_out[0])
        bwd = mamba_block(x[:, ::-1], ln_w[1], ln_b[1], W_in[1], b_in[1], conv_w[1], conv_b[1], W_xproj[1], W_dt[1], b_dt[1], A_log[1], D[1], W_out[1], b_out[1])
        bwd = bwd[:, ::-1]
        comb = jnp.concatenate([fwd, bwd], -1)
        gate = jax.nn.sigmoid(comb @ Wg + bg)
        value = comb @ Wv + bv
        return (gate * value + (1.0 - gate) * fwd + (1.0 - gate) * bwd) / 2.0

    def _L0_attn_b_ref(query, Wq, bq, Wk, bk, Wv, bv, Wo, bo):
        import jax, jax.numpy as jnp
        import numpy as np
        NUM_HEADS = 16
        EPS = 1e-06

        def elu_plus_one(x):
            return jax.nn.elu(x) + 1.0
        B, L, E = query.shape
        H = NUM_HEADS
        d = E // H

        def proj(x, W, b):
            return jnp.einsum('ble,fe->blf', x, W) + b

        def heads(x):
            return x.reshape(B, L, H, d).transpose(0, 2, 1, 3)
        Q = heads(proj(query, Wq, bq))
        K = heads(proj(query, Wk, bk))
        V = heads(proj(query, Wv, bv))
        phiQ = elu_plus_one(Q)
        phiK = elu_plus_one(K)
        S = jnp.einsum('bhki,bhkj->bhij', phiK, V)
        Z = phiK.sum(axis=-2)
        num = jnp.einsum('bhqi,bhij->bhqj', phiQ, S)
        denom = jnp.einsum('bhqi,bhi->bhq', phiQ, Z)[..., None] + EPS
        context = (num / denom).transpose(0, 2, 1, 3).reshape(B, L, E)
        return jnp.einsum('ble,fe->blf', context, Wo) + bo

    def _L0_ffn_ref(x, gate_w, w1, b1, ln1_g, ln1_b, w2, b2, ln_g, ln_b):
        import jax, jax.numpy as jnp
        import numpy as np
        DIM = 128
        E = 8
        K = 2
        EPS = 1e-05

        def _ln(x, g, b):
            mu = jnp.mean(x, axis=-1, keepdims=True)
            var = jnp.mean(jnp.square(x - mu), axis=-1, keepdims=True)
            return (x - mu) * jax.lax.rsqrt(var + EPS) * g + b
        shape = x.shape
        xf = x.reshape(-1, shape[-1])
        gates = jax.nn.softmax(xf @ gate_w, axis=-1)
        topw, topi = jax.lax.top_k(gates, K)
        topw = topw / jnp.sum(topw, axis=-1, keepdims=True)
        combine = jnp.sum(topw[:, :, None] * jax.nn.one_hot(topi, E, dtype=xf.dtype), axis=1)
        h = jnp.einsum('td,edh->teh', xf, w1) + b1
        h = _ln(h, ln1_g, ln1_b)
        h = jax.nn.gelu(h, approximate=False)
        y = jnp.einsum('teh,ehd->ted', h, w2) + b2
        out = jnp.einsum('ted,te->td', y, combine)
        out = _ln(out + xf, ln_g, ln_b)
        return out.reshape(shape)

    def _L1_attn_a_ref(x, Wq, Wk, Wv, Wg, Wo, gn_w, gn_b):
        import jax, jax.numpy as jnp
        import numpy as np
        EMBED_DIM = 128
        NUM_HEADS = 16
        HEAD_DIM = EMBED_DIM // NUM_HEADS
        SCALING = HEAD_DIM ** (-0.5)
        EPS = 1e-05

        def _rope(seq_len):
            inv_freq = 1.0 / 10000.0 ** (jnp.arange(0, HEAD_DIM, 2, dtype=jnp.float32) / HEAD_DIM)
            freqs = jnp.arange(seq_len, dtype=jnp.float32)[:, None] * inv_freq[None, :]
            emb = jnp.concatenate([freqs, freqs], axis=-1)
            return (jnp.cos(emb), jnp.sin(emb))

        def _rotate(x, cos, sin):
            d = x.shape[-1]
            x1, x2 = (x[..., :d // 2], x[..., d // 2:])
            rotated = jnp.concatenate([-x2, x1], axis=-1)
            return x * cos + rotated * sin
        B, S, D = x.shape
        H, Dh = (NUM_HEADS, HEAD_DIM)

        def split_heads(t):
            return t.reshape(B, S, H, Dh).transpose(0, 2, 1, 3)
        q = split_heads(x @ Wq.T)
        k = split_heads(x @ Wk.T)
        v = split_heads(x @ Wv.T)
        cos, sin = _rope(S)
        q = _rotate(q, cos, sin)
        k = _rotate(k, cos, sin)
        retention = jnp.einsum('bhsd,bhtd->bhst', q, k) * SCALING
        gammas = 1.0 - 2.0 ** (-5.0 - jnp.arange(H, dtype=jnp.float32))
        diff = jnp.arange(S)[:, None] - jnp.arange(S)[None, :]
        causal = diff >= 0
        decay = jnp.where(causal, gammas[:, None, None] ** jnp.maximum(diff, 0).astype(jnp.float32), 0.0)
        retention = retention * decay[None]
        out = jnp.einsum('bhst,bhtd->bhsd', retention, v)
        out = out.transpose(0, 2, 1, 3).reshape(B * S, H, Dh)
        mean = out.mean(axis=-1, keepdims=True)
        var = out.var(axis=-1, keepdims=True)
        out = (out - mean) * jax.lax.rsqrt(var + EPS)
        out = out * gn_w.reshape(H, Dh) + gn_b.reshape(H, Dh)
        out = out.reshape(B, S, D)
        gate = jax.nn.silu(x @ Wg.T)
        return gate * out @ Wo.T

    def _L1_attn_b_ref(x, wq, bq, wqc, bqc, wqr, bqr, wkv, bkv, wkr, bkr, wkc, bkc, wv, bv, wo, bo):
        import jax, jax.numpy as jnp
        import numpy as np
        import math
        B, S, E = (2, 256, 128)
        H, DC, DR = (16, 32, 128)
        HD = E // H

        def _linear_params(key, din, dout):
            k1, k2 = jax.random.split(key)
            bound = 1.0 / math.sqrt(din)
            w = jax.random.uniform(k1, (din, dout), minval=-bound, maxval=bound, dtype=jnp.float32)
            b = jax.random.uniform(k2, (dout,), minval=-bound, maxval=bound, dtype=jnp.float32)
            return (w, b)

        def _gelu(x):
            return jax.nn.gelu(x, approximate=False)

        def _rope_cos_sin(seq_len, d_rope):
            inv_freq = 1.0 / 10000.0 ** (jnp.arange(0, d_rope, 2, dtype=jnp.float32) / d_rope)
            t = jnp.arange(seq_len, dtype=jnp.float32)
            freqs = t[:, None] * inv_freq[None, :]
            emb = jnp.concatenate([freqs, freqs], axis=-1)
            return (jnp.cos(emb), jnp.sin(emb))

        def _apply_rope(x, cos, sin):
            d = x.shape[-1]
            x1, x2 = (x[..., :d // 2], x[..., d // 2:])
            rot = jnp.concatenate([-x2, x1], axis=-1)
            return x * cos + rot * sin
        b, s, _ = x.shape
        cq = _gelu(x @ wq + bq)
        q_c = cq @ wqc + bqc
        q_r = x @ wqr + bqr
        ckv = _gelu(x @ wkv + bkv)
        k_r = x @ wkr + bkr
        k_c = ckv @ wkc + bkc
        v = (ckv @ wv + bv).reshape(b, s, H, HD).transpose(0, 2, 1, 3)
        cos, sin = _rope_cos_sin(s, DR)
        q_r = _apply_rope(q_r, cos, sin)
        k_r = _apply_rope(k_r, cos, sin)
        q = _gelu(jnp.concatenate([q_c, q_r], axis=-1)).reshape(b, s, H, HD).transpose(0, 2, 1, 3)
        k = _gelu(jnp.concatenate([k_c, k_r], axis=-1)).reshape(b, s, H, HD).transpose(0, 2, 1, 3)
        scale = 1.0 / math.sqrt(HD)
        scores = jnp.einsum('bhqd,bhkd->bhqk', q, k) * scale
        causal = jnp.triu(jnp.ones((s, s), dtype=bool), k=1)
        scores = jnp.where(causal[None, None], -jnp.inf, scores)
        attn = jax.nn.softmax(scores, axis=-1)
        out = jnp.einsum('bhqk,bhkd->bhqd', attn, v)
        out = out.transpose(0, 2, 1, 3).reshape(b, s, E)
        return out @ wo + bo

    def _L1_ffn_ref(x, Wq, Wk, Wv, Wo, bo, Wr, We1, be1, We2, be2, ln1_g, ln1_b, ln2_g, ln2_b):
        import jax, jax.numpy as jnp
        import numpy as np
        B, S, D, H, F, E = (2, 128, 128, 16, 512, 8)
        HD = D // H
        EPS = 1e-06

        def _layernorm(x, g, b):
            m = jnp.mean(x, axis=-1, keepdims=True)
            v = jnp.var(x, axis=-1, keepdims=True)
            return (x - m) / jnp.sqrt(v + EPS) * g + b
        b, s, d = x.shape

        def split_heads(t):
            return t.reshape(b, s, H, HD).transpose(0, 2, 1, 3)
        q = split_heads(x @ Wq)
        k = split_heads(x @ Wk)
        v = split_heads(x @ Wv)
        scores = jnp.einsum('bhqd,bhkd->bhqk', q, k) / jnp.sqrt(jnp.float32(HD))
        attn_w = jax.nn.softmax(scores, axis=-1)
        ctx = jnp.einsum('bhqk,bhkd->bhqd', attn_w, v)
        ctx = ctx.transpose(0, 2, 1, 3).reshape(b, s, d)
        attn_out = ctx @ Wo + bo
        out1 = _layernorm(x + attn_out, ln1_g, ln1_b)
        router_probs = jax.nn.softmax(out1 @ Wr, axis=-1)
        top_g, top_i = jax.lax.top_k(router_probs, 2)
        top_g = jax.nn.softmax(top_g, axis=-1)
        acc = jnp.zeros_like(out1)
        for e in range(E):
            sel = top_i == e
            msk = jnp.any(sel, axis=-1)[..., None].astype(out1.dtype)
            h = jax.nn.gelu(out1 * msk @ We1[e] + be1[e], approximate=False)
            o = h @ We2[e] + be2[e]
            gate = jnp.sum(top_g * sel.astype(top_g.dtype), axis=-1, keepdims=True)
            acc = acc + o * gate
        return _layernorm(out1 + acc, ln2_g, ln2_b)
    x = L0_attn_a_x
    x = x + _L0_attn_a_ref(_layernorm(x, axis=-1), L0_attn_a_ln_w, L0_attn_a_ln_b, L0_attn_a_W_in, L0_attn_a_b_in, L0_attn_a_conv_w, L0_attn_a_conv_b, L0_attn_a_W_xproj, L0_attn_a_W_dt, L0_attn_a_b_dt, L0_attn_a_A_log, L0_attn_a_D, L0_attn_a_W_out, L0_attn_a_b_out, L0_attn_a_Wg, L0_attn_a_bg, L0_attn_a_Wv, L0_attn_a_bv)
    x = x + _L0_ffn_ref(_layernorm(x, axis=-1), L0_ffn_gate_w, L0_ffn_w1, L0_ffn_b1, L0_ffn_ln1_g, L0_ffn_ln1_b, L0_ffn_w2, L0_ffn_b2, L0_ffn_ln_g, L0_ffn_ln_b)
    x = x + _L0_attn_b_ref(_layernorm(x, axis=-1), L0_attn_b_Wq, L0_attn_b_bq, L0_attn_b_Wk, L0_attn_b_bk, L0_attn_b_Wv, L0_attn_b_bv, L0_attn_b_Wo, L0_attn_b_bo)
    x = x + _L0_ffn_ref(_layernorm(x, axis=-1), L0_ffn_gate_w, L0_ffn_w1, L0_ffn_b1, L0_ffn_ln1_g, L0_ffn_ln1_b, L0_ffn_w2, L0_ffn_b2, L0_ffn_ln_g, L0_ffn_ln_b)
    x = x + _L1_attn_a_ref(_layernorm(x, axis=-1), L1_attn_a_Wq, L1_attn_a_Wk, L1_attn_a_Wv, L1_attn_a_Wg, L1_attn_a_Wo, L1_attn_a_gn_w, L1_attn_a_gn_b)
    x = x + _L1_ffn_ref(_layernorm(x, axis=-1), L1_ffn_Wq, L1_ffn_Wk, L1_ffn_Wv, L1_ffn_Wo, L1_ffn_bo, L1_ffn_Wr, L1_ffn_We1, L1_ffn_be1, L1_ffn_We2, L1_ffn_be2, L1_ffn_ln1_g, L1_ffn_ln1_b, L1_ffn_ln2_g, L1_ffn_ln2_b)
    x = x + _L1_attn_b_ref(_layernorm(x, axis=-1), L1_attn_b_wq, L1_attn_b_bq, L1_attn_b_wqc, L1_attn_b_bqc, L1_attn_b_wqr, L1_attn_b_bqr, L1_attn_b_wkv, L1_attn_b_bkv, L1_attn_b_wkr, L1_attn_b_bkr, L1_attn_b_wkc, L1_attn_b_bkc, L1_attn_b_wv, L1_attn_b_bv, L1_attn_b_wo, L1_attn_b_bo)
    x = x + _L1_ffn_ref(_layernorm(x, axis=-1), L1_ffn_Wq, L1_ffn_Wk, L1_ffn_Wv, L1_ffn_Wo, L1_ffn_bo, L1_ffn_Wr, L1_ffn_We1, L1_ffn_be1, L1_ffn_We2, L1_ffn_be2, L1_ffn_ln1_g, L1_ffn_ln1_b, L1_ffn_ln2_g, L1_ffn_ln2_b)
    return x

_drawn_inputs = setup_inputs


def setup_inputs(seed=0):
    import zlib

    import numpy as np

    out = dict(_drawn_inputs(seed))
    spreads = {'L0_attn_a_ln_w': (1.0, 0.2),
     'L0_attn_a_ln_b': (0.0, 0.1),
     'L0_attn_a_b_in': (0.0, 0.1),
     'L0_attn_a_conv_b': (0.0, 0.343),
     'L0_attn_a_D': (1.0, 0.2),
     'L0_attn_a_b_out': (0.0, 0.1),
     'L0_attn_a_bg': (0.0, 0.316),
     'L0_attn_a_bv': (0.0, 0.27),
     'L0_ffn_ln1_g': (1.0, 0.2),
     'L0_ffn_ln1_b': (0.0, 0.371),
     'L0_ffn_ln_g': (1.0, 0.2),
     'L0_ffn_ln_b': (0.0, 0.1),
     'L1_attn_a_gn_w': (1.0, 0.2),
     'L1_attn_a_gn_b': (0.0, 0.448),
     'L1_ffn_bo': (0.0, 0.1),
     'L1_ffn_be1': (0.0, 0.8),
     'L1_ffn_be2': (0.0, 0.284),
     'L1_ffn_ln1_g': (1.0, 0.2),
     'L1_ffn_ln1_b': (0.0, 0.1),
     'L1_ffn_ln2_g': (1.0, 0.2),
     'L1_ffn_ln2_b': (0.0, 0.1)}
    factors = {'L0_attn_a_W_dt': 8.0,
     'L0_attn_a_b_dt': 8.0,
     'L0_attn_a_A_log': 3.288,
     'L0_attn_b_Wq': 6.88,
     'L0_attn_b_bq': 22.422,
     'L0_attn_b_Wk': 4.217,
     'L0_attn_b_bk': 26.665,
     'L0_attn_b_bv': 8.0,
     'L0_attn_b_bo': 8.0,
     'L0_ffn_b1': 2.971,
     'L0_ffn_b2': 2.847,
     'L1_attn_b_wqr': 8.0,
     'L1_attn_b_bqr': 8.0,
     'L1_attn_b_wkv': 8.0,
     'L1_attn_b_bkv': 8.0,
     'L1_attn_b_wkr': 8.0,
     'L1_attn_b_bkr': 8.0,
     'L1_attn_b_wv': 6.462,
     'L1_attn_b_bv': 3.912,
     'L1_attn_b_wo': 3.171,
     'L1_attn_b_bo': 21.786,
     'L1_ffn_Wq': 8.0,
     'L1_ffn_Wk': 8.0,
     'L1_ffn_Wv': 8.0,
     'L1_ffn_Wo': 8.0,
     'L1_ffn_We1': 3.787,
     'L1_ffn_We2': 3.424}
    for name, (base, spread) in spreads.items():
        noise = np.random.default_rng([zlib.crc32(name.encode()), seed]).standard_normal(out[name].shape)
        drawn = base * np.exp(spread * noise) if base else spread * noise
        out[name] = jnp.asarray(drawn.astype(out[name].dtype))
    for name, factor in factors.items():
        out[name] = (out[name] * factor).astype(out[name].dtype)
    return out
```

```python
import concourse.bass as bass
from concourse import mybir
from contextlib import ExitStack
import numpy as np


FP32 = mybir.dt.float32
BF16 = mybir.dt.bfloat16
ALU = mybir.AluOpType
ACT = mybir.ActivationFunctionType
AXX = mybir.AxisListType.X

P = 128
T = 512
NT = T // P
SLOTS = 2
H = 16
HD = P // H
HP = H // 2
E = 8
DI = 2 * P
NS = 16
RK = 64
H0 = 256
H1 = 512
TAPS = 4
PADW = T + TAPS - 1
SCORE_SCALE = float(HD) ** -0.5
MASKED = -1.0e30

Q_PARTS = (0, 0, 1, 0, 2, 1)
K_PARTS = (0, 1, 0, 2, 0, 1)
NSTACK = len(Q_PARTS) * HD
NMAX = NSTACK + 3


def layout(sections):
    at, where = 0, {}
    for name, width in sections:
        where[name] = (at, width)
        at += width
    return where, at


WEIGHTS = [
    ("ln_w", 2), ("ln_b", 2), ("b_in", 8), ("conv_w", 4 * TAPS), ("conv_b", 4), ("b_dt", 4),
    ("A", 4 * NS), ("D", 4), ("b_out", 2), ("bg", 1), ("bv", 1), ("bq_lin", 1),
    ("b1", 2 * E), ("g1", 2 * E), ("be_ln1", 2 * E), ("be1", 4 * E),
    ("bqr", 1), ("bqr_rot", 1), ("bkr", 1), ("bkr_rot", 1), ("bkv", 1),
    ("W_in", 2 * 2 * DI), ("W_x", 2 * 2 * (RK + 2 * NS)), ("W_dt", 2 * DI), ("W_out", 2 * 2 * P),
    ("Wg", 2 * P), ("Wv", 2 * P),
    ("gate_w", E), ("v2", E), ("w1", E * H0), ("w2", E * 2 * P), ("b2", P),
    ("lin_Wq", P), ("lin_Wk", P), ("lin_Wv", P), ("lin_Wo", P),
    ("ret_Wq", P), ("ret_Wq_rot", P), ("ret_Wk", P), ("ret_Wk_rot", P), ("ret_Wv", P),
    ("ret_Wg", P), ("ret_Wo", P),
    ("f_Wq", P), ("f_Wk", P), ("f_Wv", P), ("f_Wo", P), ("f_Wr", E), ("f_b2", P),
    ("lat_wqr", P), ("lat_wqr_rot", P), ("lat_wkr", P), ("lat_wkr_rot", P),
    ("lat_wkv", 32), ("lat_wv", P), ("lat_wo", P),
    ("We1", E * H1), ("We2", E * 4 * P),
]
W_AT, W_WIDTH = layout(WEIGHTS)

ROWS = [
    ("lin_bk", P), ("lin_bv", P), ("lin_bo", P), ("ln_g", P), ("ln_be", P), ("gn_w", P), ("gn_b", P),
    ("f_bo", P), ("f_ln1g", P), ("f_ln1b", P), ("f_ln2g", P), ("f_ln2b", P), ("lat_bv", P), ("lat_bo", P),
]
R_AT, R_WIDTH = layout(ROWS)

CONSTS = [
    ("ident", P), ("anti", P), ("sel32", 2 * NS), ("sel8", E), ("mask_q", P), ("mask_k", P),
    ("blocks", P), ("block16", H), ("earlier", E * E), ("gamma_chunk", 1),
    ("k_decay", P), ("q_decay", P), ("decay", H * P),
]
C_AT, C_WIDTH = layout(CONSTS)
TABLES = ("ret_cos", "ret_sin", "lat_cos", "lat_sin")

NORM = {"var": 1, "rstd": 1, "normed": 1, "bank0": 1}
RAISES = {
    "load": {"x_loaded": 16},
    "norm": NORM,
    "mamba_in": {"var": 1, "rstd": 1, "normed": 1, "bank0": 1, "bank1": 1},
    "mamba_dir": {"gate_tanh": 1, "conv": 1, "conv_tanh": 1, "conv_out": 1,
                  "bc_parts": 1, "minus_abs": 1, "exp_abs": 1, "one_plus": 1, "log": 1, "delta": 1,
                  "bank0": 2, "bank1": 3, "bank2": 2, "bank3": 2},
    "scan": {"decay_ready": 1, "state": 1, "state_c": 1, "summed": 1, "bank0": 1, "bank1": 1},
    "scan_first": {"decay_ready": 1, "state": 1, "state_c": 1, "bank0": 1, "bank1": 1},
    "mamba_out": {"summed": 1, "gated": 1, "bank0": 1, "bank2": 1, "bank3": 1},
    "combine": {"mixed": 1, "bank0": 1, "bank1": 1, "bank2": 1},
    "moe0_in": {"exped": 1, "weighed": 1, "expert_var": 1, "expert_root": 1, "root_parts": 1,
                "bank0": 2, "bank1": NT, "bank2": NT, "bank3": 1},
    "moe0_first": {"hidden": 2, "bank0": 1, "bank1": 1, "bank2": 1},
    "moe0": {"hidden": 2, "bank0": 1, "bank1": 1, "bank2": 1, "bank3": 1},
    "moe0_out": {"var": 1, "rstd": 1, "added": 1, "bank0": 1, "bank3": 1},
    "linear": {"negative": 1, "elu": 1, "features": 1, "kv": 1, "context": 1, "bank0": 2, "bank1": 2,
               "bank2": 1, "bank3": 1},
    "project": {"bank2": 1, "bank3": 1},
    "ret_in": {"table": 32, "rotated": 2, "k_decayed": 1, "q_parts": 1, "k_parts": 1, "gate": 1, "q_decayed": 1,
               "entering": 1, "bank0": 2, "bank1": 2, "bank2": 2, "bank3": 2},
    "stack": {"ones": 1, "parts_out": 32, "stacked": 16 * 4 * len(Q_PARTS)},
    "ret_head_first": {"bank0": 1},
    "ret_head": {"retained": 1, "bank0": 1},
    "ret_out": {"var": 1, "rstd": 1, "context": 1, "bank2": 1},
    "attn_in": {"q_parts": 1, "k_parts": 1, "bank0": 1, "bank1": 1, "bank2": 1},
    "lat_in": {"table": 32, "rotated": 2, "activated": 2, "q_parts": 1, "k_parts": 1, "bank0": 2, "bank1": 2,
               "bank2": 1, "bank3": 1},
    "row_max": {"bank0": 1, "bank1": 1, "bank2": 1, "bank3": 1},
    "max_rows": {"max_parts": 1, "max_out": 16, "max_stacked": 32, "bank0": 1},
    "attend_first": {"multiplied": 2, "bank0": 2, "bank1": 2},
    "attend": {"multiplied": 4, "bank0": 2, "bank1": 2},
    "attended": {"multiplied": 2, "context": 1, "bank2": 1, "bank3": 1},
    "moe1_in": {"var": 1, "rstd": 1, "normed": 1, "exped": 1, "above": 1, "exped_again": 1, "weighed": 1,
                "bank0": 1, "bank1": 1, "bank3": 1},
    "moe1_first": {"bank0": 2, "bank1": 2},
    "moe1": {"bank0": 2, "bank1": 2, "bank2": 1},
    "moe1_out": {"var": 1, "rstd": 1, "added": 1, "bank2": 1, "bank3": 1},
    "store": {"x_stored": 16},
}


def schedule(n_heads=H):
    mamba = [("norm", 0), ("mamba_in", 0)]
    for d in range(2):
        mamba += [("mamba_dir", d)] + [("scan_first" if n < 2 else "scan", (d, n)) for n in range(NS)] + [("mamba_out", d)]
    mamba += [("combine", 0)]
    steps = [("load", 0)] + mamba
    experts0 = [("norm", 0), ("moe0_in", 0)]
    experts0 += [("moe0" if e else "moe0_first", e) for e in range(E)] + [("moe0_out", 0)]
    linear = [("norm", 0), ("linear", 0), ("project", ("lin_Wo", "lin_bo", 1.0, "X"))]
    retention = [("norm", 0), ("ret_in", 0), ("stack", 0)]
    retention += [("ret_head" if h else "ret_head_first", h) for h in range(H)]
    retention += [("ret_out", 0), ("project", ("ret_Wo", None, 0.5, "X"))]
    def attention(causal):
        part = [("stack", 0)] + [("row_max", (h, causal)) for h in range(H)] + [("max_rows", 0)]
        part += [("attend" if h else "attend_first", (h, causal)) for h in range(H)]
        return part + [("attended", causal)]

    experts1 = [("norm", 0), ("attn_in", 0)] + attention(False) + [("project", ("f_Wo", "f_bo", 1.0, "W"))]
    experts1 += [("moe1_in", 0)] + [("moe1" if e else "moe1_first", e) for e in range(E)] + [("moe1_out", 0)]
    latent = [("norm", 0), ("lat_in", 0)] + attention(True) + [("project", ("lat_wo", "lat_bo", 1.0, "X"))]
    steps += experts0
    steps += linear
    steps += experts0
    steps += retention
    steps += experts1
    steps += latent
    steps += experts1
    return steps + [("store", 0)]


class Program:

    def __init__(self, nc, steps):
        self.nc, self.steps = nc, steps
        self.sems = {}
        self.raised = {}
        self.before = []
        seen = {}
        for kind, _ in steps:
            self.before.append(dict(seen))
            for name, n in RAISES[kind].items():
                seen[name] = seen.get(name, 0) + n
        self.names = sorted(seen)


    def check(self):
        for slot in range(SLOTS):
            for pos, (kind, arg) in enumerate(self.steps):
                for name, n in RAISES[kind].items():
                    for key in (name, name + "_drained") if name[:4] == "bank" else (name,):
                        got = self.raised.get((slot, pos, key), 0)
                        assert got == n, (kind, arg, key, got, n)


class Cursor:

    def __init__(self, prog, eng, slot, pos, own):
        self.prog, self.eng, self.slot, self.pos, self.own = prog, eng, slot, pos, own
        self.base = prog.before[pos]

    def sem(self, name):
        return self.prog.sems[name, self.slot]

    def nth(self, name, k=1):
        return self.base.get(name, 0) + k

    def past(self, name, back=0):
        assert self.base.get(name, 0) >= back
        return self.base.get(name, 0) - back

    def raises(self, name, by=1):
        self.count(name, by)
        return self.sem(name)

    def count(self, name, by=1):
        key = (self.slot, self.pos, name)
        self.prog.raised[key] = self.prog.raised.get(key, 0) + by

    def filled(self, b):
        return self.prog.sems[f"filled{b}", self.slot]

    def drained(self, b):
        return self.prog.sems[f"drained{b}", self.slot]

    def fills(self, b):
        self.count(f"bank{b}")
        return self.filled(b)

    def drains(self, b):
        self.count(f"bank{b}_drained")
        return self.drained(b)

    def fill(self, b, j=0):
        return self.base.get(f"bank{b}", 0) + j + 1

    def fill_before(self, b, j=0):
        return self.fill(b, j) - 1

    def fill_past(self, b, back=0):
        assert self.base.get(f"bank{b}", 0) >= back
        return self.base.get(f"bank{b}", 0) - back

    def link(self, ins):
        self.own["n"] += 1
        ins.then_inc(self.own["sem"], 1)
        self.eng.wait_ge(self.own["sem"], self.own["n"])


def network(nc, x, wts, rows, consts, tables, out):
    steps = schedule()
    prog = Program(nc, steps)
    stack = ExitStack()
    with stack:
        def sb(name, shape, dt=FP32):
            return stack.enter_context(nc.sbuf_tensor(name, shape, dt))

        def dram(name, shape, dt):
            return nc.dram_tensor(name, shape, dt, kind="Internal").ap()

        Wt = sb("weights", [P, W_WIDTH])
        Rt = sb("rows", [P, R_WIDTH])
        Ct = sb("consts", [P, C_WIDTH])

        def w(name, lo=0, n=None):
            at, width = W_AT[name]
            return Wt[:, at + lo:at + (lo + n if n is not None else width)]

        def row(name):
            at, width = R_AT[name]
            return Rt[:, at:at + width]

        def const(name, lo=0, n=None):
            at, width = C_AT[name]
            return Ct[:, at + lo:at + (lo + n if n is not None else width)]

        identb = sb("identb", [P, P], BF16)
        maskb = sb("maskb", [P, 2, P], BF16)
        selb = sb("selb", [3 * 2 * NS, 2 * NS], BF16)
        sel8b = sb("sel8b", [3 * E, E], BF16)
        G = sb("G", [P, E, P])
        ce = sb("ce", [P, E])
        half_bin = sb("half_bin", [P, 8])
        half_bg = sb("half_bg", [P, 1])
        mhalf64 = sb("mhalf64", [P, NT * H])
        mhalf = mhalf64[:, 0:NT * E]
        ARENA = 11968
        X = [sb(f"X{s}", [P, NT, P]) for s in range(SLOTS)]
        W = [sb(f"W{s}", [P, NT, P]) for s in range(SLOTS)]
        WT = [sb(f"WT{s}", [P, T]) for s in range(SLOTS)]
        small = [sb(f"small{s}", [P, 128]) for s in range(SLOTS)]
        arena = [sb(f"arena{s}", [P, ARENA]) for s in range(SLOTS)]
        banks = [[stack.enter_context(nc.psum_tensor(f"bank{s}{b}", [P, T], FP32)) for b in range(4)]
                 for s in range(SLOTS)]

        def ar(s, at, n, dt=FP32):
            if dt is FP32:
                return arena[s][:, at:at + n]
            return arena[s][:, at:at + n // 2].bitcast(BF16)

        def sm(s, at, n):
            return small[s][:, at:at + n]

        stats = lambda s: sm(s, 0, 24).rearrange("p (t k) -> p t k", t=NT)
        moments = lambda s: sm(s, 24, 8).rearrange("p (t k) -> p t k", t=NT)
        var = lambda s: sm(s, 32, NT)
        rstd = lambda s: sm(s, 36, NT)

        def halves(ap):
            return ap.rearrange("p (h t) -> p h t", h=2)

        def over_tokens(ap):
            return ap.unsqueeze(1).to_broadcast([P, NT, ap.shape[1]])

        def bank(s, b):
            return banks[s][b]

        setup_sems = {n: stack.enter_context(nc.semaphore(n)) for n in
                      ("weights_loaded", "halved", "A_exp", "A_ready", "centred", "w1_turned", "w1T_ready",
                       "gram", "gram_ready", "consts_ready", "mhalf_ready", "sq_ready",
                       "vector_setup", "scalar_setup", "pool_setup", "tensor_setup")}
        barrier = {n: stack.enter_context(nc.semaphore(n)) for n in ("pair_done", "cleared", "left")}
        loop_sems = []
        for s in range(SLOTS):
            for name in prog.names:
                for full_name in ((f"filled{name[4:]}", f"drained{name[4:]}") if name[:4] == "bank" and name[4:].isdigit() else (name,)):
                    prog.sems[full_name, s] = stack.enter_context(nc.semaphore(f"{full_name}_{s}"))
                    loop_sems.append(prog.sems[full_name, s])
        chains = {n: {"sem": stack.enter_context(nc.semaphore(f"{n}_chain")), "n": 0}
                  for n in ("vector", "scalar", "gpsimd")}
        loop_sems += [c["sem"] for c in chains.values()]
        setup_chain = {"sem": setup_sems["vector_setup"], "n": 0}

        def run(eng, own, table):
            for slot, pos in ORDER:
                kind, arg = steps[pos]
                if kind in table:
                    table[kind](Cursor(prog, eng, slot, pos, own), slot, arg)

        ORDER = [(slot, pos) for pos in range(len(steps)) for slot in range(SLOTS)]

        def leave(eng, clears=False):
            if clears:
                eng.wait_ge(barrier["pair_done"], 4)
                for sem in loop_sems:
                    eng.sem_clear(sem)
                eng.sem_clear(barrier["pair_done"])
                eng.sem_inc(barrier["cleared"], 1)
                eng.wait_ge(barrier["left"], 4)
                eng.sem_clear(barrier["cleared"])
                eng.sem_clear(barrier["left"])
            else:
                eng.sem_inc(barrier["pair_done"], 1)
                eng.wait_ge(barrier["cleared"], 1)
                eng.sem_inc(barrier["left"], 1)

        v, a, g, pe = nc.vector, nc.scalar, nc.gpsimd, nc.tensor
        I = const("ident")

        def norm_vector(c, s, src, dst, eps, k=1):
            for t in range(NT):
                last = v.bn_stats(stats(s)[:, t, :], src[:, t, :])
            c.link(last)
            for t in range(NT):
                last = v.bn_aggr(moments(s)[:, t, :], stats(s)[:, t, :])
            c.link(last)
            v.tensor_scalar(var(s), moments(s)[:, :, 1], eps, None, ALU.add).then_inc(c.raises("var"), 1)
            v.wait_ge(c.sem("rstd"), c.nth("rstd", k))
            for t in range(NT):
                last = v.tensor_scalar(dst[:, t, :], src[:, t, :], moments(s)[:, t, 0:1], rstd(s)[:, t:t + 1],
                                       ALU.subtract, ALU.mult)
            return last

        def norm_pool(c, s, k=1):
            g.wait_ge(c.sem("var"), c.nth("var", k))
            g.tensor_tensor(rstd(s), var(s), mhalf[:, 0:NT], ALU.pow).then_inc(c.raises("rstd"), 1)

        def turn(c, s, src, b, last_j=0, identity=None, reverse=False):
            for t in range(NT):
                at = (NT - 1 - t if reverse else t) * P
                last = pe.matmul(bank(s, b)[:, at:at + P], src[:, t, :], identity, is_transpose=True,
                                 start=True, stop=True)
            last.then_inc(c.fills(b), 1)

        def residual_ready(c):
            kind = steps[c.pos - 1][0]
            if kind == "load":
                c.eng.wait_ge(c.sem("x_loaded"), c.past("x_loaded"))
            elif kind in ("moe0_out", "moe1_out"):
                c.eng.wait_ge(c.sem("added"), c.past("added"))
            else:
                c.eng.wait_ge(c.drained({"combine": 2, "project": 3}[kind]), c.fill_past({"combine": 2, "project": 3}[kind]))

        def norm_v(c, s, arg):
            residual_ready(c)
            norm_vector(c, s, X[s], W[s], 1e-5).then_inc(c.raises("normed"), 1)

        def norm_p(c, s, arg):
            norm_pool(c, s)

        def norm_t(c, s, arg):
            pe.wait_ge(c.sem("normed"), c.nth("normed"))
            pe.wait_ge(c.drained(0), c.fill_before(0))
            turn(c, s, W[s], 0, identity=I)

        def norm_s(c, s, arg):
            a.wait_ge(c.filled(0), c.fill(0))
            a.copy(WT[s][:, :], bank(s, 0)[:, :]).then_inc(c.drains(0), 1)


        XL, XC, SZ, DELTA, DX, BCP, BCT, BCR, RING = 0, 1024, 2048, 3072, 4096, 5120, 5376, 5568, 5824
        U2 = RING
        XPAD, ACC, THC, ZH, THZ, DTT = RING, RING + 1032, RING + 2056, RING + 3080, RING + 4104, RING + 5176
        XB, EA, W1P, LW = RING, RING + 1024, RING + 2048, RING + 3072
        DA = lambda s, n: halves(ar(s, RING + 1024 * (n % 2), 1024))
        BX = lambda s, n: halves(ar(s, RING + 2048 + 1024 * (n % 3), 1024))
        CB = lambda s, n: ar(s, RING + 5120 + 512 * (n % 2), 512)
        LAG = 2
        u2 = lambda s: ar(s, U2, T).rearrange("p (t d) -> p t d", t=NT)
        xl = lambda s, d: ar(s, XL + T * d, T)
        f = xl
        xpad = lambda s: ar(s, XPAD, 2 * 516).rearrange("p (h t) -> p h t", h=2)
        bct = lambda s: ar(s, BCT, NT * 3 * 32, BF16).rearrange("p (t k n) -> p t k n", t=NT, k=3)
        bcp = lambda s: ar(s, BCP, T, BF16)[0:96, :]

        def split3(c, src, parts, rest, drain=None):
            c.link(v.tensor_copy(parts[0], src))
            ins = v.tensor_tensor(rest, src, parts[0], ALU.subtract)
            if drain is None:
                c.link(ins)
            else:
                ins.then_inc(c.drains(drain[0]), 1)
                v.wait_ge(c.drained(drain[0]), c.fill(drain[0], drain[1]))
            c.link(v.tensor_copy(parts[1], rest))
            c.link(v.tensor_tensor(rest, rest, parts[1], ALU.subtract))
            return v.tensor_copy(parts[2], rest)

        def mamba_in_v(c, s, arg):
            v.wait_ge(c.sem("normed"), c.past("normed"))
            norm_vector(c, s, W[s], u2(s), 1e-5).then_inc(c.raises("normed"), 1)

        def mamba_in_p(c, s, arg):
            norm_pool(c, s)

        def mamba_in_t(c, s, arg):
            pe.wait_ge(c.sem("normed"), c.nth("normed"))
            pe.wait_ge(c.drained(0), c.fill_before(0))
            turn(c, s, u2(s), 0, identity=I)
            pe.wait_ge(c.drained(1), c.fill_before(1))
            turn(c, s, u2(s), 1, identity=const("anti"), reverse=True)

        def mamba_in_s(c, s, arg):
            for d in range(2):
                a.wait_ge(c.filled(d), c.fill(d))
                a.activation(xl(s, d), bank(s, d)[:, :], ACT.Identity, bias=w("ln_b", d, 1),
                                     scale=w("ln_w", d, 1)).then_inc(c.drains(d), 1)

        def mamba_dir_t(c, s, d):
            pe.wait_ge(c.drained(0), c.fill_past(0))
            pe.wait_ge(c.drained(1), c.fill_past(1))
            for j in range(4):
                pe.wait_ge(c.drained(j), c.fill_before(j))
                pe.matmul(bank(s, j)[:, :], w("W_in", (d * 4 + j) * P, P), xl(s, d), start=True, stop=True).then_inc(c.fills(j), 1)
            pe.wait_ge(c.sem("conv_out"), c.nth("conv_out"))
            pe.wait_ge(c.drained(0), c.fill_before(0, 1))
            for h in range(2):
                last = pe.matmul(bank(s, 0)[0:RK, :], w("W_x", (d * 2 + h) * 96, RK), ar(s, XC + h * T, T),
                                 start=h == 0, stop=h == 1)
            last.then_inc(c.fills(0), 1)
            pe.wait_ge(c.drained(1), c.fill_before(1, 1))
            for t in range(NT):
                for h in range(2):
                    last = pe.matmul(bank(s, 1)[:, t * 32:(t + 1) * 32], ar(s, XC + h * T + t * P, P),
                                     w("W_x", (d * 2 + h) * 96 + RK, 32), start=h == 0, stop=h == 1)
            last.then_inc(c.fills(1), 1)
            pe.wait_ge(c.drained(0), c.fill(0, 1))
            for h in range(2):
                pe.wait_ge(c.drained(2 + h), c.fill_before(2 + h, 1))
                pe.matmul(bank(s, 2 + h)[:, :], w("W_dt", d * DI + h * P, P)[0:RK, :],
                                   ar(s, DTT, T)[0:RK, :], start=True, stop=True).then_inc(c.fills(2 + h), 1)
            pe.wait_ge(c.sem("bc_parts"), c.nth("bc_parts"))
            pe.wait_ge(c.drained(1), c.fill_before(1, 2))
            for t in range(NT):
                last = pe.matmul(bank(s, 1)[0:96, t * P // 2:(t + 1) * P // 2].bitcast(BF16),
                                 bct(s)[:, t, :, :].rearrange("p k n -> p (k n)"), identb[:, :],
                                 is_transpose=True, start=True, stop=True)
            last.then_inc(c.fills(1), 1)

        def mamba_dir_s(c, s, d):
            if d:
                a.wait_ge(c.sem("gated"), c.past("gated"))
            for h in range(2):
                a.wait_ge(c.filled(h), c.fill(h))
                a.activation(xpad(s)[:, h, TAPS - 1:PADW], bank(s, h)[:, :], ACT.Identity,
                                     bias=w("b_in", d * 4 + h, 1)).then_inc(c.drains(h), 1)
            for h in range(2):
                a.wait_ge(c.filled(2 + h), c.fill(2 + h))
                a.activation(ar(s, ZH + h * T, T), bank(s, 2 + h)[:, :], ACT.Identity,
                                     bias=half_bin[:, d * 4 + 2 + h:d * 4 + 3 + h], scale=0.5).then_inc(c.drains(2 + h), 1)
            a.wait_ge(c.drained(3), c.fill(3))
            a.activation(ar(s, THZ, 1024), ar(s, ZH, 1024), ACT.Tanh).then_inc(c.raises("gate_tanh"), 1)
            a.wait_ge(c.sem("conv"), c.nth("conv"))
            a.activation(ar(s, THC, 1024), ar(s, ACC, 1024), ACT.Tanh).then_inc(c.raises("conv_tanh"), 1)
            a.wait_ge(c.filled(0), c.fill(0, 1))
            a.copy(ar(s, DTT, T)[0:RK, :], bank(s, 0)[0:RK, :]).then_inc(c.drains(0), 1)
            for h in range(2):
                a.wait_ge(c.filled(2 + h), c.fill(2 + h, 1))
                a.activation(ar(s, XB + h * T, T), bank(s, 2 + h)[:, :], ACT.Identity,
                                     bias=w("b_dt", d * 2 + h, 1)).then_inc(c.drains(2 + h), 1)
            a.wait_ge(c.drained(3), c.fill(3, 1))
            a.activation(ar(s, EA, 1024), ar(s, XB, 1024), ACT.Abs).then_inc(c.raises("minus_abs"), 1)
            a.wait_ge(c.sem("minus_abs"), c.nth("minus_abs"))
            a.activation(ar(s, EA, 1024), ar(s, EA, 1024), ACT.Exp, scale=-1.0).then_inc(c.raises("exp_abs"), 1)
            a.wait_ge(c.filled(1), c.fill(1, 2))
            a.copy(bcp(s), bank(s, 1)[0:96, 0:T // 2].bitcast(BF16)).then_inc(c.drains(1), 1)
            a.wait_ge(c.sem("one_plus"), c.nth("one_plus"))
            a.activation(ar(s, LW, 1024), ar(s, W1P, 1024), ACT.Ln).then_inc(c.raises("log"), 1)

        def mamba_dir_v(c, s, d):
            if d:
                v.wait_ge(c.sem("gated"), c.past("gated"))
            v.wait_ge(c.drained(1), c.fill(1))
            c.link(v.memset(xpad(s)[:, :, 0:TAPS - 1], 0.0))
            for k in range(TAPS):
                for h in range(2):
                    tap = w("conv_w", (d * 2 + h) * TAPS + k, 1)
                    acc = ar(s, ACC + h * T, T)
                    src = xpad(s)[:, h, k:k + T]
                    if k == 0:
                        ins = v.tensor_scalar(acc, src, tap, w("conv_b", d * 2 + h, 1), ALU.mult, ALU.add)
                    else:
                        ins = v.scalar_tensor_tensor(acc, src, tap, acc, ALU.mult, ALU.add)
                if k < TAPS - 1:
                    c.link(ins)
            ins.then_inc(c.raises("conv"), 1)
            v.wait_ge(c.drained(3), c.fill(3))
            v.wait_ge(c.sem("gate_tanh"), c.nth("gate_tanh"))
            v.scalar_tensor_tensor(ar(s, SZ, 1024), ar(s, THZ, 1024), 1.0, ar(s, ZH, 1024), ALU.add, ALU.mult)
            v.wait_ge(c.sem("conv_tanh"), c.nth("conv_tanh"))
            v.scalar_tensor_tensor(ar(s, XC, 1024), ar(s, THC, 1024), 1.0, ar(s, ACC, 1024),
                                          ALU.add, ALU.mult).then_inc(c.raises("conv_out"), 1)
            v.wait_ge(c.filled(1), c.fill(1, 1))
            src = bank(s, 1)[:, 0:NT * 32].rearrange("p (t n) -> p t n", t=NT)
            split3(c, src, [bct(s)[:, :, k, :] for k in range(3)],
                          ar(s, BCR, 128).rearrange("p (t n) -> p t n", t=NT), (1, 1)).then_inc(c.raises("bc_parts"), 1)
            e, w1p, lw, delta = (ar(s, k, 1024) for k in (EA, W1P, LW, DELTA))
            v.wait_ge(c.sem("exp_abs"), c.nth("exp_abs"))
            v.tensor_scalar(w1p, e, 1.0, None, ALU.add).then_inc(c.raises("one_plus"), 1)
            v.wait_ge(c.sem("one_plus"), c.nth("one_plus"))
            c.link(v.scalar_tensor_tensor(e, w1p, 1.0, e, ALU.subtract, ALU.subtract))
            v.wait_ge(c.sem("log"), c.nth("log"))
            c.link(v.scalar_tensor_tensor(delta, ar(s, XB, 1024), 0.0, lw, ALU.max, ALU.add))
            c.link(v.tensor_tensor(delta, delta, e, ALU.subtract))
            for n in range(2):
                v.memset(DA(s, n)[:, :, 0:1], 0.0)
            v.tensor_tensor(ar(s, DX, 1024), delta, ar(s, XC, 1024), ALU.mult).then_inc(c.raises("delta"), 1)

        def scan_t(c, s, arg):
            d, n = arg
            if n == 0:
                pe.wait_ge(c.drained(1), c.fill_past(1))
            for k in range(2):
                pe.wait_ge(c.drained(k), c.fill_before(k))
                pe.matmul(bank(s, k)[:, :], selb[0:96, k * NS + n:k * NS + n + 1].to_broadcast([96, P]),
                                   bcp(s), start=True, stop=True).then_inc(c.fills(k), 1)
            if n >= LAG:
                sum_states(c, s, n - LAG, LAG)

        def sum_states(c, s, n, back):
            pe.wait_ge(c.sem("state_c"), c.past("state_c", back - 1))
            for h in range(2):
                if n == 0:
                    pe.wait_ge(c.drained(2 + h), c.fill_before(2 + h))
                last = pe.matmul(bank(s, 2 + h)[:, :], I, BX(s, n)[:, h, :], start=n == 0, stop=n == NS - 1)
                if n == NS - 1:
                    last.then_inc(c.fills(2 + h), 1)
            if n < NS - 1:
                last.then_inc(c.raises("summed"), 1)

        def scan_s(c, s, arg):
            d, n = arg
            if n == 0:
                a.wait_ge(c.sem("delta"), c.past("delta"))
            if n >= 2:
                a.wait_ge(c.sem("state"), c.past("state", 1))
            for h in range(2):
                last = a.activation(DA(s, n)[:, h, 1:T], ar(s, DELTA + h * T + 1, T - 1), ACT.Exp,
                                    scale=w("A", (d * 2 + h) * NS + n, 1))
            last.then_inc(c.raises("decay_ready"), 1)
            a.wait_ge(c.filled(1), c.fill(1))
            if n >= 2:
                a.wait_ge(c.sem("state_c"), c.past("state_c", 1))
            a.copy(CB(s, n), bank(s, 1)[:, :]).then_inc(c.drains(1), 1)

        def scan_v(c, s, arg):
            d, n = arg
            if n == 0:
                v.wait_ge(c.sem("delta"), c.past("delta"))
            v.wait_ge(c.filled(0), c.fill(0))
            if n >= 3:
                v.wait_ge(c.sem("summed"), c.past("summed", 0))
            v.tensor_tensor(BX(s, n), halves(ar(s, DX, 1024)),
                                    bank(s, 0)[:, :].unsqueeze(1).to_broadcast([P, 2, T]), ALU.mult).then_inc(c.drains(0), 1)
            v.wait_ge(c.drained(0), c.fill(0))
            v.wait_ge(c.sem("decay_ready"), c.nth("decay_ready"))
            flat = ar(s, RING + 2048 + 1024 * (n % 3), 1024)
            v.tensor_tensor_scan(flat, ar(s, RING + 1024 * (n % 2), 1024), flat, 0.0, ALU.mult, ALU.add).then_inc(c.raises("state"), 1)

        def scan_p(c, s, arg):
            d, n = arg
            g.wait_ge(c.sem("state"), c.nth("state"))
            g.wait_ge(c.drained(1), c.fill(1))
            g.tensor_tensor(BX(s, n), BX(s, n), CB(s, n).unsqueeze(1).to_broadcast([P, 2, T]), ALU.mult).then_inc(c.raises("state_c"), 1)

        def mamba_out_t(c, s, d):
            sum_states(c, s, NS - 2, 2)
            sum_states(c, s, NS - 1, 1)
            pe.wait_ge(c.sem("gated"), c.nth("gated"))
            pe.wait_ge(c.drained(0), c.fill_before(0))
            for h in range(2):
                last = pe.matmul(bank(s, 0)[:, :], w("W_out", (d * 2 + h) * P, P), ar(s, DELTA + h * T, T),
                                 start=h == 0, stop=h == 1)
            last.then_inc(c.fills(0), 1)

        def mamba_out_v(c, s, d):
            y = ar(s, DELTA, 1024)
            for h in range(2):
                v.wait_ge(c.filled(2 + h), c.fill(2 + h))
                v.scalar_tensor_tensor(ar(s, DELTA + h * T, T), ar(s, XC + h * T, T), w("D", d * 2 + h, 1),
                                               bank(s, 2 + h)[:, :], ALU.mult, ALU.add).then_inc(c.drains(2 + h), 1)
            v.wait_ge(c.drained(3), c.fill(3))
            v.tensor_tensor(y, y, ar(s, SZ, 1024), ALU.mult).then_inc(c.raises("gated"), 1)
            v.wait_ge(c.filled(0), c.fill(0))
            src = bank(s, 0)[:, :] if d == 0 else bank(s, 0)[:, T - 1::-1]
            v.scalar_tensor_tensor(f(s, d), src, w("b_out", d, 1), WT[s][:, :], ALU.add, ALU.add).then_inc(c.drains(0), 1)

        def combine_t(c, s, arg):
            pe.wait_ge(c.drained(0), c.fill_past(0))
            for b, name in ((0, "Wg"), (1, "Wv")):
                pe.wait_ge(c.drained(b), c.fill_before(b))
                for d in range(2):
                    last = pe.matmul(bank(s, b)[:, :], w(name, d * P, P), f(s, d), start=d == 0, stop=d == 1)
                last.then_inc(c.fills(b), 1)
            pe.wait_ge(c.sem("mixed"), c.nth("mixed"))
            pe.wait_ge(c.drained(2), c.fill_before(2))
            for t in range(NT):
                last = pe.matmul(bank(s, 2)[:, t * P:(t + 1) * P], ar(s, ACC + t * P, P), I, is_transpose=True,
                                 start=True, stop=True)
            last.then_inc(c.fills(2), 1)

        def combine_s(c, s, arg):
            a.wait_ge(c.filled(0), c.fill(0))
            a.activation(ar(s, XPAD, T), bank(s, 0)[:, :], ACT.Tanh, bias=half_bg[:, 0:1], scale=0.5).then_inc(c.drains(0), 1)

        def combine_v(c, s, arg):
            v.wait_ge(c.drained(0), c.fill_past(0))
            both, diff, o = ar(s, THC, T), ar(s, ZH, T), ar(s, ACC, T)
            c.link(v.tensor_tensor(both, f(s, 0), f(s, 1), ALU.add))
            v.wait_ge(c.filled(1), c.fill(1))
            v.scalar_tensor_tensor(diff, bank(s, 1)[:, :], w("bv"), both, ALU.add, ALU.subtract).then_inc(c.drains(1), 1)
            v.wait_ge(c.drained(1), c.fill(1))
            v.wait_ge(c.drained(0), c.fill(0))
            c.link(v.scalar_tensor_tensor(diff, ar(s, XPAD, T), 1.0, diff, ALU.add, ALU.mult))
            v.scalar_tensor_tensor(o, diff, 0.5, both, ALU.mult, ALU.add).then_inc(c.raises("mixed"), 1)
            v.wait_ge(c.filled(2), c.fill(2))
            x4 = X[s][:, :, :].rearrange("p t d -> p (t d)")
            v.scalar_tensor_tensor(x4, bank(s, 2)[:, :], 0.5, x4, ALU.mult, ALU.add).then_inc(c.drains(2), 1)

        RT = 9800
        probs = lambda s: ar(s, RT, NT * E).rearrange("p (t e) -> p t e", t=NT)
        weight = lambda s: ar(s, RT + 32, NT * E).rearrange("p (t e) -> p t e", t=NT)
        chosen = lambda s: ar(s, RT + 64, NT * E).rearrange("p (t e) -> p t e", t=NT)
        top = lambda s: ar(s, RT + 96, NT)
        whole = lambda s: ar(s, RT + 100, NT)
        rvar = lambda s: ar(s, RT + 104, NT * E)
        rroot = lambda s: ar(s, RT + 136, NT * E).rearrange("p (t e) -> p t e", t=NT)
        pairs = lambda s, k: ar(s, RT + 168 + 256 * k, NT * E * E).rearrange("p (t e j) -> p t e j", t=NT, e=E)
        rparts = lambda s: ar(s, RT + 680, NT * 3 * E, BF16).rearrange("p (t k e) -> p t k e", t=NT, k=3)
        weightT = lambda s: ar(s, RT + 728, T)[0:E, :]
        rrest = lambda s: ar(s, RT + 1240, NT * E).rearrange("p (t e) -> p t e", t=NT)

        def per_expert(ap):
            return ap.unsqueeze(2).to_broadcast([P, NT, E])

        def router_v(c, s, logits, b, j, again):
            p, wt, sel = probs(s), weight(s), chosen(s)
            c.link(v.tensor_reduce(top(s), logits, AXX, ALU.max))
            v.tensor_tensor(p, logits, per_expert(top(s)), ALU.subtract).then_inc(c.drains(b), 1)
            v.wait_ge(c.sem("exped"), c.nth("exped"))
            c.link(v.tensor_reduce(whole(s), p, AXX, ALU.add))
            c.link(v.reciprocal(whole(s), whole(s)))
            c.link(v.tensor_tensor(p, p, per_expert(whole(s)), ALU.mult))
            mine = p.unsqueeze(3).to_broadcast([P, NT, E, E])
            other = p.unsqueeze(2).to_broadcast([P, NT, E, E])
            v.tensor_tensor(pairs(s, 0), other, mine, ALU.is_gt)
            c.link(v.tensor_tensor(pairs(s, 1), other, mine, ALU.is_equal))
            flat0, flat1 = (pairs(s, k).rearrange("p t e j -> p t (e j)") for k in range(2))
            c.link(v.tensor_tensor(flat1, flat1, over_tokens(const("earlier")), ALU.mult))
            c.link(v.tensor_tensor(flat0, flat0, flat1, ALU.add))
            c.link(v.tensor_reduce(sel, pairs(s, 0), AXX, ALU.add))
            c.link(v.tensor_scalar(sel, sel, 1.5, None, ALU.is_lt))
            if again:
                c.link(v.tensor_reduce(top(s), p, AXX, ALU.max))
                v.tensor_tensor(wt, p, per_expert(top(s)), ALU.subtract).then_inc(c.raises("above"), 1)
                v.wait_ge(c.sem("exped_again"), c.nth("exped_again"))
                c.link(v.tensor_tensor(wt, wt, sel, ALU.mult))
            else:
                c.link(v.tensor_tensor(wt, p, sel, ALU.mult))
            c.link(v.tensor_reduce(whole(s), wt, AXX, ALU.add))
            c.link(v.reciprocal(whole(s), whole(s)))
            v.tensor_tensor(wt, wt, per_expert(whole(s)), ALU.mult).then_inc(c.raises("weighed"), 1)

        def router_s(c, s, b, j, again):
            a.wait_ge(c.drained(b), c.fill(b, j))
            a.activation(probs(s), probs(s), ACT.Exp).then_inc(c.raises("exped"), 1)
            if again:
                a.wait_ge(c.sem("above"), c.nth("above"))
                a.activation(weight(s), weight(s), ACT.Exp).then_inc(c.raises("exped_again"), 1)

        def turn_weights(c, s, b, j):
            pe.wait_ge(c.sem("weighed"), c.nth("weighed"))
            pe.wait_ge(c.drained(b), c.fill_before(b, j))
            for t in range(NT):
                last = pe.matmul(bank(s, b)[0:E, t * P:(t + 1) * P], weight(s)[:, t, :], I, is_transpose=True,
                                 start=True, stop=True)
            last.then_inc(c.fills(b), 1)

        Z0, H0B, RB, ACC0, PROD = 0, 1024, 3072, 4096, 4608
        z0 = lambda s, j: ar(s, Z0 + T * j, T)
        h0 = lambda s, e, j: ar(s, H0B + 1024 * (e % 2) + T * j, T)
        rb = lambda s, e: ar(s, RB + T * (e % 2), T)
        acc0 = lambda s: ar(s, ACC0, T).rearrange("p (t d) -> p t d", t=NT)
        rT = lambda s: ar(s, PROD + 512, T, BF16)[0:3 * E, :]
        quad = lambda s: rrest(s)

        def moe0_in_t(c, s, arg):
            pe.wait_ge(c.drained(0), c.fill_past(0))
            pe.wait_ge(c.drained(0), c.fill_before(0))
            for t in range(NT):
                last = pe.matmul(bank(s, 0)[:, t * 16:(t + 1) * 16], WT[s][:, t * P:(t + 1) * P],
                                 Wt[:, W_AT["gate_w"][0]:W_AT["gate_w"][0] + 16], start=True, stop=True)
            last.then_inc(c.fills(0), 1)
            for t in range(NT):
                for k in range(2):
                    pe.wait_ge(c.drained(1 + k), c.fill_before(1 + k, t))
                    pe.matmul(bank(s, 1 + k)[:, :], WT[s][:, t * P:(t + 1) * P], G[:, 4 * k:4 * k + 4, :],
                                       start=True, stop=True).then_inc(c.fills(1 + k), 1)
            turn_weights(c, s, 3, 0)
            pe.wait_ge(c.sem("root_parts"), c.nth("root_parts"))
            pe.wait_ge(c.drained(0), c.fill_before(0, 1))
            for t in range(NT):
                last = pe.matmul(bank(s, 0)[0:3 * E, t * P // 2:(t + 1) * P // 2].bitcast(BF16),
                                 rparts(s)[:, t, :, :].rearrange("p k n -> p (k n)"), identb[:, :],
                                 is_transpose=True, start=True, stop=True)
            last.then_inc(c.fills(0), 1)

        def moe0_in_v(c, s, arg):
            prod = lambda k: ar(s, PROD - 0 + 0, T).rearrange("p (e d) -> p e d", e=4)
            v.wait_ge(c.filled(0), c.fill(0))
            lg = bank(s, 0)[:, 0:64].rearrange("p (t k) -> p t k", t=NT)
            c.link(v.tensor_copy(rroot(s), lg[:, :, E:2 * E]))
            router_v(c, s, lg[:, :, 0:E], 0, 0, False)
            for t in range(NT):
                for k in range(2):
                    v.wait_ge(c.filled(1 + k), c.fill(1 + k, t))
                    v.tensor_tensor(prod(k), bank(s, 1 + k)[:, :].rearrange("p (e d) -> p e d", e=4),
                                            W[s][:, t, :].unsqueeze(1).to_broadcast([P, 4, P]), ALU.mult).then_inc(c.drains(1 + k), 1)
                    v.wait_ge(c.drained(1 + k), c.fill(1 + k, t))
                    c.link(v.tensor_reduce(quad(s)[:, t, 4 * k:4 * k + 4], prod(k), AXX, ALU.add))
            c.link(v.tensor_tensor(quad(s), quad(s), rroot(s), ALU.add))
            v.tensor_tensor(rvar(s).rearrange("p (t e) -> p t e", t=NT), quad(s), over_tokens(ce[:, :]), ALU.add).then_inc(c.raises("expert_var"), 1)
            v.wait_ge(c.sem("expert_root"), c.nth("expert_root"))
            split3(c, rroot(s), [rparts(s)[:, :, k, :] for k in range(3)], rrest(s)).then_inc(c.raises("root_parts"), 1)

        def moe0_in_p(c, s, arg):
            g.wait_ge(c.sem("expert_var"), c.nth("expert_var"))
            g.tensor_tensor(rroot(s).rearrange("p t e -> p (t e)"), rvar(s), mhalf[:, :], ALU.pow).then_inc(c.raises("expert_root"), 1)

        def moe0_in_s(c, s, arg):
            router_s(c, s, 0, 0, False)
            a.wait_ge(c.filled(3), c.fill(3))
            a.copy(weightT(s), bank(s, 3)[0:E, :]).then_inc(c.drains(3), 1)
            a.wait_ge(c.filled(0), c.fill(0, 1))
            a.copy(rT(s), bank(s, 0)[0:3 * E, 0:T // 2].bitcast(BF16)).then_inc(c.drains(0), 1)

        def moe0_t(c, s, e):
            if e == 0:
                pe.wait_ge(c.drained(0), c.fill_past(0))
            pe.wait_ge(c.drained(0), c.fill_before(0))
            pe.matmul(bank(s, 0)[:, :], sel8b[0:3 * E, e:e + 1].to_broadcast([3 * E, P]), rT(s),
                               start=True, stop=True).then_inc(c.fills(0), 1)
            for j in range(2):
                pe.wait_ge(c.drained(1 + j), c.fill_before(1 + j))
                pe.matmul(bank(s, 1 + j)[:, :], w("w1", e * H0 + j * P, P), WT[s][:, :], start=True, stop=True).then_inc(c.fills(1 + j), 1)
            if e:
                moe0_second(c, s, e - 1, 2, 0)

        def moe0_second(c, s, e, back, j0):
            pe.wait_ge(c.sem("hidden"), c.past("hidden", back - 2))
            pe.wait_ge(c.drained(3), c.fill_before(3, j0))
            for t in range(NT):
                for j in range(2):
                    last = pe.matmul(bank(s, 3)[:, t * P:(t + 1) * P], h0(s, e, j)[:, t * P:(t + 1) * P],
                                     w("w2", (e * 2 + j) * P, P), start=j == 0, stop=j == 1)
            last.then_inc(c.fills(3), 1)

        def moe0_s(c, s, e):
            a.wait_ge(c.filled(0), c.fill(0))
            if e >= 2:
                a.wait_ge(c.drained(2), c.fill_past(2, 1))
            a.copy(rb(s, e), bank(s, 0)[:, :]).then_inc(c.drains(0), 1)
            if e >= 2:
                a.wait_ge(c.drained(3), c.fill_past(3))
            for j in range(2):
                a.wait_ge(c.drained(1 + j), c.fill(1 + j))
                a.activation(h0(s, e, j), z0(s, j), ACT.Gelu, bias=w("be_ln1", e * 2 + j, 1),
                                    scale=w("g1", e * 2 + j, 1)).then_inc(c.raises("hidden"), 1)

        def moe0_v(c, s, e):
            v.wait_ge(c.drained(0), c.fill(0))
            if e:
                v.wait_ge(c.sem("hidden"), c.past("hidden"))
            for j in range(2):
                v.wait_ge(c.filled(1 + j), c.fill(1 + j))
                v.scalar_tensor_tensor(z0(s, j), bank(s, 1 + j)[:, :], w("b1", e * 2 + j, 1), rb(s, e),
                                               ALU.add, ALU.mult).then_inc(c.drains(1 + j), 1)
            if e:
                moe0_add(c, s, e - 1, 0)

        def moe0_add(c, s, e, j0):
            v.wait_ge(c.filled(3), c.fill(3, j0))
            if e:
                v.wait_ge(c.drained(3), c.fill_past(3))
            for t in range(NT):
                last = v.scalar_tensor_tensor(acc0(s)[:, t, :], bank(s, 3)[:, t * P:(t + 1) * P], weight(s)[:, t, e:e + 1],
                                              W[s][:, t, :] if e == 0 else acc0(s)[:, t, :], ALU.mult, ALU.add)
            last.then_inc(c.drains(3), 1)

        def moe0_out_t(c, s, arg):
            moe0_second(c, s, E - 1, 2, 0)
            pe.wait_ge(c.drained(0), c.fill_before(0))
            for t in range(NT):
                last = pe.matmul(bank(s, 0)[:, t * P:(t + 1) * P], weightT(s)[:, t * P:(t + 1) * P], w("b2")[0:E, :],
                                 start=True, stop=True)
            last.then_inc(c.fills(0), 1)

        def flat(ap):
            return ap.rearrange("p t d -> p (t d)")

        def finish_norm_v(c, s, acc, o, eps, gain, offset):
            c.link(norm_vector(c, s, acc, o, eps))
            c.link(v.tensor_tensor(o, o, over_tokens(gain), ALU.mult))
            v_ins = v.tensor_tensor(o, o, over_tokens(offset), ALU.add)
            c.link(v_ins)
            v.tensor_tensor(X[s][:, :, :], X[s][:, :, :], o, ALU.add).then_inc(c.raises("added"), 1)

        def moe0_out_v(c, s, arg):
            moe0_add(c, s, E - 1, 0)
            v.wait_ge(c.drained(3), c.fill(3))
            v.wait_ge(c.filled(0), c.fill(0))
            v.tensor_tensor(flat(acc0(s)), flat(acc0(s)), bank(s, 0)[:, :], ALU.add).then_inc(c.drains(0), 1)
            v.wait_ge(c.drained(0), c.fill(0))
            finish_norm_v(c, s, acc0(s), ar(s, PROD, T).rearrange("p (t d) -> p t d", t=NT), 1e-5, row("ln_g"), row("ln_be"))

        def moe0_out_p(c, s, arg):
            norm_pool(c, s)

        QS, KS, QF, KF, QP, KP, VA = 0, 2048, 4096, 4608, 5120, 5888, 6656
        PROBS, NM, NMP, NMR, MT, CN, CT, TMP, TMP2, REC = 7232, 9280, 9344, 9440, 9504, 9760, 10272, 10784, 11296, 11808
        stacks = lambda s, at: ar(s, at, HP * T, BF16).rearrange("p (a t) -> p a t", a=HP)
        three = lambda s, at: ar(s, at, 3 * T, BF16).rearrange("p (k t) -> p k t", k=3)
        vaug = lambda s: ar(s, VA, NT * H * (HD + 1)).rearrange("p (t h d) -> p t h d", t=NT, h=H)
        prob = lambda s, kt: ar(s, PROBS + T * kt, T)
        minus_max = lambda s: ar(s, NM, NT * H).rearrange("p (t h) -> p t h", t=NT)
        max_parts = lambda s: ar(s, NMP, NT * 3 * H, BF16).rearrange("p (t k h) -> p t k h", t=NT, k=3)
        maxT = lambda s: ar(s, MT, T, BF16)[0:3 * H, :]
        context = lambda s: ar(s, CN, T).rearrange("p (t d) -> p t d", t=NT)
        parts_dram = [[dram(f"parts{s}{k}", [3, P, T], BF16) for k in range(2)] for s in range(SLOTS)]
        max_dram = [dram(f"maxima{s}", [3 * H, T], BF16) for s in range(SLOTS)]
        ONES_WORD = float(np.array([0x3F803F80], dtype=np.uint32).view(np.float32)[0])

        def head_rows(h, n):
            return slice(64 * (h % 2), 64 * (h % 2) + n)

        def project_t(c, s, arg):
            pe.wait_ge(c.sem("context"), c.past("context"))
            pe.wait_ge(c.drained(2), c.fill_before(2))
            for t in range(NT):
                last = pe.matmul(bank(s, 2)[:, t * P:(t + 1) * P], context(s)[:, t, :], I, is_transpose=True, start=True, stop=True)
            last.then_inc(c.fills(2), 1)
            pe.wait_ge(c.drained(2), c.fill(2))
            pe.wait_ge(c.drained(3), c.fill_before(3))
            for t in range(NT):
                last = pe.matmul(bank(s, 3)[:, t * P:(t + 1) * P], ar(s, CT + t * P, P), w(arg[0]), start=True, stop=True)
            last.then_inc(c.fills(3), 1)

        def project_s(c, s, arg):
            a.wait_ge(c.filled(2), c.fill(2))
            a.copy(ar(s, CT, T), bank(s, 2)[:, :]).then_inc(c.drains(2), 1)

        def project_v(c, s, arg):
            dst = flat(X[s][:, :, :] if arg[3] == "X" else W[s][:, :, :])
            if arg[1]:
                d3 = X[s][:, :, :] if arg[3] == "X" else W[s][:, :, :]
                c.link(v.tensor_tensor(d3, d3, over_tokens(row(arg[1])), ALU.add))
            v.wait_ge(c.filled(3), c.fill(3))
            v.scalar_tensor_tensor(dst, bank(s, 3)[:, :], arg[2], dst, ALU.mult, ALU.add).then_inc(c.drains(3), 1)

        LQ, LK, LV, LE, LF, LS = 0, 512, 1024, 1600, 2112, 2624
        lin = lambda s, at: ar(s, at, T).rearrange("p (t d) -> p t d", t=NT)

        def linear_t(c, s, arg):
            pe.wait_ge(c.drained(0), c.fill_past(0))
            pe.wait_ge(c.drained(0), c.fill_before(0))
            pe.matmul(bank(s, 0)[:, :], w("lin_Wq"), WT[s][:, :], start=True, stop=True).then_inc(c.fills(0), 1)
            for b, name in ((1, "lin_Wk"), (2, "lin_Wv")):
                pe.wait_ge(c.drained(b), c.fill_before(b))
                for t in range(NT):
                    last = pe.matmul(bank(s, b)[:, t * P:(t + 1) * P], WT[s][:, t * P:(t + 1) * P], w(name), start=True, stop=True)
                last.then_inc(c.fills(b), 1)
            pe.wait_ge(c.sem("features"), c.nth("features"))
            pe.wait_ge(c.drained(3), c.fill_before(3))
            va = ar(s, LV, NT * (P + 1)).rearrange("p (t d) -> p t d", t=NT)
            for t in range(NT):
                last = pe.matmul(bank(s, 3)[:, 0:P + 1], lin(s, LK)[:, t, :], va[:, t, :], start=t == 0, stop=t == NT - 1)
            last.then_inc(c.fills(3), 1)
            pe.wait_ge(c.sem("kv"), c.nth("kv"))
            for b in range(2):
                pe.wait_ge(c.drained(b), c.fill_before(b, 1))
                for t in range(2):
                    tok = 2 * b + t
                    last = pe.matmul(bank(s, b)[:, t * 144:(t + 1) * 144], ar(s, LQ + tok * P, P), ar(s, LS, 144), start=True, stop=True)
                last.then_inc(c.fills(b), 1)

        def linear_v(c, s, arg):
            va = ar(s, LV, NT * (P + 1)).rearrange("p (t d) -> p t d", t=NT)
            v.memset(va[:, :, P:P + 1], 1.0)
            v.wait_ge(c.filled(0), c.fill(0))
            v.tensor_scalar(ar(s, LQ, T), bank(s, 0)[:, :], w("bq_lin"), None, ALU.add).then_inc(c.drains(0), 1)
            v.wait_ge(c.filled(1), c.fill(1))
            v.tensor_tensor(lin(s, LK), bank(s, 1)[:, :].rearrange("p (t d) -> p t d", t=NT), over_tokens(row("lin_bk")), ALU.add).then_inc(c.drains(1), 1)
            v.wait_ge(c.drained(0), c.fill(0))
            v.wait_ge(c.drained(1), c.fill(1))
            v.tensor_scalar(ar(s, LE, T), ar(s, LQ, T), 0.0, None, ALU.min)
            v.tensor_scalar(ar(s, LF, T), ar(s, LK, T), 0.0, None, ALU.min).then_inc(c.raises("negative"), 1)
            v.wait_ge(c.filled(2), c.fill(2))
            v.tensor_tensor(va[:, :, 0:P], bank(s, 2)[:, :].rearrange("p (t d) -> p t d", t=NT), over_tokens(row("lin_bv")), ALU.add).then_inc(c.drains(2), 1)
            v.wait_ge(c.sem("elu"), c.nth("elu"))
            v.scalar_tensor_tensor(ar(s, LQ, T), ar(s, LQ, T), 0.0, ar(s, LE, T), ALU.max, ALU.add)
            v.scalar_tensor_tensor(ar(s, LK, T), ar(s, LK, T), 0.0, ar(s, LF, T), ALU.max, ALU.add).then_inc(c.raises("features"), 1)
            v.wait_ge(c.filled(3), c.fill(3))
            c.link(v.tensor_copy(ar(s, LS + 144, 1), bank(s, 3)[:, P:P + 1]))
            v.tensor_scalar(ar(s, LS + P, H), const("block16"), ar(s, LS + 144, 1), None, ALU.mult)
            v.tensor_tensor(ar(s, LS, P), bank(s, 3)[:, 0:P], const("blocks"), ALU.mult).then_inc(c.drains(3), 1)
            v.wait_ge(c.drained(3), c.fill(3))
            v.memset(ar(s, LS + 145, 1), 0.0).then_inc(c.raises("kv"), 1)
            for b in range(2):
                v.wait_ge(c.filled(b), c.fill(b, 1))
                src = bank(s, b)[:, 0:288].rearrange("p (t k) -> p t k", t=2)
                rec = ar(s, REC, 2 * H).rearrange("p (t h) -> p t h", t=2)
                c.link(v.tensor_scalar(rec, src[:, :, P:P + H], 1e-6, None, ALU.add))
                c.link(v.reciprocal(rec, rec))
                ins = v.tensor_tensor(context(s)[:, 2 * b:2 * b + 2, :].rearrange("p t (h d) -> p t h d", h=H),
                                      src[:, :, 0:P].rearrange("p t (h d) -> p t h d", h=H),
                                      rec.unsqueeze(3).to_broadcast([P, 2, H, HD]), ALU.mult)
                ins.then_inc(c.drains(b), 1)
                v.wait_ge(c.drained(b), c.fill(b, 1))
            v.memset(ar(s, LS + 145, 1), 0.0).then_inc(c.raises("context"), 1)

        def linear_s(c, s, arg):
            a.wait_ge(c.sem("negative"), c.nth("negative"))
            a.activation(ar(s, LE, 2 * T), ar(s, LE, 2 * T), ACT.Exp).then_inc(c.raises("elu"), 1)

        def split_rows(c, s, src, at, name, drain=None):
            parts = three(s, at)
            split3(c, src, [parts[:, k, :] for k in range(3)], ar(s, TMP, T), drain).then_inc(c.raises(name), 1)

        def stack_p(c, s, arg):
            g.wait_ge(c.sem("normed"), c.past("normed"))
            g.memset(ar(s, KS, HP * T // 2), ONES_WORD).then_inc(c.raises("ones"), 1)

        def stack_y(c, s, arg):
            for k, (at, name) in enumerate(((QP, "q_parts"), (KP, "k_parts"))):
                nc.sync.wait_ge(c.sem(name), c.past(name))
                nc.sync.dma_start(parts_dram[s][k].rearrange("k p t -> p k t"), three(s, at)).then_inc(c.raises("parts_out", 16), 16)
            nc.sync.wait_ge(c.sem("parts_out"), c.nth("parts_out", 32))
            nc.sync.wait_ge(c.sem("ones"), c.nth("ones"))
            for k, (at, order) in enumerate(((QS, Q_PARTS), (KS, K_PARTS))):
                src = parts_dram[s][k].rearrange("k (a h r) t -> k h r a t", a=HP, h=2)
                for par in range(2):
                    for n, part in enumerate(order):
                        lo = 64 * par + n * HD
                        nc.sync.dma_start(stacks(s, at)[lo:lo + HD, :, :], src[part, par, :, :, :]).then_inc(c.raises("stacked", 16), 16)

        RC, RSN, RR, KD, KDT, RS = PROBS, PROBS + T, PROBS, PROBS + 2 * T, PROBS + 3 * T, PROBS + 3 * T + 384
        value = lambda s: ar(s, VA, T).rearrange("p (t d) -> p t d", t=NT)
        chunks = lambda ap: ap.rearrange("p (c n) -> p c n", c=NT)

        def tables_y(c, s, arg):
            nc.sync.wait_ge(c.sem("normed"), c.past("normed"))
            for k in range(2):
                nc.sync.dma_start(ar(s, RC + T * k, T), tables[arg + k, :, :]).then_inc(c.raises("table", 16), 16)

        def rotary_t(c, s, names):
            for b, name in enumerate(names):
                pe.wait_ge(c.drained(b), c.fill_before(b))
                pe.matmul(bank(s, b)[:, :], w(name), WT[s][:, :], start=True, stop=True).then_inc(c.fills(b), 1)

        def rotary_v(c, s, biases):
            v.wait_ge(c.sem("table"), c.nth("table", 32))
            for n, dst in enumerate((QF, KF)):
                if n:
                    v.wait_ge(c.sem("rotated"), c.nth("rotated"))
                for k in range(2):
                    b = 2 * n + k
                    v.wait_ge(c.filled(b), c.fill(b))
                    out_ap, table = ar(s, TMP + T * k, T), ar(s, RC + T * k, T)
                    if biases:
                        ins = v.scalar_tensor_tensor(out_ap, bank(s, b)[:, :], w(biases[b]), table, ALU.add, ALU.mult)
                    else:
                        ins = v.tensor_tensor(out_ap, bank(s, b)[:, :], table, ALU.mult)
                    ins.then_inc(c.drains(b), 1)
                    v.wait_ge(c.drained(b), c.fill(b))
                v.tensor_tensor(ar(s, dst, T), ar(s, TMP, T), ar(s, TMP2, T), ALU.add).then_inc(c.raises("rotated"), 1)

        def ret_in_t(c, s, arg):
            pe.wait_ge(c.drained(0), c.fill_past(0))
            rotary_t(c, s, ("ret_Wq", "ret_Wq_rot", "ret_Wk", "ret_Wk_rot"))
            for b, name in ((0, "ret_Wv"), (1, "ret_Wg")):
                pe.wait_ge(c.drained(b), c.fill_before(b, 1))
                for t in range(NT):
                    last = pe.matmul(bank(s, b)[:, t * P:(t + 1) * P], WT[s][:, t * P:(t + 1) * P], w(name), start=True, stop=True)
                last.then_inc(c.fills(b), 1)
            pe.wait_ge(c.sem("k_decayed"), c.nth("k_decayed"))
            pe.wait_ge(c.drained(2), c.fill_before(2, 1))
            for t in range(NT - 1):
                last = pe.matmul(bank(s, 2)[:, t * P:(t + 1) * P], ar(s, KD + t * P, P), I, is_transpose=True, start=True, stop=True)
            last.then_inc(c.fills(2), 1)
            pe.wait_ge(c.drained(0), c.fill(0, 1))
            pe.wait_ge(c.drained(2), c.fill(2, 1))
            pe.wait_ge(c.drained(3), c.fill_before(3, 1))
            for t in range(NT - 1):
                last = pe.matmul(bank(s, 3)[:, t * P:(t + 1) * P], ar(s, KDT + t * P, P), value(s)[:, t, :], start=True, stop=True)
            last.then_inc(c.fills(3), 1)

        def ret_in_s(c, s, arg):
            a.wait_ge(c.filled(0), c.fill(0, 1))
            a.copy(flat(value(s)), bank(s, 0)[:, :]).then_inc(c.drains(0), 1)
            a.wait_ge(c.filled(1), c.fill(1, 1))
            a.copy(ar(s, CT, T), bank(s, 1)[:, :]).then_inc(c.raises("gate"), 1)
            a.activation(ar(s, CN, T), bank(s, 1)[:, :], ACT.Tanh, scale=0.5).then_inc(c.drains(1), 1)
            a.wait_ge(c.filled(2), c.fill(2, 1))
            a.copy(ar(s, KDT, 384), bank(s, 2)[:, 0:384]).then_inc(c.drains(2), 1)

        def ret_in_v(c, s, arg):
            rotary_v(c, s, None)
            v.wait_ge(c.sem("rotated"), c.nth("rotated", 2))
            v.tensor_tensor(chunks(ar(s, KD, T)), chunks(ar(s, KF, T)), over_tokens(const("k_decay")), ALU.mult).then_inc(c.raises("k_decayed"), 1)
            split_rows(c, s, ar(s, QF, T), QP, "q_parts")
            v.wait_ge(c.sem("q_parts"), c.nth("q_parts"))
            split_rows(c, s, ar(s, KF, T), KP, "k_parts")
            v.wait_ge(c.sem("gate"), c.nth("gate"))
            v.wait_ge(c.drained(1), c.fill(1, 1))
            c.link(v.scalar_tensor_tensor(ar(s, CT, T), ar(s, CN, T), 1.0, ar(s, CT, T), ALU.add, ALU.mult))
            v.wait_ge(c.sem("k_parts"), c.nth("k_parts"))
            v.tensor_tensor(chunks(ar(s, TMP, T)), chunks(ar(s, QF, T)), over_tokens(const("q_decay")), ALU.mult).then_inc(c.raises("q_decayed"), 1)
            v.wait_ge(c.filled(3), c.fill(3, 1))
            for k in range(3):
                src = bank(s, 3)[:, k * P:(k + 1) * P]
                dst = ar(s, RS + k * P, P)
                ins = v.tensor_tensor(dst, src, const("blocks"), ALU.mult)
                if k == 2:
                    ins.then_inc(c.drains(3), 1)
                    v.wait_ge(c.drained(3), c.fill(3, 1))
                else:
                    c.link(ins)
                if k:
                    ins = v.scalar_tensor_tensor(dst, ar(s, RS + (k - 1) * P, P), const("gamma_chunk"), dst, ALU.mult, ALU.add)
                    if k < 2:
                        c.link(ins)
                    else:
                        ins.then_inc(c.raises("entering"), 1)

        def ret_head_t(c, s, h):
            if h == 0:
                pe.wait_ge(c.sem("stacked"), c.past("stacked"))
                pe.wait_ge(c.sem("q_decayed"), c.past("q_decayed"))
                pe.wait_ge(c.sem("entering"), c.past("entering"))
                pe.wait_ge(c.drained(2), c.fill_before(2))
                for t in range(1, NT):
                    pe.matmul(bank(s, 2)[:, t * P:(t + 1) * P], ar(s, TMP + t * P, P), ar(s, RS + (t - 1) * P, P),
                              start=t == 1, stop=True, skip_group_check=True)
            r = head_rows(h, NSTACK)
            pe.wait_ge(c.drained(0), c.fill_before(0))
            for t in range(NT):
                last = pe.matmul(bank(s, 0)[:, t * P:(t + 1) * P], stacks(s, KS)[r, h // 2, t * P:(t + 1) * P],
                                 stacks(s, QS)[r, h // 2, t * P:(t + 1) * P], start=True, stop=True)
            last.then_inc(c.fills(0), 1)
            if h:
                ret_values(c, s, h - 1)

        def ret_values(c, s, h):
            pe.wait_ge(c.drained(0), c.fill_past(0))
            for t in range(NT):
                last = pe.matmul(bank(s, 2)[:, t * P + h * HD:t * P + (h + 1) * HD], ar(s, RR + T * (h % 2) + t * P, P),
                                 value(s)[:, t, h * HD:(h + 1) * HD], start=False,
                                 stop=True, skip_group_check=True)
            if h == H - 1:
                last.then_inc(c.fills(2), 1)
            else:
                last.then_inc(c.raises("retained"), 1)

        def ret_head_v(c, s, h):
            if h >= 2:
                v.wait_ge(c.sem("retained"), c.past("retained", 0))
            v.wait_ge(c.filled(0), c.fill(0))
            v.tensor_tensor(chunks(ar(s, RR + T * (h % 2), T)), chunks(bank(s, 0)[:, :]),
                                    over_tokens(const("decay", h * P, P)), ALU.mult).then_inc(c.drains(0), 1)

        def ret_out_t(c, s, arg):
            ret_values(c, s, H - 1)

        def ret_out_v(c, s, arg):
            groups = lambda ap: ap.rearrange("p (n d) -> p n d", d=HD)
            wide = lambda ap: ap.unsqueeze(2).to_broadcast([P, NT * H, HD])
            mean, sq = ar(s, NM, NT * H), ar(s, TMP2, T)
            o = ar(s, CN, T)
            v.wait_ge(c.filled(2), c.fill(2))
            c.link(v.tensor_reduce(mean, groups(bank(s, 2)[:, :]), AXX, ALU.add))
            c.link(v.tensor_scalar(mean, mean, 1.0 / HD, None, ALU.mult))
            v.tensor_tensor(groups(o), groups(bank(s, 2)[:, :]), wide(mean), ALU.subtract).then_inc(c.drains(2), 1)
            v.wait_ge(c.drained(2), c.fill(2))
            c.link(v.tensor_tensor(sq, o, o, ALU.mult))
            c.link(v.tensor_reduce(mean, groups(sq), AXX, ALU.add))
            v.tensor_scalar(mean, mean, 1.0 / HD, 1e-5, ALU.mult, ALU.add).then_inc(c.raises("var"), 1)
            v.wait_ge(c.sem("rstd"), c.nth("rstd"))
            c.link(v.tensor_tensor(groups(o), groups(o), wide(ar(s, NMP, NT * H)), ALU.mult))
            for ins in ((row("gn_w"), ALU.mult), (row("gn_b"), ALU.add)):
                c.link(v.tensor_tensor(context(s), context(s), over_tokens(ins[0]), ins[1]))
            v.tensor_tensor(o, o, ar(s, CT, T), ALU.mult).then_inc(c.raises("context"), 1)

        def ret_out_p(c, s, arg):
            g.wait_ge(c.sem("var"), c.nth("var"))
            g.tensor_tensor(ar(s, NMP, NT * H), ar(s, NM, NT * H), mhalf64[:, :], ALU.pow).then_inc(c.raises("rstd"), 1)

        def query_tiles(causal, kt):
            return kt * P if causal else 0

        def row_max_t(c, s, arg):
            h, causal = arg
            if h == 0:
                pe.wait_ge(c.sem("stacked"), c.past("stacked"))
            r = head_rows(h, NSTACK)
            for qt in range(NT):
                n = (qt + 1) * P if causal else T
                pe.wait_ge(c.drained(qt), c.fill_before(qt))
                last = pe.matmul(bank(s, qt)[:, 0:n], stacks(s, QS)[r, h // 2, qt * P:(qt + 1) * P],
                                 stacks(s, KS)[r, h // 2, 0:n], start=True, stop=not causal)
                if causal:
                    last = pe.matmul(bank(s, qt)[:, qt * P:n], identb[:, :], maskb[:, 0, :], start=False, stop=True)
                last.then_inc(c.fills(qt), 1)

        def row_max_v(c, s, arg):
            h, causal = arg
            for qt in range(NT):
                n = (qt + 1) * P if causal else T
                v.wait_ge(c.filled(qt), c.fill(qt))
                v.tensor_reduce(minus_max(s)[:, qt, h:h + 1], bank(s, qt)[:, 0:n], AXX, ALU.max, negate=True).then_inc(c.drains(qt), 1)

        def max_rows_v(c, s, arg):
            for b in range(4):
                v.wait_ge(c.drained(b), c.fill_past(b))
            split3(c, minus_max(s), [max_parts(s)[:, :, k, :] for k in range(3)],
                          ar(s, NMR, NT * H).rearrange("p (t h) -> p t h", t=NT)).then_inc(c.raises("max_parts"), 1)

        def max_rows_t(c, s, arg):
            pe.wait_ge(c.sem("max_parts"), c.nth("max_parts"))
            pe.wait_ge(c.drained(0), c.fill_before(0))
            for t in range(NT):
                last = pe.matmul(bank(s, 0)[0:3 * H, t * P // 2:(t + 1) * P // 2].bitcast(BF16),
                                 max_parts(s)[:, t, :, :].rearrange("p k h -> p (k h)"), identb[:, :],
                                 is_transpose=True, start=True, stop=True)
            last.then_inc(c.fills(0), 1)

        def max_rows_s(c, s, arg):
            a.wait_ge(c.filled(0), c.fill(0))
            a.copy(maxT(s), bank(s, 0)[0:3 * H, 0:T // 2].bitcast(BF16)).then_inc(c.drains(0), 1)

        def max_rows_y(c, s, arg):
            nc.sync.wait_ge(c.drained(0), c.fill(0))
            nc.sync.dma_start(max_dram[s], maxT(s)).then_inc(c.raises("max_out", 16), 16)
            nc.sync.wait_ge(c.sem("max_out"), c.nth("max_out", 16))
            src = max_dram[s].rearrange("(k a h) t -> h k a t", k=3, a=HP)
            for par in range(2):
                lo = 64 * par + NSTACK
                nc.sync.dma_start(stacks(s, QS)[lo:lo + 3, :, :], src[par, :, :, :]).then_inc(c.raises("max_stacked", 16), 16)

        def attend_t(c, s, arg):
            h, causal = arg
            if h == 0:
                pe.wait_ge(c.sem("max_stacked"), c.past("max_stacked"))
            r = head_rows(h, NMAX)
            for kt in range(NT):
                q0 = query_tiles(causal, kt)
                b = kt % 2
                pe.wait_ge(c.drained(b), c.fill_before(b, kt // 2))
                last = pe.matmul(bank(s, b)[:, 0:T - q0], stacks(s, KS)[r, h // 2, kt * P:(kt + 1) * P],
                                 stacks(s, QS)[r, h // 2, q0:T], start=True, stop=not causal)
                if causal:
                    last = pe.matmul(bank(s, b)[:, 0:P], identb[:, :], maskb[:, 1, :], start=False, stop=True)
                last.then_inc(c.fills(b), 1)
                if kt >= 2:
                    pe.wait_ge(c.drained(kt - 2), c.fill(kt - 2))
                    attend_values(c, s, h, kt - 2, causal)
                elif h:
                    pe.wait_ge(c.drained(kt), c.fill_past(kt))
                    attend_values(c, s, h - 1, kt + 2, causal)

        def attend_values(c, s, h, kt, causal):
            for qt in range(kt if causal else 0, NT):
                if h == 0 and kt == 0 and qt % 2 == 0:
                    pe.wait_ge(c.drained(2 + qt // 2), c.fill_before(2 + qt // 2))
                at = (qt % 2) * 144 + 9 * h
                q0 = qt * P - query_tiles(causal, kt)
                last = pe.matmul(bank(s, 2 + qt // 2)[:, at:at + HD + 1], prob(s, kt)[:, q0:q0 + P], vaug(s)[:, kt, h, :],
                                 start=h == 0 and kt == 0 and qt % 2 == 0, stop=True, skip_group_check=True)
            last.then_inc(c.raises("multiplied"), 1)

        def attend_s(c, s, arg):
            h, causal = arg
            for kt in range(NT):
                n = T - query_tiles(causal, kt)
                a.wait_ge(c.filled(kt % 2), c.fill(kt % 2, kt // 2))
                if h and kt < 2:
                    a.wait_ge(c.sem("multiplied"), c.past("multiplied", 1 - kt))
                elif h:
                    a.wait_ge(c.sem("multiplied"), c.nth("multiplied", kt - 1))
                a.activation(prob(s, kt)[:, 0:n], bank(s, kt % 2)[:, 0:n], ACT.Exp, scale=SCORE_SCALE).then_inc(c.drains(kt % 2), 1)

        def attended_t(c, s, causal):
            for kt in range(2, NT):
                pe.wait_ge(c.drained(kt - 2), c.fill_past(kt - 2))
                attend_values(c, s, H - 1, kt, causal)
            for b in range(2):
                pe.matmul(bank(s, 2 + b)[:, 500:501], identb[:, :], identb[:, 0:1], start=False, stop=True,
                                   skip_group_check=True).then_inc(c.fills(2 + b), 1)

        def attended_v(c, s, arg):
            for b in range(2):
                v.wait_ge(c.filled(2 + b), c.fill(2 + b))
                src = bank(s, 2 + b)[:, 0:288].rearrange("p (t h d) -> p t h d", t=2, h=H)
                rec = ar(s, REC + 32 * b, 2 * H).rearrange("p (t h) -> p t h", t=2)
                c.link(v.reciprocal(rec, src[:, :, :, HD]))
                v.tensor_tensor(context(s)[:, 2 * b:2 * b + 2, :].rearrange("p t (h d) -> p t h d", h=H),
                                        src[:, :, :, 0:HD], rec.unsqueeze(3).to_broadcast([P, 2, H, HD]), ALU.mult).then_inc(c.drains(2 + b), 1)
            v.wait_ge(c.drained(3), c.fill(3))
            v.memset(ar(s, REC + 64, 1), 0.0).then_inc(c.raises("context"), 1)

        def attn_in_t(c, s, arg):
            pe.wait_ge(c.drained(0), c.fill_past(0))
            for b, name in ((0, "f_Wq"), (1, "f_Wk")):
                pe.wait_ge(c.drained(b), c.fill_before(b))
                pe.matmul(bank(s, b)[:, :], w(name), WT[s][:, :], start=True, stop=True).then_inc(c.fills(b), 1)
            pe.wait_ge(c.drained(2), c.fill_before(2))
            for t in range(NT):
                last = pe.matmul(bank(s, 2)[:, t * P:(t + 1) * P], WT[s][:, t * P:(t + 1) * P], w("f_Wv"), start=True, stop=True)
            last.then_inc(c.fills(2), 1)

        def split_heads(ap):
            return ap.rearrange("p (t h d) -> p t h d", t=NT, h=H)

        def attn_in_v(c, s, arg):
            v.wait_ge(c.filled(0), c.fill(0))
            split_rows(c, s, bank(s, 0)[:, :], QP, "q_parts", (0, 0))
            v.wait_ge(c.sem("q_parts"), c.nth("q_parts"))
            v.wait_ge(c.filled(1), c.fill(1))
            split_rows(c, s, bank(s, 1)[:, :], KP, "k_parts", (1, 0))
            v.memset(vaug(s)[:, :, :, HD:HD + 1], 1.0)
            v.wait_ge(c.filled(2), c.fill(2))
            v.tensor_copy(vaug(s)[:, :, :, 0:HD], split_heads(bank(s, 2)[:, :])).then_inc(c.drains(2), 1)

        HB1, OT1, ACC1, O1 = 0, 4096, 4608, 5120
        h1 = lambda s, e, j: ar(s, HB1 + 2048 * (e % 2) + T * j, T)
        acc1 = lambda s: ar(s, ACC1, T).rearrange("p (t d) -> p t d", t=NT)
        o1 = lambda s: ar(s, O1, T).rearrange("p (t d) -> p t d", t=NT)

        def moe1_in_v(c, s, arg):
            v.wait_ge(c.drained(3), c.fill_past(3))
            c.link(norm_vector(c, s, W[s], o1(s), 1e-6))
            c.link(v.tensor_tensor(o1(s), o1(s), over_tokens(row("f_ln1g")), ALU.mult))
            v.tensor_tensor(o1(s), o1(s), over_tokens(row("f_ln1b")), ALU.add).then_inc(c.raises("normed"), 1)
            v.wait_ge(c.filled(1), c.fill(1))
            router_v(c, s, bank(s, 1)[:, 0:NT * E].rearrange("p (t e) -> p t e", t=NT), 1, 0, True)

        def moe1_in_p(c, s, arg):
            norm_pool(c, s)

        def moe1_in_t(c, s, arg):
            pe.wait_ge(c.sem("normed"), c.nth("normed"))
            pe.wait_ge(c.drained(0), c.fill_before(0))
            turn(c, s, o1(s), 0, identity=I)
            pe.wait_ge(c.drained(0), c.fill(0))
            pe.wait_ge(c.drained(1), c.fill_before(1))
            for t in range(NT):
                last = pe.matmul(bank(s, 1)[:, t * E:(t + 1) * E], ar(s, OT1 + t * P, P), w("f_Wr"), start=True, stop=True)
            last.then_inc(c.fills(1), 1)
            turn_weights(c, s, 3, 0)

        def moe1_in_s(c, s, arg):
            a.wait_ge(c.filled(0), c.fill(0))
            a.copy(ar(s, OT1, T), bank(s, 0)[:, :]).then_inc(c.drains(0), 1)
            router_s(c, s, 1, 0, True)
            a.wait_ge(c.filled(3), c.fill(3))
            a.copy(weightT(s), bank(s, 3)[0:E, :]).then_inc(c.drains(3), 1)

        def moe1_t(c, s, e):
            for j in range(4):
                pe.wait_ge(c.drained(j % 2), c.fill_before(j % 2, j // 2))
                pe.matmul(bank(s, j % 2)[:, :], w("We1", e * H1 + j * P, P), ar(s, OT1, T), start=True, stop=True).then_inc(c.fills(j % 2), 1)
            if e:
                moe1_second(c, s, e - 1)

        def moe1_second(c, s, e):
            pe.wait_ge(c.drained(1), c.fill_past(1))
            pe.wait_ge(c.drained(2), c.fill_before(2))
            for t in range(NT):
                for j in range(4):
                    last = pe.matmul(bank(s, 2)[:, t * P:(t + 1) * P], h1(s, e, j)[:, t * P:(t + 1) * P],
                                     w("We2", (e * 4 + j) * P, P), start=j == 0, stop=j == 3)
            last.then_inc(c.fills(2), 1)

        def moe1_s(c, s, e):
            if e >= 2:
                a.wait_ge(c.filled(2), c.fill_past(2))
            for j in range(4):
                a.wait_ge(c.filled(j % 2), c.fill(j % 2, j // 2))
                a.activation(h1(s, e, j), bank(s, j % 2)[:, :], ACT.Gelu, bias=w("be1", e * 4 + j, 1)).then_inc(c.drains(j % 2), 1)

        def moe1_v(c, s, e):
            if e:
                moe1_add(c, s, e - 1)

        def moe1_add(c, s, e):
            v.wait_ge(c.filled(2), c.fill(2))
            if e:
                v.wait_ge(c.drained(2), c.fill_past(2))
            for t in range(NT):
                last = v.scalar_tensor_tensor(acc1(s)[:, t, :], bank(s, 2)[:, t * P:(t + 1) * P], weight(s)[:, t, e:e + 1],
                                              o1(s)[:, t, :] if e == 0 else acc1(s)[:, t, :], ALU.mult, ALU.add)
            last.then_inc(c.drains(2), 1)

        def moe1_out_t(c, s, arg):
            moe1_second(c, s, E - 1)
            pe.wait_ge(c.drained(3), c.fill_before(3))
            for t in range(NT):
                last = pe.matmul(bank(s, 3)[:, t * P:(t + 1) * P], weightT(s)[:, t * P:(t + 1) * P], w("f_b2")[0:E, :],
                                 start=True, stop=True)
            last.then_inc(c.fills(3), 1)

        def moe1_out_v(c, s, arg):
            moe1_add(c, s, E - 1)
            v.wait_ge(c.drained(2), c.fill(2))
            v.wait_ge(c.filled(3), c.fill(3))
            v.tensor_tensor(flat(acc1(s)), flat(acc1(s)), bank(s, 3)[:, :], ALU.add).then_inc(c.drains(3), 1)
            v.wait_ge(c.drained(3), c.fill(3))
            finish_norm_v(c, s, acc1(s), ar(s, 5632, T).rearrange("p (t d) -> p t d", t=NT), 1e-6, row("f_ln2g"), row("f_ln2b"))

        LATENT = ("bqr", "bqr_rot", "bkr", "bkr_rot")

        def lat_in_t(c, s, arg):
            pe.wait_ge(c.drained(0), c.fill_past(0))
            rotary_t(c, s, ("lat_wqr", "lat_wqr_rot", "lat_wkr", "lat_wkr_rot"))
            pe.wait_ge(c.drained(0), c.fill_before(0, 1))
            pe.matmul(bank(s, 0)[0:32, :], w("lat_wkv"), WT[s][:, :], start=True, stop=True).then_inc(c.fills(0), 1)
            pe.wait_ge(c.drained(0), c.fill(0, 1))
            pe.wait_ge(c.drained(1), c.fill_before(1, 1))
            for t in range(NT):
                last = pe.matmul(bank(s, 1)[:, t * P:(t + 1) * P], ar(s, CT + t * P, P)[0:32, :], w("lat_wv")[0:32, :],
                                 start=True, stop=True)
            last.then_inc(c.fills(1), 1)

        def lat_in_s(c, s, arg):
            for k, at in enumerate((QF, KF)):
                a.wait_ge(c.sem("rotated"), c.nth("rotated", k + 1))
                a.activation(ar(s, at, T), ar(s, at, T), ACT.Gelu).then_inc(c.raises("activated"), 1)
                if k == 0:
                    a.wait_ge(c.filled(0), c.fill(0, 1))
                    a.activation(ar(s, CT, T)[0:32, :], bank(s, 0)[0:32, :], ACT.Gelu, bias=w("bkv")[0:32, :]).then_inc(c.drains(0), 1)

        def lat_in_v(c, s, arg):
            rotary_v(c, s, LATENT)
            v.memset(vaug(s)[:, :, :, HD:HD + 1], 1.0)
            v.wait_ge(c.filled(1), c.fill(1, 1))
            bias = row("lat_bv").rearrange("p (h d) -> p h d", h=H)
            v.tensor_tensor(vaug(s)[:, :, :, 0:HD], split_heads(bank(s, 1)[:, :]),
                                    bias.unsqueeze(1).to_broadcast([P, NT, H, HD]), ALU.add).then_inc(c.drains(1), 1)
            v.wait_ge(c.sem("rotated"), c.nth("rotated", 2))
            v.wait_ge(c.sem("activated"), c.nth("activated", 1))
            split_rows(c, s, ar(s, QF, T), QP, "q_parts")
            v.wait_ge(c.sem("q_parts"), c.nth("q_parts"))
            v.wait_ge(c.sem("activated"), c.nth("activated", 2))
            split_rows(c, s, ar(s, KF, T), KP, "k_parts")

        VECTOR = {"norm": norm_v, "mamba_in": mamba_in_v, "mamba_dir": mamba_dir_v, "scan": scan_v, "scan_first": scan_v,
                  "mamba_out": mamba_out_v, "combine": combine_v}
        POOL = {"norm": norm_p, "mamba_in": mamba_in_p, "scan": scan_p, "scan_first": scan_p}
        TENSOR = {"norm": norm_t, "mamba_in": mamba_in_t, "mamba_dir": mamba_dir_t, "scan": scan_t, "scan_first": scan_t,
                  "mamba_out": mamba_out_t, "combine": combine_t}
        SCALAR = {"norm": norm_s, "mamba_in": mamba_in_s, "mamba_dir": mamba_dir_s, "scan": scan_s, "scan_first": scan_s, "combine": combine_s}
        VECTOR.update({"moe0_in": moe0_in_v, "moe0": moe0_v, "moe0_first": moe0_v, "moe0_out": moe0_out_v})
        POOL.update({"moe0_in": moe0_in_p, "moe0_out": moe0_out_p})
        TENSOR.update({"moe0_in": moe0_in_t, "moe0": moe0_t, "moe0_first": moe0_t, "moe0_out": moe0_out_t})
        SCALAR.update({"moe0_in": moe0_in_s, "moe0": moe0_s, "moe0_first": moe0_s})
        VECTOR.update({"project": project_v, "linear": linear_v, "ret_in": ret_in_v, "ret_head_first": ret_head_v,
                       "ret_head": ret_head_v, "ret_out": ret_out_v})
        POOL.update({"stack": stack_p, "ret_out": ret_out_p})
        TENSOR.update({"project": project_t, "linear": linear_t, "ret_in": ret_in_t, "ret_head_first": ret_head_t,
                       "ret_head": ret_head_t, "ret_out": ret_out_t})
        SCALAR.update({"project": project_s, "linear": linear_s, "ret_in": ret_in_s})
        VECTOR.update({"attn_in": attn_in_v, "lat_in": lat_in_v, "row_max": row_max_v, "max_rows": max_rows_v,
                       "attended": attended_v, "moe1_in": moe1_in_v, "moe1": moe1_v, "moe1_out": moe1_out_v})
        POOL.update({"moe1_in": moe1_in_p, "moe1_out": moe1_in_p})
        TENSOR.update({"attn_in": attn_in_t, "lat_in": lat_in_t, "row_max": row_max_t, "max_rows": max_rows_t,
                       "attend_first": attend_t, "attend": attend_t, "attended": attended_t, "moe1_in": moe1_in_t,
                       "moe1_first": moe1_t, "moe1": moe1_t, "moe1_out": moe1_out_t})
        SCALAR.update({"lat_in": lat_in_s, "max_rows": max_rows_s, "attend_first": attend_s, "attend": attend_s,
                       "moe1_in": moe1_in_s, "moe1_first": moe1_s, "moe1": moe1_s})
        SYNC = {"lat_in": lambda c, s, arg: tables_y(c, s, 2), "max_rows": max_rows_y, "stack": stack_y, "ret_in": lambda c, s, arg: tables_y(c, s, 0)}

        setup = setup_sems
        WEIGHT_LOADS = 3 * 16

        ones = arena[0][:, 64:64 + P]
        b1_sq, sq_sum = arena[0][:, 16:32], arena[0][:, 32:40]
        b1_sum = arena[0][:, 40:48]
        w1T = arena[0][:, 256:512]

        block = stack.enter_context(nc.Block())

        @block.sync
        def _(sp):
            sp.dma_start(Ct[:, :], consts).then_inc(setup["weights_loaded"], 16)
            sp.dma_start(Wt[:, :], wts).then_inc(setup["weights_loaded"], 16)
            sp.dma_start(Rt[:, :], rows.to_broadcast([P, R_WIDTH])).then_inc(setup["weights_loaded"], 16)
            with sp.Fori(0, x.shape[0]) as pair:
                def load(c, s, arg):
                    sp.dma_start(X[s][:, :, :], x[pair, s, :, :].rearrange("(t p) d -> p t d", p=P)).then_inc(c.raises("x_loaded", 16), 16)

                def store(c, s, arg):
                    residual_ready(c)
                    sp.dma_start(out[pair, s, :, :].rearrange("(t p) d -> p t d", p=P), X[s][:, :, :]).then_inc(c.raises("x_stored", 16), 16)
                    sp.wait_ge(c.sem("x_stored"), c.nth("x_stored", 16))

                run(sp, None, {"load": load, "store": store, **SYNC})
                leave(sp, clears=True)

        @block.gpsimd
        def _(pool):
            pool.memset(mhalf64[:, :], -0.5).then_inc(setup["mhalf_ready"], 1)
            pool.wait_ge(setup["mhalf_ready"], 1)
            with pool.Fori(0, x.shape[0]):
                run(pool, chains["gpsimd"], POOL)
                leave(pool)

        @block.scalar
        def _(act):
            act.wait_ge(setup["weights_loaded"], WEIGHT_LOADS)
            act.activation(w("A"), w("A"), ACT.Exp).then_inc(setup["A_exp"], 1)
            act.wait_ge(setup["halved"], 1)
            with act.Fori(0, x.shape[0]):
                run(act, chains["scalar"], SCALAR)
                leave(act)

        @block.vector
        def _(dve):
            c = Cursor(prog, dve, 0, 0, setup_chain)
            dve.wait_ge(setup["weights_loaded"], WEIGHT_LOADS)
            for src, dst in ((w("b_in"), half_bin[:, :]), (w("bg"), half_bg[:, :]), (w("conv_w"), w("conv_w")),
                             (w("conv_b"), w("conv_b"))):
                v.tensor_scalar(dst, src, 0.5, None, ALU.mult)
            v.tensor_copy(identb[:, :], I)
            v.memset(ones, 1.0)
            v.tensor_reduce(b1_sum, w("b1").rearrange("p (e j) -> p e j", j=2), AXX, ALU.add).then_inc(setup["consts_ready"], 1)
            v.tensor_copy(selb[:, :], const("sel32")[0:96, :])
            v.tensor_copy(sel8b[:, :], const("sel8")[0:3 * E, :])
            v.tensor_copy(maskb[:, 0, :], const("mask_q"))
            v.tensor_copy(maskb[:, 1, :], const("mask_k"))
            dve.wait_ge(setup["A_exp"], 1)
            v.tensor_scalar(w("A"), w("A"), -1.0, None, ALU.mult).then_inc(setup["halved"], 1)
            dve.wait_ge(setup["halved"], 1)
            w1 = w("w1").rearrange("p (e n) -> p e n", e=E)
            mean = arena[0][:, 0:E]
            c.link(v.tensor_reduce(mean, w1, AXX, ALU.add))
            c.link(v.tensor_scalar(mean, mean, 1.0 / H0, None, ALU.mult))
            v.tensor_tensor(w1, w1, mean.unsqueeze(2).to_broadcast([P, E, H0]), ALU.subtract).then_inc(setup["centred"], 1)
            dve.wait_ge(setup["w1_turned"], 1)
            v.scalar_tensor_tensor(w("b1").rearrange("p (e j) -> p e j", j=2), banks[0][0][:, 0:E].unsqueeze(2).to_broadcast([P, E, 2]), -1.0 / H0,
                                   w("b1").rearrange("p (e j) -> p e j", j=2), ALU.mult, ALU.add).then_inc(setup["centred"], 1)
            dve.wait_ge(setup["centred"], 2)
            c.link(v.tensor_tensor(b1_sq, w("b1"), w("b1"), ALU.mult))
            v.tensor_reduce(sq_sum, b1_sq.rearrange("p (e j) -> p e j", j=2), AXX, ALU.add).then_inc(setup["sq_ready"], 1)
            for e in range(E):
                dve.wait_ge(setup["w1_turned"], 2 + e)
                if e:
                    dve.wait_ge(setup["gram"], e)
                v.tensor_copy(w1T, banks[0][1][:, 0:2 * P]).then_inc(setup["w1T_ready"], 1)
                dve.wait_ge(setup["gram"], e + 1)
                v.tensor_scalar(G[:, e, :], banks[0][2][:, 0:P], 1.0 / H0, None, ALU.mult)
                v.tensor_scalar(w("v2", e, 1), banks[0][3][:, 0:1], 2.0 / H0, None, ALU.mult).then_inc(setup["gram_ready"], 1)
            dve.wait_ge(setup["w1_turned"], 2 + E)
            v.tensor_scalar(ce[:, :], banks[0][0][:, 0:E], 1.0 / H0, 1e-5, ALU.mult, ALU.add).then_inc(setup["gram_ready"], 1)
            dve.wait_ge(setup["gram_ready"], E + 1)
            with dve.Fori(0, x.shape[0]):
                run(dve, chains["vector"], VECTOR)
                leave(dve)

        @block.tensor
        def _(ten):
            ten.wait_ge(setup["weights_loaded"], WEIGHT_LOADS)
            ten.wait_ge(setup["halved"], 1)
            ten.wait_ge(setup["consts_ready"], 1)
            pe.matmul(banks[0][0][:, 0:E], ones, b1_sum, start=True, stop=True).then_inc(setup["w1_turned"], 1)
            ten.wait_ge(setup["centred"], 2)
            for e in range(E):
                if e:
                    ten.wait_ge(setup["w1T_ready"], e)
                for j in range(2):
                    last = pe.matmul(banks[0][1][:, j * P:(j + 1) * P], w("w1", e * H0 + j * P, P), I, is_transpose=True,
                                     start=True, stop=True)
                last.then_inc(setup["w1_turned"], 1)
                ten.wait_ge(setup["w1T_ready"], e + 1)
                if e:
                    ten.wait_ge(setup["gram_ready"], e)
                for j in range(2):
                    pe.matmul(banks[0][2][:, 0:P], w1T[:, j * P:(j + 1) * P], w1T[:, j * P:(j + 1) * P], start=j == 0, stop=j == 1)
                for j in range(2):
                    last = pe.matmul(banks[0][3][:, 0:1], w1T[:, j * P:(j + 1) * P], w("b1", e * 2 + j, 1), start=j == 0, stop=j == 1)
                last.then_inc(setup["gram"], 1)
            ten.wait_ge(setup["sq_ready"], 1)
            pe.matmul(banks[0][0][:, 0:E], ones, sq_sum, start=True, stop=True).then_inc(setup["w1_turned"], 1)
            ten.wait_ge(setup["gram_ready"], E + 1)
            with ten.Fori(0, x.shape[0]):
                run(ten, None, TENSOR)
                leave(ten)

        prog.check()


def _pack(np, sections, parts):
    out = []
    for name, width in sections:
        a = parts[name]
        a = a.reshape(a.shape[0], -1)
        assert a.shape[1] == width, (name, a.shape, width)
        if a.shape[0] < P:
            a = np.concatenate([a, np.zeros((P - a.shape[0], width), a.dtype)], 0)
        out.append(a)
    return np.ascontiguousarray(np.concatenate(out, 1))


def _constants(np):
    f = np.float32
    p, q = np.arange(P)[:, None], np.arange(P)[None, :]
    gamma = 1.0 - 2.0 ** (-5.0 - np.arange(H))
    head = np.arange(P) // HD
    c = {
        "ident": (p == q), "anti": (p + q == P - 1),
        "sel32": np.arange(P)[:, None] % 32 == np.arange(32)[None, :],
        "sel8": np.arange(P)[:, None] % 8 == np.arange(8)[None, :],
        "mask_q": np.where(q > p, MASKED, 0.0), "mask_k": np.where(p > q, MASKED, 0.0),
        "blocks": head[:, None] == head[None, :], "block16": head[:, None] == np.arange(H)[None, :],
        "earlier": np.broadcast_to((np.arange(E)[None, :] < np.arange(E)[:, None]).reshape(1, -1), (P, E * E)),
        "gamma_chunk": (gamma[head] ** P)[:, None],
        "k_decay": gamma[head][:, None] ** (P - q), "q_decay": gamma[head][:, None] ** q * SCORE_SCALE,
        "decay": np.where((q >= p)[:, None, :], gamma[None, :, None] ** np.maximum(q - p, 0)[:, None, :], 0.0) * SCORE_SCALE,
    }
    packed = _pack(np, CONSTS, {k: np.asarray(v, dtype=f) for k, v in c.items()})

    def rope(width, features):
        inv = (1.0 / f(10000.0) ** (np.arange(0, width, 2, dtype=f) / f(width))).astype(f)
        freqs = (np.arange(T, dtype=f)[:, None] * inv[None, :]).astype(f)
        emb = np.concatenate([freqs, freqs], -1)
        cos, sin = np.cos(emb).astype(f), np.sin(emb).astype(f)
        sin = sin * np.where(np.arange(width) < width // 2, f(-1), f(1))[None, :]
        return np.tile(cos, (1, features // width)).T, np.tile(sin, (1, features // width)).T

    tables = np.stack([*rope(HD, P), *rope(P, P)]).astype(f)
    return packed, np.ascontiguousarray(tables)


def _weights(np, i):
    def halves(a):
        return a.reshape(2, P, -1).transpose(1, 0, 2)

    def per_dir(name, rows):
        a = i["L0_attn_a_" + name]
        return np.stack([a[d].reshape(-1, P).T for d in range(2)], 1) if rows else a

    A = "L0_attn_a_"
    rot8 = np.concatenate([np.roll(np.arange(HD * h, HD * h + HD), HD // 2) for h in range(H)])
    rot = np.roll(np.arange(P), P // 2)
    col = lambda a: a.reshape(-1, P).T
    both = lambda a, fn: np.stack([fn(a[d]) for d in range(2)], 1)
    F0, F1, R, L, N = "L0_ffn_", "L1_ffn_", "L1_attn_a_", "L1_attn_b_", "L0_attn_b_"
    return {
        "ln_w": i[A + "ln_w"].T, "ln_b": i[A + "ln_b"].T, "b_in": both(i[A + "b_in"], col),
        "conv_w": both(i[A + "conv_w"], halves), "conv_b": both(i[A + "conv_b"], col),
        "b_dt": both(i[A + "b_dt"], col), "A": both(i[A + "A_log"], halves), "D": both(i[A + "D"], col),
        "b_out": i[A + "b_out"].T, "bg": col(i[A + "bg"]), "bv": col(i[A + "bv"]), "bq_lin": col(i[N + "bq"]),
        "b1": i[F0 + "b1"].reshape(-1, P).T, "g1": i[F0 + "ln1_g"].reshape(-1, P).T,
        "be_ln1": i[F0 + "ln1_b"].reshape(-1, P).T, "be1": i[F1 + "be1"].reshape(-1, P).T,
        "bqr": col(i[L + "bqr"]), "bqr_rot": col(i[L + "bqr"])[rot], "bkr": col(i[L + "bkr"]),
        "bkr_rot": col(i[L + "bkr"])[rot], "bkv": i[L + "bkv"].reshape(-1, 1),
        "W_in": both(i[A + "W_in"], lambda a: a), "W_x": both(i[A + "W_xproj"], halves),
        "W_dt": both(i[A + "W_dt"], lambda a: a), "W_out": both(i[A + "W_out"], halves),
        "Wg": halves(i[A + "Wg"]), "Wv": halves(i[A + "Wv"]),
        "gate_w": i[F0 + "gate_w"], "v2": np.zeros((P, E), np.float32),
        "w1": i[F0 + "w1"].transpose(1, 0, 2), "w2": i[F0 + "w2"].reshape(E, 2, P, P).transpose(2, 0, 1, 3),
        "b2": i[F0 + "b2"],
        "lin_Wq": i[N + "Wq"].T, "lin_Wk": i[N + "Wk"].T, "lin_Wv": i[N + "Wv"].T, "lin_Wo": i[N + "Wo"].T,
        "ret_Wq": i[R + "Wq"].T, "ret_Wq_rot": i[R + "Wq"].T[:, rot8], "ret_Wk": i[R + "Wk"].T,
        "ret_Wk_rot": i[R + "Wk"].T[:, rot8], "ret_Wv": i[R + "Wv"].T, "ret_Wg": i[R + "Wg"].T,
        "ret_Wo": i[R + "Wo"].T,
        "f_Wq": i[F1 + "Wq"], "f_Wk": i[F1 + "Wk"], "f_Wv": i[F1 + "Wv"], "f_Wo": i[F1 + "Wo"],
        "f_Wr": i[F1 + "Wr"], "f_b2": i[F1 + "be2"],
        "lat_wqr": i[L + "wqr"], "lat_wqr_rot": i[L + "wqr"][:, rot], "lat_wkr": i[L + "wkr"],
        "lat_wkr_rot": i[L + "wkr"][:, rot], "lat_wkv": i[L + "wkv"], "lat_wv": i[L + "wv"], "lat_wo": i[L + "wo"],
        "We1": i[F1 + "We1"].transpose(1, 0, 2), "We2": i[F1 + "We2"].reshape(E, 4, P, P).transpose(2, 0, 1, 3),
    }, {
        "lin_bk": i[N + "bk"], "lin_bv": i[N + "bv"], "lin_bo": i[N + "bo"], "ln_g": i[F0 + "ln_g"], "ln_be": i[F0 + "ln_b"],
        "gn_w": i[R + "gn_w"], "gn_b": i[R + "gn_b"], "f_bo": i[F1 + "bo"], "f_ln1g": i[F1 + "ln1_g"],
        "f_ln1b": i[F1 + "ln1_b"], "f_ln2g": i[F1 + "ln2_g"], "f_ln2b": i[F1 + "ln2_b"],
        "lat_bv": i[L + "bv"], "lat_bo": i[L + "bo"],
    }


def kernel(**inputs):
    import numpy as np
    import concourse.bacc as bacc
    from concourse.bass_utils import run_bass_kernel_spmd

    i = {k: np.asarray(v) for k, v in inputs.items()}
    weights, rows = _weights(np, i)
    consts, tables = _constants(np)
    x = i["L0_attn_a_x"]
    arrays = {
        "x": np.ascontiguousarray(x.reshape(x.shape[0] // SLOTS, SLOTS, T, P)),
        "wts": _pack(np, WEIGHTS, weights),
        "rows": np.ascontiguousarray(np.concatenate([rows[n].reshape(1, -1) for n, _ in ROWS], 1)),
        "consts": consts, "tables": tables,
    }
    nc = bacc.Bacc("TRN2", target_bir_lowering=False, num_devices=1)
    ins = [nc.dram_tensor("in_" + n, a.shape, FP32, kind="ExternalInput").ap() for n, a in arrays.items()]
    out = nc.dram_tensor("out", arrays["x"].shape, FP32, kind="ExternalOutput").ap()
    network(nc, *ins, out)
    r = run_bass_kernel_spmd(nc, [{"in_" + n: a for n, a in arrays.items()}], core_ids=[0])
    return r.results[0]["out"].reshape(x.shape)
```

```python
import concourse.bass as bass
from concourse import mybir
from contextlib import ExitStack
import numpy as np


FP32 = mybir.dt.float32
BF16 = mybir.dt.bfloat16
ALU = mybir.AluOpType
ACT = mybir.ActivationFunctionType
AXX = mybir.AxisListType.X

P = 128
T = 512
NT = T // P
SLOTS = 2
H = 16
HD = P // H
HP = H // 2
E = 8
DI = 2 * P
NS = 16
RK = 64
H0 = 256
H1 = 512
TAPS = 4
GROUP_ROWS = 3 * 32 + HD + 1
PADW = T + TAPS - 1
SCORE_SCALE = float(HD) ** -0.5
MASKED = -1.0e30

RUNS = ((0, 3), (3, 2), (5, 1))
NSTACK = 6 * HD
NMAX = NSTACK + 3


def layout(sections):
    at, where = 0, {}
    for name, width in sections:
        where[name] = (at, width)
        at += width
    return where, at


WEIGHTS = [
    ("ln_w", 2), ("ln_b", 2), ("b_in", 8), ("conv_w", 4 * TAPS), ("conv_b", 4), ("b_dt", 4),
    ("A", 4 * NS), ("D", 4), ("b_out", 2), ("bg", 1), ("bv", 1), ("bq_lin", 1),
    ("b1", 2 * E), ("g1", 2 * E), ("be_ln1", 2 * E), ("be1", 4 * E),
    ("bqr", 1), ("bqr_rot", 1), ("bkr", 1), ("bkr_rot", 1), ("bkv", 1),
    ("W_in", 2 * 2 * DI), ("W_x", 2 * 2 * (RK + 2 * NS)), ("W_dt", 2 * DI), ("W_out", 2 * 2 * P),
    ("Wg", 2 * P), ("Wv", 2 * P),
    ("gate_w", E), ("v2", E), ("w1", E * H0), ("w2", E * 2 * P), ("b2", P),
    ("lin_Wq", P), ("lin_Wk", P), ("lin_Wv", P), ("lin_Wo", P),
    ("ret_Wq", P), ("ret_Wq_rot", P), ("ret_Wk", P), ("ret_Wk_rot", P), ("ret_Wv", P),
    ("ret_Wg", P), ("ret_Wo", P),
    ("f_Wq", P), ("f_Wk", P), ("f_Wv", P), ("f_Wo", P), ("f_Wr", E), ("f_b2", P),
    ("lat_wqr", P), ("lat_wqr_rot", P), ("lat_wkr", P), ("lat_wkr_rot", P),
    ("lat_wkv", 32), ("lat_wv", P), ("lat_wo", P),
    ("We1", E * H1), ("We2", E * 4 * P),
]
W_AT, W_WIDTH = layout(WEIGHTS)

ROWS = [
    ("lin_bk", P), ("lin_bv", P), ("lin_bo", P), ("ln_g", P), ("ln_be", P), ("gn_w", P), ("gn_b", P),
    ("f_bo", P), ("f_ln1g", P), ("f_ln1b", P), ("f_ln2g", P), ("f_ln2b", P), ("lat_bv", P), ("lat_bo", P),
]
R_AT, R_WIDTH = layout(ROWS)

CONSTS = [
    ("ident", P), ("anti", P), ("sel32", 2 * NS), ("sel8", E), ("mask_q", P), ("mask_k", P),
    ("blocks", P), ("block16", H), ("earlier", E * E), ("gamma_chunk", 1),
    ("k_decay", P), ("q_decay", P), ("decay", H * P),
]
C_AT, C_WIDTH = layout(CONSTS)
TABLES = ("ret_cos", "ret_sin", "lat_cos", "lat_sin")

NORM = {"var": 1, "rstd": 1, "normed": 1, "bank0": 1}
RAISES = {
    "rest": {},
    "load": {"x_loaded": 16},
    "norm": NORM,
    "mamba_in": {"var": 1, "rstd": 1, "normed": 1, "bank0": 1, "bank1": 1},
    "mamba_dir": {"gate_tanh": 1, "conv": 1, "conv_tanh": 1, "conv_out": 1,
                  "bc_parts": 1, "minus_abs": 1, "exp_abs": 1, "one_plus": 1, "log": 1, "delta": 1,
                  "bank0": 2, "bank1": 3, "bank2": 2, "bank3": 2},
    "scan": {"decay_ready": 1, "state": 1, "state_c": 1, "summed": 1, "bank0": 1, "bank1": 1},
    "scan_first": {"decay_ready": 1, "state": 1, "state_c": 1, "bank0": 1, "bank1": 1},
    "mamba_out": {"summed": 1, "gated": 1, "bank0": 1, "bank2": 1, "bank3": 1},
    "combine": {"mixed": 1, "bank0": 1, "bank1": 1, "bank2": 1},
    "moe0_in": {"exped": 1, "weighed": 1, "expert_var": 1, "expert_root": 1, "root_parts": 1,
                "bank0": 2, "bank1": NT, "bank2": NT, "bank3": 1},
    "moe0_first": {"hidden": 2, "bank0": 1, "bank1": 1, "bank2": 1},
    "moe0": {"hidden": 2, "bank0": 1, "bank1": 1, "bank2": 1, "bank3": 1},
    "moe0_out": {"var": 1, "rstd": 1, "added": 1, "bank0": 1, "bank3": 1},
    "linear": {"negative": 1, "elu": 1, "features": 1, "kv": 1, "context": 1, "bank0": 2, "bank1": 2,
               "bank2": 1, "bank3": 1},
    "project": {"bank2": 1, "bank3": 1},
    "ret_in": {"table": 32, "rotated": 2, "k_decayed": 1, "q_parts": 1, "k_parts": 1, "gate": 1, "q_decayed": 1,
               "entering": 1, "bank0": 2, "bank1": 2, "bank2": 2, "bank3": 2},
    "stack": {"ones": 1, "parts_out": 64, "stacked": 16 * 4 * len(RUNS)},
    "ret_head_first": {"bank0": 1},
    "ret_head": {"retained": 1, "bank0": 1},
    "ret_out": {"var": 1, "rstd": 1, "context": 1, "bank2": 1},
    "attn_in": {"q_parts": 1, "k_parts": 1, "bank0": 1, "bank1": 1, "bank2": 1},
    "lat_in": {"table": 32, "rotated": 2, "activated": 2, "q_parts": 1, "k_parts": 1, "bank0": 2, "bank1": 2,
               "bank2": 1, "bank3": 1},
    "row_max": {"bank0": 1, "bank1": 1, "bank2": 1, "bank3": 1},
    "max_rows": {"max_parts": 1, "max_out": 16, "max_stacked": 32, "bank0": 1},
    "attend_first": {"multiplied": 2, "bank0": 2, "bank1": 2},
    "attend": {"multiplied": 4, "bank0": 2, "bank1": 2},
    "attend_gather": {"multiplied": 4, "gathered": 1, "bank0": 2, "bank1": 2},
    "attend_turn2": {"multiplied": 4, "bank0": 2, "bank1": 2, "bank2": 1},
    "attend_turn3": {"multiplied": 4, "bank0": 2, "bank1": 2, "bank3": 1},
    "attended": {"multiplied": 2, "gathered": 1, "context": 1, "bank3": 1},
    "moe1_in": {"var": 1, "rstd": 1, "normed": 1, "exped": 1, "above": 1, "exped_again": 1, "weighed": 1,
                "bank0": 1, "bank1": 1, "bank3": 1},
    "moe1_first": {"bank0": 2, "bank1": 2},
    "moe1": {"bank0": 2, "bank1": 2, "bank2": 1},
    "moe1_out": {"var": 1, "rstd": 1, "added": 1, "bank2": 1, "bank3": 1},
    "store": {"x_stored": 16},
}

LENGTH = {
    "load": 2, "norm": (2.5, 3), "mamba_in": (2.5, 4), "mamba_dir": (11, 9, 8), "scan_first": (1.5, 1.5), "scan": (1.5, 1.5), "mamba_out": (6, 3), "combine": (4, 4),
    "moe0_in": (19, 9, 6), "moe0_first": 4, "moe0": (2, 2), "moe0_out": (3.5, 7), "linear": (9, 4, 4), "project": (2, 3), "ret_in": (11, 6), "stack": (7, 7),
    "ret_head_first": 1.5, "ret_head": 1.5, "ret_out": (6, 13), "attn_in": 9, "lat_in": (6, 3, 6), "row_max": (1.2, 1.2), "max_rows": 6,
    "attend_first": (2.2, 2.2), "attend": (2.6, 2.6), "attend_gather": (2.2, 2.2), "attend_turn2": (2.5, 2.5), "attend_turn3": (2.5, 2.5), "attended": 5,
    "moe1_in": (6, 8, 1), "moe1_first": 4, "moe1": (3.5, 3.5), "moe1_out": (5, 8), "store": 2, "rest": 5,
}


def schedule():
    mamba = [("norm", 0), ("mamba_in", 0)]
    for d in range(2):
        mamba += [("mamba_dir", d)] + [("scan_first" if n < 2 else "scan", (d, n)) for n in range(NS)] + [("mamba_out", d)]
    mamba += [("combine", 0)]
    steps = [("load", 0)] + mamba
    experts0 = [("norm", 0), ("moe0_in", 0)]
    experts0 += [("moe0" if e else "moe0_first", e) for e in range(E)] + [("moe0_out", 0)]
    linear = [("norm", 0), ("linear", 0), ("project", ("lin_Wo", "lin_bo", 1.0, "X"))]
    retention = [("norm", 0), ("ret_in", 0), ("stack", 0)]
    retention += [("ret_head" if h else "ret_head_first", h) for h in range(H)]
    retention += [("ret_out", 0), ("project", ("ret_Wo", None, 0.5, "X"))]
    def attention(causal):
        part = [("stack", 0)] + [("row_max", (h, causal)) for h in range(H)] + [("max_rows", 0)]
        kinds = {0: "attend_first", 4: "attend_gather", 5: "attend_turn2", 8: "attend_gather", 9: "attend_turn3",
                 12: "attend_gather", 13: "attend_turn2"}
        part += [(kinds.get(h, "attend"), (h, causal)) for h in range(H)]
        return part + [("attended", causal)]

    experts1 = [("norm", 0), ("attn_in", 0)] + attention(False) + [("project", ("f_Wo", "f_bo", 1.0, "W"))]
    experts1 += [("moe1_in", 0)] + [("moe1" if e else "moe1_first", e) for e in range(E)] + [("moe1_out", 0)]
    latent = [("norm", 0), ("lat_in", 0)] + attention(True) + [("project", ("lat_wo", "lat_bo", 1.0, "X"))]
    steps += experts0
    steps += linear
    steps += experts0
    steps += retention
    rest = len(steps)
    steps += experts1
    steps += latent
    steps += experts1
    steps.insert(rest, ("rest", 0))
    return steps + [("store", 0)]


def interleave(steps, positions):
    timed = []
    for slot, own in enumerate(positions):
        at = 0.0
        for k, pos in enumerate(own):
            sections = LENGTH[steps[pos][0]]
            for n, length in enumerate(sections if type(sections) is tuple else (sections,)):
                timed.append((at, slot, k, pos, n))
                at += length
    return [(slot, pos, n) for _, slot, _, pos, n in sorted(timed)]


class Program:

    def __init__(self, nc, steps):
        self.nc, self.steps = nc, steps
        self.sems = {}
        self.raised = {}
        rest = [kind for kind, _ in steps].index("rest")
        whole, head, tail = list(range(len(steps))), list(range(rest + 1)), list(range(rest + 1, len(steps)))
        self.positions = {"enter": ([], head), "pair": (whole, tail + head), "last": (whole, tail)}
        self.order = {part: interleave(steps, both) for part, both in self.positions.items()}
        self.before = {}
        for part, both in self.positions.items():
            for slot, own in enumerate(both):
                seen = {}
                for pos in own:
                    self.before[part, slot, pos] = dict(seen)
                    for name, n in RAISES[steps[pos][0]].items():
                        seen[name] = seen.get(name, 0) + n
        self.names = sorted({name for kind, _ in steps for name in RAISES[kind]})

    def check(self):
        for part, slot, pos in self.before:
            kind, arg = self.steps[pos]
            for name, n in RAISES[kind].items():
                for key in (name, name + "_drained") if name[:4] == "bank" else (name,):
                    got = self.raised.get((part, slot, pos, key), 0)
                    assert got == n, (part, kind, arg, key, got, n)


class Cursor:

    def __init__(self, prog, eng, part, slot, pos, own):
        self.prog, self.eng, self.part, self.slot, self.pos, self.own = prog, eng, part, slot, pos, own
        self.base = prog.before[part, slot, pos] if part else {}

    def sem(self, name):
        return self.prog.sems[name, self.slot]

    def nth(self, name, k=1):
        return self.base.get(name, 0) + k

    def past(self, name, back=0):
        assert self.base.get(name, 0) >= back
        return self.base.get(name, 0) - back

    def raises(self, name, by=1):
        self.count(name, by)
        return self.sem(name)

    def count(self, name, by=1):
        key = (self.part, self.slot, self.pos, name)
        self.prog.raised[key] = self.prog.raised.get(key, 0) + by

    def filled(self, b):
        return self.prog.sems[f"filled{b}", self.slot]

    def drained(self, b):
        return self.prog.sems[f"drained{b}", self.slot]

    def fills(self, b):
        self.count(f"bank{b}")
        return self.filled(b)

    def drains(self, b):
        self.count(f"bank{b}_drained")
        return self.drained(b)

    def fill(self, b, j=0):
        return self.base.get(f"bank{b}", 0) + j + 1

    def fill_before(self, b, j=0):
        return self.fill(b, j) - 1

    def fill_past(self, b, back=0):
        assert self.base.get(f"bank{b}", 0) >= back
        return self.base.get(f"bank{b}", 0) - back

    def link(self, ins):
        self.own["n"] += 1
        ins.then_inc(self.own["sem"], 1)
        self.eng.wait_ge(self.own["sem"], self.own["n"])


def network(nc, x, wts, rows, consts, tables, out):
    steps = schedule()
    prog = Program(nc, steps)
    stack = ExitStack()
    with stack:
        def sb(name, shape, dt=FP32):
            return stack.enter_context(nc.sbuf_tensor(name, shape, dt))

        def dram(name, shape, dt):
            return nc.dram_tensor(name, shape, dt, kind="Internal").ap()

        Wt = sb("weights", [P, W_WIDTH])
        Rt = sb("rows", [P, R_WIDTH])
        Ct = sb("consts", [P, C_WIDTH])

        def w(name, lo=0, n=None):
            at, width = W_AT[name]
            return Wt[:, at + lo:at + (lo + n if n is not None else width)]

        def row(name):
            at, width = R_AT[name]
            return Rt[:, at:at + width]

        def const(name, lo=0, n=None):
            at, width = C_AT[name]
            return Ct[:, at + lo:at + (lo + n if n is not None else width)]

        identb = sb("identb", [P, P], BF16)
        zerob = sb("zerob", [1, P], BF16)
        maskb = sb("maskb", [P, 2, P], BF16)
        selb = sb("selb", [3 * 2 * NS, 2 * NS], BF16)
        sel8b = sb("sel8b", [3 * E, E], BF16)
        G = sb("G", [P, E, P])
        ce = sb("ce", [P, E])
        half_bin = sb("half_bin", [P, 8])
        half_bg = sb("half_bg", [P, 1])
        mhalf64 = sb("mhalf64", [P, NT * H])
        mhalf = mhalf64[:, 0:NT * E]
        ARENA = 11968
        X = [sb(f"X{s}", [P, NT, P]) for s in range(SLOTS)]
        W = [sb(f"W{s}", [P, NT, P]) for s in range(SLOTS)]
        WT = [sb(f"WT{s}", [P, T]) for s in range(SLOTS)]
        small = [sb(f"small{s}", [P, 128]) for s in range(SLOTS)]
        arena = [sb(f"arena{s}", [P, ARENA]) for s in range(SLOTS)]
        banks = [[stack.enter_context(nc.psum_tensor(f"bank{s}{b}", [P, T], FP32)) for b in range(4)]
                 for s in range(SLOTS)]

        def ar(s, at, n, dt=FP32):
            if dt is FP32:
                return arena[s][:, at:at + n]
            return arena[s][:, at:at + n // 2].bitcast(BF16)

        def sm(s, at, n):
            return small[s][:, at:at + n]

        stats = lambda s: sm(s, 0, 24).rearrange("p (t k) -> p t k", t=NT)
        moments = lambda s: sm(s, 24, 8).rearrange("p (t k) -> p t k", t=NT)
        var = lambda s: sm(s, 32, NT)
        rstd = lambda s: sm(s, 36, NT)

        def halves(ap):
            return ap.rearrange("p (h t) -> p h t", h=2)

        def over_tokens(ap):
            return ap.unsqueeze(1).to_broadcast([P, NT, ap.shape[1]])

        def bank(s, b):
            return banks[s][b]

        setup_sems = {n: stack.enter_context(nc.semaphore(n)) for n in
                      ("weights_loaded", "halved", "A_exp", "A_ready", "centred", "w1_turned", "w1T_ready",
                       "gram", "gram_ready", "consts_ready", "mhalf_ready", "sq_ready",
                       "vector_setup", "scalar_setup", "pool_setup", "tensor_setup")}
        barrier = {n: stack.enter_context(nc.semaphore(n)) for n in ("pair_done", "cleared", "left")}
        loop_sems = []
        for s in range(SLOTS):
            for name in prog.names:
                for full_name in ((f"filled{name[4:]}", f"drained{name[4:]}") if name[:4] == "bank" and name[4:].isdigit() else (name,)):
                    prog.sems[full_name, s] = stack.enter_context(nc.semaphore(f"{full_name}_{s}"))
                    loop_sems.append(prog.sems[full_name, s])
        chains = {n: {"sem": stack.enter_context(nc.semaphore(f"{n}_chain")), "n": 0}
                  for n in ("vector", "scalar", "gpsimd")}
        loop_sems += [c["sem"] for c in chains.values()]
        setup_chain = {"sem": setup_sems["vector_setup"], "n": 0}

        def run(eng, own, table, part):
            if own:
                own["n"] = 0
            started = {}
            for slot, pos, section in prog.order[part]:
                kind, arg = steps[pos]
                if kind in table and section == 0:
                    started[slot] = table[kind](Cursor(prog, eng, part, slot, pos, own), slot, arg)
                if kind in table and started[slot] is not None:
                    next(started[slot], None)

        def leave(eng, clears=False):
            if clears:
                eng.wait_ge(barrier["pair_done"], 4)
                for sem in loop_sems:
                    eng.sem_clear(sem)
                eng.sem_clear(barrier["pair_done"])
                eng.sem_inc(barrier["cleared"], 1)
                eng.wait_ge(barrier["left"], 4)
                eng.sem_clear(barrier["cleared"])
                eng.sem_clear(barrier["left"])
            else:
                eng.sem_inc(barrier["pair_done"], 1)
                eng.wait_ge(barrier["cleared"], 1)
                eng.sem_inc(barrier["left"], 1)

        v, a, g, pe = nc.vector, nc.scalar, nc.gpsimd, nc.tensor
        I = const("ident")

        def norm_stats(c, s, src, eps):
            for t in range(NT):
                last = v.bn_stats(stats(s)[:, t, :], src[:, t, :])
            c.link(last)
            for t in range(NT):
                last = v.bn_aggr(moments(s)[:, t, :], stats(s)[:, t, :])
            c.link(last)
            v.tensor_scalar(var(s), moments(s)[:, :, 1], eps, None, ALU.add).then_inc(c.raises("var"), 1)

        def norm_apply(c, s, src, dst):
            v.wait_ge(c.sem("rstd"), c.nth("rstd"))
            for t in range(NT):
                last = v.tensor_scalar(dst[:, t, :], src[:, t, :], moments(s)[:, t, 0:1], rstd(s)[:, t:t + 1],
                                       ALU.subtract, ALU.mult)
            return last

        def norm_vector(c, s, src, dst, eps):
            norm_stats(c, s, src, eps)
            return norm_apply(c, s, src, dst)

        def norm_pool(c, s):
            g.wait_ge(c.sem("var"), c.nth("var"))
            g.tensor_tensor(rstd(s), var(s), mhalf[:, 0:NT], ALU.pow).then_inc(c.raises("rstd"), 1)

        def turn(c, s, src, b, last_j=0, identity=None, reverse=False):
            for t in range(NT):
                at = (NT - 1 - t if reverse else t) * P
                last = pe.matmul(bank(s, b)[:, at:at + P], src[:, t, :], identity, is_transpose=True,
                                 start=True, stop=True)
            last.then_inc(c.fills(b), 1)

        def residual_ready(c):
            kind = steps[c.pos - 1][0]
            if kind == "rest":
                if c.slot:
                    return
                kind = steps[c.pos - 2][0]
            if kind == "load":
                c.eng.wait_ge(c.sem("x_loaded"), c.past("x_loaded"))
            elif kind in ("moe0_out", "moe1_out"):
                c.eng.wait_ge(c.sem("added"), c.past("added"))
            else:
                c.eng.wait_ge(c.drained({"combine": 2, "project": 3}[kind]), c.fill_past({"combine": 2, "project": 3}[kind]))

        def norm_v(c, s, arg):
            residual_ready(c)
            norm_stats(c, s, X[s], 1e-5)
            yield
            norm_apply(c, s, X[s], W[s]).then_inc(c.raises("normed"), 1)

        def norm_p(c, s, arg):
            norm_pool(c, s)

        def norm_t(c, s, arg):
            yield
            pe.wait_ge(c.sem("normed"), c.nth("normed"))
            pe.wait_ge(c.drained(0), c.fill_before(0))
            turn(c, s, W[s], 0, identity=I)

        def norm_s(c, s, arg):
            yield
            a.wait_ge(c.filled(0), c.fill(0))
            a.copy(WT[s][:, :], bank(s, 0)[:, :]).then_inc(c.drains(0), 1)


        XL, XC, SZ, DELTA, DX, BCP, BCT, BCR, RING = 0, 1024, 2048, 3072, 4096, 5120, 5376, 5568, 5824
        U2 = RING
        XPAD, ACC, THC, ZH, THZ, DTT = RING, RING + 1032, RING + 2056, RING + 3080, RING + 4104, RING + 5176
        XB, EA, W1P, LW = RING, RING + 1024, RING + 2048, RING + 3072
        DA = lambda s, n: halves(ar(s, RING + 1024 * (n % 2), 1024))
        BX = lambda s, n: halves(ar(s, RING + 2048 + 1024 * (n % 3), 1024))
        CB = lambda s, n: ar(s, RING + 5120 + 512 * (n % 2), 512)
        LAG = 2
        u2 = lambda s: ar(s, U2, T).rearrange("p (t d) -> p t d", t=NT)
        xl = lambda s, d: ar(s, XL + T * d, T)
        f = xl
        xpad = lambda s: ar(s, XPAD, 2 * 516).rearrange("p (h t) -> p h t", h=2)
        bct = lambda s: ar(s, BCT, NT * 3 * 32, BF16).rearrange("p (t k n) -> p t k n", t=NT, k=3)
        bcp = lambda s: ar(s, BCP, T, BF16)[0:96, :]

        def split3(c, src, parts, rest, drain=None):
            c.link(v.tensor_copy(parts[0], src))
            ins = v.tensor_tensor(rest, src, parts[0], ALU.subtract)
            if drain is None:
                c.link(ins)
            else:
                ins.then_inc(c.drains(drain[0]), 1)
                v.wait_ge(c.drained(drain[0]), c.fill(drain[0], drain[1]))
            c.link(v.tensor_copy(parts[1], rest))
            c.link(v.tensor_tensor(rest, rest, parts[1], ALU.subtract))
            return v.tensor_copy(parts[2], rest)

        def mamba_in_v(c, s, arg):
            v.wait_ge(c.sem("normed"), c.past("normed"))
            norm_stats(c, s, W[s], 1e-5)
            yield
            norm_apply(c, s, W[s], u2(s)).then_inc(c.raises("normed"), 1)

        def mamba_in_p(c, s, arg):
            norm_pool(c, s)

        def mamba_in_t(c, s, arg):
            yield
            pe.wait_ge(c.sem("normed"), c.nth("normed"))
            pe.wait_ge(c.drained(0), c.fill_before(0))
            turn(c, s, u2(s), 0, identity=I)
            pe.wait_ge(c.drained(1), c.fill_before(1))
            turn(c, s, u2(s), 1, identity=const("anti"), reverse=True)

        def mamba_in_s(c, s, arg):
            yield
            for d in range(2):
                a.wait_ge(c.filled(d), c.fill(d))
                a.activation(xl(s, d), bank(s, d)[:, :], ACT.Identity, bias=w("ln_b", d, 1),
                                     scale=w("ln_w", d, 1)).then_inc(c.drains(d), 1)

        def mamba_dir_t(c, s, d):
            pe.wait_ge(c.drained(0), c.fill_past(0))
            pe.wait_ge(c.drained(1), c.fill_past(1))
            for j in range(4):
                pe.wait_ge(c.drained(j), c.fill_before(j))
                pe.matmul(bank(s, j)[:, :], w("W_in", (d * 4 + j) * P, P), xl(s, d), start=True, stop=True).then_inc(c.fills(j), 1)
            yield
            pe.wait_ge(c.sem("conv_out"), c.nth("conv_out"))
            pe.wait_ge(c.drained(0), c.fill_before(0, 1))
            for h in range(2):
                last = pe.matmul(bank(s, 0)[0:RK, :], w("W_x", (d * 2 + h) * 96, RK), ar(s, XC + h * T, T),
                                 start=h == 0, stop=h == 1)
            last.then_inc(c.fills(0), 1)
            pe.wait_ge(c.drained(1), c.fill_before(1, 1))
            for t in range(NT):
                for h in range(2):
                    last = pe.matmul(bank(s, 1)[:, t * 32:(t + 1) * 32], ar(s, XC + h * T + t * P, P),
                                     w("W_x", (d * 2 + h) * 96 + RK, 32), start=h == 0, stop=h == 1)
            last.then_inc(c.fills(1), 1)
            pe.wait_ge(c.drained(0), c.fill(0, 1))
            for h in range(2):
                pe.wait_ge(c.drained(2 + h), c.fill_before(2 + h, 1))
                pe.matmul(bank(s, 2 + h)[:, :], w("W_dt", d * DI + h * P, P)[0:RK, :],
                                   ar(s, DTT, T)[0:RK, :], start=True, stop=True).then_inc(c.fills(2 + h), 1)
            yield
            pe.wait_ge(c.sem("bc_parts"), c.nth("bc_parts"))
            pe.wait_ge(c.drained(1), c.fill_before(1, 2))
            for t in range(NT):
                last = pe.matmul(bank(s, 1)[0:96, t * P // 2:(t + 1) * P // 2].bitcast(BF16),
                                 bct(s)[:, t, :, :].rearrange("p k n -> p (k n)"), identb[:, :],
                                 is_transpose=True, start=True, stop=True)
            last.then_inc(c.fills(1), 1)

        def mamba_dir_s(c, s, d):
            if d:
                a.wait_ge(c.sem("gated"), c.past("gated"))
            for h in range(2):
                a.wait_ge(c.filled(h), c.fill(h))
                a.activation(xpad(s)[:, h, TAPS - 1:PADW], bank(s, h)[:, :], ACT.Identity,
                                     bias=w("b_in", d * 4 + h, 1)).then_inc(c.drains(h), 1)
            for h in range(2):
                a.wait_ge(c.filled(2 + h), c.fill(2 + h))
                a.activation(ar(s, ZH + h * T, T), bank(s, 2 + h)[:, :], ACT.Identity,
                                     bias=half_bin[:, d * 4 + 2 + h:d * 4 + 3 + h], scale=0.5).then_inc(c.drains(2 + h), 1)
            a.wait_ge(c.drained(3), c.fill(3))
            a.activation(ar(s, THZ, 1024), ar(s, ZH, 1024), ACT.Tanh).then_inc(c.raises("gate_tanh"), 1)
            yield
            a.wait_ge(c.sem("conv"), c.nth("conv"))
            a.activation(ar(s, THC, 1024), ar(s, ACC, 1024), ACT.Tanh).then_inc(c.raises("conv_tanh"), 1)
            a.wait_ge(c.filled(0), c.fill(0, 1))
            a.copy(ar(s, DTT, T)[0:RK, :], bank(s, 0)[0:RK, :]).then_inc(c.drains(0), 1)
            for h in range(2):
                a.wait_ge(c.filled(2 + h), c.fill(2 + h, 1))
                a.activation(ar(s, XB + h * T, T), bank(s, 2 + h)[:, :], ACT.Identity,
                                     bias=w("b_dt", d * 2 + h, 1)).then_inc(c.drains(2 + h), 1)
            a.wait_ge(c.drained(3), c.fill(3, 1))
            a.activation(ar(s, EA, 1024), ar(s, XB, 1024), ACT.Abs).then_inc(c.raises("minus_abs"), 1)
            yield
            a.wait_ge(c.sem("minus_abs"), c.nth("minus_abs"))
            a.activation(ar(s, EA, 1024), ar(s, EA, 1024), ACT.Exp, scale=-1.0).then_inc(c.raises("exp_abs"), 1)
            a.wait_ge(c.filled(1), c.fill(1, 2))
            a.copy(bcp(s), bank(s, 1)[0:96, 0:T // 2].bitcast(BF16)).then_inc(c.drains(1), 1)
            a.wait_ge(c.sem("one_plus"), c.nth("one_plus"))
            a.activation(ar(s, LW, 1024), ar(s, W1P, 1024), ACT.Ln).then_inc(c.raises("log"), 1)

        def mamba_dir_v(c, s, d):
            if d:
                v.wait_ge(c.sem("gated"), c.past("gated"))
            v.wait_ge(c.drained(1), c.fill(1))
            c.link(v.memset(xpad(s)[:, :, 0:TAPS - 1], 0.0))
            for k in range(TAPS):
                for h in range(2):
                    tap = w("conv_w", (d * 2 + h) * TAPS + k, 1)
                    acc = ar(s, ACC + h * T, T)
                    src = xpad(s)[:, h, k:k + T]
                    if k == 0:
                        ins = v.tensor_scalar(acc, src, tap, w("conv_b", d * 2 + h, 1), ALU.mult, ALU.add)
                    else:
                        ins = v.scalar_tensor_tensor(acc, src, tap, acc, ALU.mult, ALU.add)
                if k < TAPS - 1:
                    c.link(ins)
            ins.then_inc(c.raises("conv"), 1)
            yield
            v.wait_ge(c.drained(3), c.fill(3))
            v.wait_ge(c.sem("gate_tanh"), c.nth("gate_tanh"))
            v.scalar_tensor_tensor(ar(s, SZ, 1024), ar(s, THZ, 1024), 1.0, ar(s, ZH, 1024), ALU.add, ALU.mult)
            v.wait_ge(c.sem("conv_tanh"), c.nth("conv_tanh"))
            v.scalar_tensor_tensor(ar(s, XC, 1024), ar(s, THC, 1024), 1.0, ar(s, ACC, 1024),
                                          ALU.add, ALU.mult).then_inc(c.raises("conv_out"), 1)
            v.wait_ge(c.filled(1), c.fill(1, 1))
            src = bank(s, 1)[:, 0:NT * 32].rearrange("p (t n) -> p t n", t=NT)
            split3(c, src, [bct(s)[:, :, k, :] for k in range(3)],
                          ar(s, BCR, 128).rearrange("p (t n) -> p t n", t=NT), (1, 1)).then_inc(c.raises("bc_parts"), 1)
            yield
            e, w1p, lw, delta = (ar(s, k, 1024) for k in (EA, W1P, LW, DELTA))
            v.wait_ge(c.sem("exp_abs"), c.nth("exp_abs"))
            v.tensor_scalar(w1p, e, 1.0, None, ALU.add).then_inc(c.raises("one_plus"), 1)
            v.wait_ge(c.sem("one_plus"), c.nth("one_plus"))
            c.link(v.scalar_tensor_tensor(e, w1p, 1.0, e, ALU.subtract, ALU.subtract))
            v.wait_ge(c.sem("log"), c.nth("log"))
            c.link(v.scalar_tensor_tensor(delta, ar(s, XB, 1024), 0.0, lw, ALU.max, ALU.add))
            c.link(v.tensor_tensor(delta, delta, e, ALU.subtract))
            for n in range(2):
                v.memset(DA(s, n)[:, :, 0:1], 0.0)
            v.tensor_tensor(ar(s, DX, 1024), delta, ar(s, XC, 1024), ALU.mult).then_inc(c.raises("delta"), 1)

        def scan_t(c, s, arg):
            d, n = arg
            if n == 0:
                pe.wait_ge(c.drained(1), c.fill_past(1))
            for k in range(2):
                pe.wait_ge(c.drained(k), c.fill_before(k))
                pe.matmul(bank(s, k)[:, :], selb[0:96, k * NS + n:k * NS + n + 1].to_broadcast([96, P]),
                                   bcp(s), start=True, stop=True).then_inc(c.fills(k), 1)
            yield
            if n >= LAG:
                sum_states(c, s, n - LAG, LAG)

        def sum_states(c, s, n, back):
            pe.wait_ge(c.sem("state_c"), c.past("state_c", back - 1))
            for h in range(2):
                if n == 0:
                    pe.wait_ge(c.drained(2 + h), c.fill_before(2 + h))
                last = pe.matmul(bank(s, 2 + h)[:, :], I, BX(s, n)[:, h, :], start=n == 0, stop=n == NS - 1)
                if n == NS - 1:
                    last.then_inc(c.fills(2 + h), 1)
            if n < NS - 1:
                last.then_inc(c.raises("summed"), 1)

        def scan_s(c, s, arg):
            d, n = arg
            if n == 0:
                a.wait_ge(c.sem("delta"), c.past("delta"))
            if n >= 2:
                a.wait_ge(c.sem("state"), c.past("state", 1))
            for h in range(2):
                last = a.activation(DA(s, n)[:, h, 1:T], ar(s, DELTA + h * T + 1, T - 1), ACT.Exp,
                                    scale=w("A", (d * 2 + h) * NS + n, 1))
            last.then_inc(c.raises("decay_ready"), 1)
            a.wait_ge(c.filled(1), c.fill(1))
            if n >= 2:
                a.wait_ge(c.sem("state_c"), c.past("state_c", 1))
            a.copy(CB(s, n), bank(s, 1)[:, :]).then_inc(c.drains(1), 1)

        def scan_v(c, s, arg):
            d, n = arg
            if n == 0:
                v.wait_ge(c.sem("delta"), c.past("delta"))
            v.wait_ge(c.filled(0), c.fill(0))
            if n >= 3:
                v.wait_ge(c.sem("summed"), c.past("summed", 0))
            v.tensor_tensor(BX(s, n), halves(ar(s, DX, 1024)),
                                    bank(s, 0)[:, :].unsqueeze(1).to_broadcast([P, 2, T]), ALU.mult).then_inc(c.drains(0), 1)
            v.wait_ge(c.drained(0), c.fill(0))
            v.wait_ge(c.sem("decay_ready"), c.nth("decay_ready"))
            flat = ar(s, RING + 2048 + 1024 * (n % 3), 1024)
            v.tensor_tensor_scan(flat, ar(s, RING + 1024 * (n % 2), 1024), flat, 0.0, ALU.mult, ALU.add).then_inc(c.raises("state"), 1)

        def scan_p(c, s, arg):
            d, n = arg
            g.wait_ge(c.sem("state"), c.nth("state"))
            g.wait_ge(c.drained(1), c.fill(1))
            g.tensor_tensor(BX(s, n), BX(s, n), CB(s, n).unsqueeze(1).to_broadcast([P, 2, T]), ALU.mult).then_inc(c.raises("state_c"), 1)

        def mamba_out_t(c, s, d):
            sum_states(c, s, NS - 2, 2)
            sum_states(c, s, NS - 1, 1)
            yield
            pe.wait_ge(c.sem("gated"), c.nth("gated"))
            pe.wait_ge(c.drained(0), c.fill_before(0))
            for h in range(2):
                last = pe.matmul(bank(s, 0)[:, :], w("W_out", (d * 2 + h) * P, P), ar(s, DELTA + h * T, T),
                                 start=h == 0, stop=h == 1)
            last.then_inc(c.fills(0), 1)

        def mamba_out_v(c, s, d):
            y = ar(s, DELTA, 1024)
            for h in range(2):
                v.wait_ge(c.filled(2 + h), c.fill(2 + h))
                v.scalar_tensor_tensor(ar(s, DELTA + h * T, T), ar(s, XC + h * T, T), w("D", d * 2 + h, 1),
                                               bank(s, 2 + h)[:, :], ALU.mult, ALU.add).then_inc(c.drains(2 + h), 1)
            v.wait_ge(c.drained(3), c.fill(3))
            v.tensor_tensor(y, y, ar(s, SZ, 1024), ALU.mult).then_inc(c.raises("gated"), 1)
            yield
            v.wait_ge(c.filled(0), c.fill(0))
            src = bank(s, 0)[:, :] if d == 0 else bank(s, 0)[:, T - 1::-1]
            v.scalar_tensor_tensor(f(s, d), src, w("b_out", d, 1), WT[s][:, :], ALU.add, ALU.add).then_inc(c.drains(0), 1)

        def combine_t(c, s, arg):
            pe.wait_ge(c.drained(0), c.fill_past(0))
            for b, name in ((0, "Wg"), (1, "Wv")):
                pe.wait_ge(c.drained(b), c.fill_before(b))
                for d in range(2):
                    last = pe.matmul(bank(s, b)[:, :], w(name, d * P, P), f(s, d), start=d == 0, stop=d == 1)
                last.then_inc(c.fills(b), 1)
            yield
            pe.wait_ge(c.sem("mixed"), c.nth("mixed"))
            pe.wait_ge(c.drained(2), c.fill_before(2))
            for t in range(NT):
                last = pe.matmul(bank(s, 2)[:, t * P:(t + 1) * P], ar(s, ACC + t * P, P), I, is_transpose=True,
                                 start=True, stop=True)
            last.then_inc(c.fills(2), 1)

        def combine_s(c, s, arg):
            a.wait_ge(c.filled(0), c.fill(0))
            a.activation(ar(s, XPAD, T), bank(s, 0)[:, :], ACT.Tanh, bias=half_bg[:, 0:1], scale=0.5).then_inc(c.drains(0), 1)

        def combine_v(c, s, arg):
            v.wait_ge(c.drained(0), c.fill_past(0))
            both, diff, o = ar(s, THC, T), ar(s, ZH, T), ar(s, ACC, T)
            c.link(v.tensor_tensor(both, f(s, 0), f(s, 1), ALU.add))
            v.wait_ge(c.filled(1), c.fill(1))
            v.scalar_tensor_tensor(diff, bank(s, 1)[:, :], w("bv"), both, ALU.add, ALU.subtract).then_inc(c.drains(1), 1)
            v.wait_ge(c.drained(1), c.fill(1))
            v.wait_ge(c.drained(0), c.fill(0))
            c.link(v.scalar_tensor_tensor(diff, ar(s, XPAD, T), 1.0, diff, ALU.add, ALU.mult))
            v.scalar_tensor_tensor(o, diff, 0.5, both, ALU.mult, ALU.add).then_inc(c.raises("mixed"), 1)
            yield
            v.wait_ge(c.filled(2), c.fill(2))
            x4 = X[s][:, :, :].rearrange("p t d -> p (t d)")
            v.scalar_tensor_tensor(x4, bank(s, 2)[:, :], 0.5, x4, ALU.mult, ALU.add).then_inc(c.drains(2), 1)

        RT = 9800
        probs = lambda s: ar(s, RT, NT * E).rearrange("p (t e) -> p t e", t=NT)
        weight = lambda s: ar(s, RT + 32, NT * E).rearrange("p (t e) -> p t e", t=NT)
        chosen = lambda s: ar(s, RT + 64, NT * E).rearrange("p (t e) -> p t e", t=NT)
        top = lambda s: ar(s, RT + 96, NT)
        whole = lambda s: ar(s, RT + 100, NT)
        rvar = lambda s: ar(s, RT + 104, NT * E)
        rroot = lambda s: ar(s, RT + 136, NT * E).rearrange("p (t e) -> p t e", t=NT)
        pairs = lambda s, k: ar(s, RT + 168 + 256 * k, NT * E * E).rearrange("p (t e j) -> p t e j", t=NT, e=E)
        rparts = lambda s: ar(s, RT + 680, NT * 3 * E, BF16).rearrange("p (t k e) -> p t k e", t=NT, k=3)
        weightT = lambda s: ar(s, RT + 728, T)[0:E, :]
        rrest = lambda s: ar(s, RT + 1240, NT * E).rearrange("p (t e) -> p t e", t=NT)

        def per_expert(ap):
            return ap.unsqueeze(2).to_broadcast([P, NT, E])

        def router_v(c, s, logits, b, j, again):
            p, wt, sel = probs(s), weight(s), chosen(s)
            c.link(v.tensor_reduce(top(s), logits, AXX, ALU.max))
            v.tensor_tensor(p, logits, per_expert(top(s)), ALU.subtract).then_inc(c.drains(b), 1)
            v.wait_ge(c.sem("exped"), c.nth("exped"))
            c.link(v.tensor_reduce(whole(s), p, AXX, ALU.add))
            c.link(v.reciprocal(whole(s), whole(s)))
            c.link(v.tensor_tensor(p, p, per_expert(whole(s)), ALU.mult))
            mine = p.unsqueeze(3).to_broadcast([P, NT, E, E])
            other = p.unsqueeze(2).to_broadcast([P, NT, E, E])
            v.tensor_tensor(pairs(s, 0), other, mine, ALU.is_gt)
            c.link(v.tensor_tensor(pairs(s, 1), other, mine, ALU.is_equal))
            flat0, flat1 = (pairs(s, k).rearrange("p t e j -> p t (e j)") for k in range(2))
            c.link(v.tensor_tensor(flat1, flat1, over_tokens(const("earlier")), ALU.mult))
            c.link(v.tensor_tensor(flat0, flat0, flat1, ALU.add))
            c.link(v.tensor_reduce(sel, pairs(s, 0), AXX, ALU.add))
            c.link(v.tensor_scalar(sel, sel, 1.5, None, ALU.is_lt))
            if again:
                c.link(v.tensor_reduce(top(s), p, AXX, ALU.max))
                v.tensor_tensor(wt, p, per_expert(top(s)), ALU.subtract).then_inc(c.raises("above"), 1)
                v.wait_ge(c.sem("exped_again"), c.nth("exped_again"))
                c.link(v.tensor_tensor(wt, wt, sel, ALU.mult))
            else:
                c.link(v.tensor_tensor(wt, p, sel, ALU.mult))
            c.link(v.tensor_reduce(whole(s), wt, AXX, ALU.add))
            c.link(v.reciprocal(whole(s), whole(s)))
            v.tensor_tensor(wt, wt, per_expert(whole(s)), ALU.mult).then_inc(c.raises("weighed"), 1)

        def router_s(c, s, b, j, again):
            a.wait_ge(c.drained(b), c.fill(b, j))
            a.activation(probs(s), probs(s), ACT.Exp).then_inc(c.raises("exped"), 1)
            if again:
                a.wait_ge(c.sem("above"), c.nth("above"))
                a.activation(weight(s), weight(s), ACT.Exp).then_inc(c.raises("exped_again"), 1)

        def turn_weights(c, s, b, j):
            pe.wait_ge(c.sem("weighed"), c.nth("weighed"))
            pe.wait_ge(c.drained(b), c.fill_before(b, j))
            for t in range(NT):
                last = pe.matmul(bank(s, b)[0:E, t * P:(t + 1) * P], weight(s)[:, t, :], I, is_transpose=True,
                                 start=True, stop=True)
            last.then_inc(c.fills(b), 1)

        Z0, H0B, RB, ACC0, PROD = 0, 1024, 3072, 4096, 4608
        z0 = lambda s, j: ar(s, Z0 + T * j, T)
        h0 = lambda s, e, j: ar(s, H0B + 1024 * (e % 2) + T * j, T)
        rb = lambda s, e: ar(s, RB + T * (e % 2), T)
        acc0 = lambda s: ar(s, ACC0, T).rearrange("p (t d) -> p t d", t=NT)
        rT = lambda s: ar(s, PROD + 512, T, BF16)[0:3 * E, :]
        quad = lambda s: rrest(s)

        def moe0_in_t(c, s, arg):
            pe.wait_ge(c.drained(0), c.fill_past(0))
            pe.wait_ge(c.drained(0), c.fill_before(0))
            for t in range(NT):
                last = pe.matmul(bank(s, 0)[:, t * 16:(t + 1) * 16], WT[s][:, t * P:(t + 1) * P],
                                 Wt[:, W_AT["gate_w"][0]:W_AT["gate_w"][0] + 16], start=True, stop=True)
            last.then_inc(c.fills(0), 1)
            for t in range(NT):
                for k in range(2):
                    pe.wait_ge(c.drained(1 + k), c.fill_before(1 + k, t))
                    pe.matmul(bank(s, 1 + k)[:, :], WT[s][:, t * P:(t + 1) * P], G[:, 4 * k:4 * k + 4, :],
                                       start=True, stop=True).then_inc(c.fills(1 + k), 1)
            yield
            turn_weights(c, s, 3, 0)
            yield
            pe.wait_ge(c.sem("root_parts"), c.nth("root_parts"))
            pe.wait_ge(c.drained(0), c.fill_before(0, 1))
            for t in range(NT):
                last = pe.matmul(bank(s, 0)[0:3 * E, t * P // 2:(t + 1) * P // 2].bitcast(BF16),
                                 rparts(s)[:, t, :, :].rearrange("p k n -> p (k n)"), identb[:, :],
                                 is_transpose=True, start=True, stop=True)
            last.then_inc(c.fills(0), 1)

        def moe0_in_v(c, s, arg):
            prod = lambda k: ar(s, PROD, T).rearrange("p (e d) -> p e d", e=4)
            v.wait_ge(c.filled(0), c.fill(0))
            lg = bank(s, 0)[:, 0:64].rearrange("p (t k) -> p t k", t=NT)
            c.link(v.tensor_copy(rroot(s), lg[:, :, E:2 * E]))
            router_v(c, s, lg[:, :, 0:E], 0, 0, False)
            for t in range(NT):
                for k in range(2):
                    v.wait_ge(c.filled(1 + k), c.fill(1 + k, t))
                    v.tensor_tensor(prod(k), bank(s, 1 + k)[:, :].rearrange("p (e d) -> p e d", e=4),
                                            W[s][:, t, :].unsqueeze(1).to_broadcast([P, 4, P]), ALU.mult).then_inc(c.drains(1 + k), 1)
                    v.wait_ge(c.drained(1 + k), c.fill(1 + k, t))
                    c.link(v.tensor_reduce(quad(s)[:, t, 4 * k:4 * k + 4], prod(k), AXX, ALU.add))
            yield
            c.link(v.tensor_tensor(quad(s), quad(s), rroot(s), ALU.add))
            v.tensor_tensor(rvar(s).rearrange("p (t e) -> p t e", t=NT), quad(s), over_tokens(ce[:, :]), ALU.add).then_inc(c.raises("expert_var"), 1)
            yield
            v.wait_ge(c.sem("expert_root"), c.nth("expert_root"))
            split3(c, rroot(s), [rparts(s)[:, :, k, :] for k in range(3)], rrest(s)).then_inc(c.raises("root_parts"), 1)

        def moe0_in_p(c, s, arg):
            yield
            g.wait_ge(c.sem("expert_var"), c.nth("expert_var"))
            g.tensor_tensor(rroot(s).rearrange("p t e -> p (t e)"), rvar(s), mhalf[:, :], ALU.pow).then_inc(c.raises("expert_root"), 1)

        def moe0_in_s(c, s, arg):
            router_s(c, s, 0, 0, False)
            yield
            a.wait_ge(c.filled(3), c.fill(3))
            a.copy(weightT(s), bank(s, 3)[0:E, :]).then_inc(c.drains(3), 1)
            yield
            a.wait_ge(c.filled(0), c.fill(0, 1))
            a.copy(rT(s), bank(s, 0)[0:3 * E, 0:T // 2].bitcast(BF16)).then_inc(c.drains(0), 1)

        def moe0_t(c, s, e):
            if e == 0:
                pe.wait_ge(c.drained(0), c.fill_past(0))
            pe.wait_ge(c.drained(0), c.fill_before(0))
            pe.matmul(bank(s, 0)[:, :], sel8b[0:3 * E, e:e + 1].to_broadcast([3 * E, P]), rT(s),
                               start=True, stop=True).then_inc(c.fills(0), 1)
            for j in range(2):
                pe.wait_ge(c.drained(1 + j), c.fill_before(1 + j))
                pe.matmul(bank(s, 1 + j)[:, :], w("w1", e * H0 + j * P, P), WT[s][:, :], start=True, stop=True).then_inc(c.fills(1 + j), 1)
            if e:
                yield
                moe0_second(c, s, e - 1, 2, 0)

        def moe0_second(c, s, e, back, j0):
            pe.wait_ge(c.sem("hidden"), c.past("hidden", back - 2))
            pe.wait_ge(c.drained(3), c.fill_before(3, j0))
            for t in range(NT):
                for j in range(2):
                    last = pe.matmul(bank(s, 3)[:, t * P:(t + 1) * P], h0(s, e, j)[:, t * P:(t + 1) * P],
                                     w("w2", (e * 2 + j) * P, P), start=j == 0, stop=j == 1)
            last.then_inc(c.fills(3), 1)

        def moe0_s(c, s, e):
            a.wait_ge(c.filled(0), c.fill(0))
            if e >= 2:
                a.wait_ge(c.drained(2), c.fill_past(2, 1))
            a.copy(rb(s, e), bank(s, 0)[:, :]).then_inc(c.drains(0), 1)
            if e >= 2:
                a.wait_ge(c.drained(3), c.fill_past(3))
            for j in range(2):
                a.wait_ge(c.drained(1 + j), c.fill(1 + j))
                a.activation(h0(s, e, j), z0(s, j), ACT.Gelu, bias=w("be_ln1", e * 2 + j, 1),
                                    scale=w("g1", e * 2 + j, 1)).then_inc(c.raises("hidden"), 1)

        def moe0_v(c, s, e):
            v.wait_ge(c.drained(0), c.fill(0))
            if e:
                v.wait_ge(c.sem("hidden"), c.past("hidden"))
            for j in range(2):
                v.wait_ge(c.filled(1 + j), c.fill(1 + j))
                v.scalar_tensor_tensor(z0(s, j), bank(s, 1 + j)[:, :], w("b1", e * 2 + j, 1), rb(s, e),
                                               ALU.add, ALU.mult).then_inc(c.drains(1 + j), 1)
            if e:
                yield
                moe0_add(c, s, e - 1, 0)

        def moe0_add(c, s, e, j0):
            v.wait_ge(c.filled(3), c.fill(3, j0))
            if e:
                v.wait_ge(c.drained(3), c.fill_past(3))
            for t in range(NT):
                last = v.scalar_tensor_tensor(acc0(s)[:, t, :], bank(s, 3)[:, t * P:(t + 1) * P], weight(s)[:, t, e:e + 1],
                                              W[s][:, t, :] if e == 0 else acc0(s)[:, t, :], ALU.mult, ALU.add)
            last.then_inc(c.drains(3), 1)

        def moe0_out_t(c, s, arg):
            moe0_second(c, s, E - 1, 2, 0)
            pe.wait_ge(c.drained(0), c.fill_before(0))
            for t in range(NT):
                last = pe.matmul(bank(s, 0)[:, t * P:(t + 1) * P], weightT(s)[:, t * P:(t + 1) * P], w("b2")[0:E, :],
                                 start=True, stop=True)
            last.then_inc(c.fills(0), 1)

        def flat(ap):
            return ap.rearrange("p t d -> p (t d)")

        def finish_norm_v(c, s, acc, o, eps, gain, offset):
            c.link(norm_vector(c, s, acc, o, eps))
            c.link(v.tensor_tensor(o, o, over_tokens(gain), ALU.mult))
            v_ins = v.tensor_tensor(o, o, over_tokens(offset), ALU.add)
            c.link(v_ins)
            v.tensor_tensor(X[s][:, :, :], X[s][:, :, :], o, ALU.add).then_inc(c.raises("added"), 1)

        def moe0_out_v(c, s, arg):
            moe0_add(c, s, E - 1, 0)
            v.wait_ge(c.drained(3), c.fill(3))
            v.wait_ge(c.filled(0), c.fill(0))
            v.tensor_tensor(flat(acc0(s)), flat(acc0(s)), bank(s, 0)[:, :], ALU.add).then_inc(c.drains(0), 1)
            v.wait_ge(c.drained(0), c.fill(0))
            yield
            finish_norm_v(c, s, acc0(s), ar(s, PROD, T).rearrange("p (t d) -> p t d", t=NT), 1e-5, row("ln_g"), row("ln_be"))

        def moe0_out_p(c, s, arg):
            yield
            norm_pool(c, s)

        QS, KS, QF, KF, QP, KP, VA = 0, 2048, 4096, 4608, 5120, 5888, 6656
        PROBS, NM, NMP, NMR, MT, CN, CT, TMP, TMP2, REC = 7232, 9280, 9344, 9440, 9504, 9760, 10272, 10784, 11296, 11808
        stacks = lambda s, at: ar(s, at, HP * T, BF16).rearrange("p (a t) -> p a t", a=HP)
        three = lambda s, at: ar(s, at, 3 * T, BF16).rearrange("p (k t) -> p k t", k=3)
        vaug = lambda s: ar(s, VA, NT * H * (HD + 1)).rearrange("p (t h d) -> p t h d", t=NT, h=H)
        prob = lambda s, kt: ar(s, PROBS + T * kt, T)
        minus_max = lambda s: ar(s, NM, NT * H).rearrange("p (t h) -> p t h", t=NT)
        max_parts = lambda s: ar(s, NMP, NT * 3 * H, BF16).rearrange("p (t k h) -> p t k h", t=NT, k=3)
        maxT = lambda s: ar(s, MT, T, BF16)[0:3 * H, :]
        context = lambda s: ar(s, CN, T).rearrange("p (t d) -> p t d", t=NT)
        parts_dram = [[dram(f"parts{s}{k}", [2, 3, P // 2, T], BF16) for k in range(2)] for s in range(SLOTS)]
        max_dram = [dram(f"maxima{s}", [3 * H, T], BF16) for s in range(SLOTS)]
        ONES_WORD = float(np.array([0x3F803F80], dtype=np.uint32).view(np.float32)[0])

        def head_rows(h, n):
            return slice(64 * (h % 2), 64 * (h % 2) + n)

        def project_t(c, s, arg):
            pe.wait_ge(c.sem("context"), c.past("context"))
            pe.wait_ge(c.drained(2), c.fill_before(2))
            for t in range(NT):
                last = pe.matmul(bank(s, 2)[:, t * P:(t + 1) * P], context(s)[:, t, :], I, is_transpose=True, start=True, stop=True)
            last.then_inc(c.fills(2), 1)
            yield
            pe.wait_ge(c.drained(2), c.fill(2))
            pe.wait_ge(c.drained(3), c.fill_before(3))
            for t in range(NT):
                last = pe.matmul(bank(s, 3)[:, t * P:(t + 1) * P], ar(s, CT + t * P, P), w(arg[0]), start=True, stop=True)
            last.then_inc(c.fills(3), 1)

        def project_s(c, s, arg):
            a.wait_ge(c.filled(2), c.fill(2))
            a.copy(ar(s, CT, T), bank(s, 2)[:, :]).then_inc(c.drains(2), 1)

        def project_v(c, s, arg):
            dst = flat(X[s][:, :, :] if arg[3] == "X" else W[s][:, :, :])
            if arg[1]:
                d3 = X[s][:, :, :] if arg[3] == "X" else W[s][:, :, :]
                c.link(v.tensor_tensor(d3, d3, over_tokens(row(arg[1])), ALU.add))
            yield
            v.wait_ge(c.filled(3), c.fill(3))
            v.scalar_tensor_tensor(dst, bank(s, 3)[:, :], arg[2], dst, ALU.mult, ALU.add).then_inc(c.drains(3), 1)

        LQ, LK, LV, LE, LF, LS = 0, 512, 1024, 1600, 2112, 2624
        lin = lambda s, at: ar(s, at, T).rearrange("p (t d) -> p t d", t=NT)

        def linear_t(c, s, arg):
            pe.wait_ge(c.drained(0), c.fill_past(0))
            pe.wait_ge(c.drained(0), c.fill_before(0))
            pe.matmul(bank(s, 0)[:, :], w("lin_Wq"), WT[s][:, :], start=True, stop=True).then_inc(c.fills(0), 1)
            for b, name in ((1, "lin_Wk"), (2, "lin_Wv")):
                pe.wait_ge(c.drained(b), c.fill_before(b))
                for t in range(NT):
                    last = pe.matmul(bank(s, b)[:, t * P:(t + 1) * P], WT[s][:, t * P:(t + 1) * P], w(name), start=True, stop=True)
                last.then_inc(c.fills(b), 1)
            yield
            pe.wait_ge(c.sem("features"), c.nth("features"))
            pe.wait_ge(c.drained(3), c.fill_before(3))
            va = ar(s, LV, NT * (P + 1)).rearrange("p (t d) -> p t d", t=NT)
            for t in range(NT):
                last = pe.matmul(bank(s, 3)[:, 0:P + 1], lin(s, LK)[:, t, :], va[:, t, :], start=t == 0, stop=t == NT - 1)
            last.then_inc(c.fills(3), 1)
            yield
            pe.wait_ge(c.sem("kv"), c.nth("kv"))
            for b in range(2):
                pe.wait_ge(c.drained(b), c.fill_before(b, 1))
                for t in range(2):
                    tok = 2 * b + t
                    last = pe.matmul(bank(s, b)[:, t * 144:(t + 1) * 144], ar(s, LQ + tok * P, P), ar(s, LS, 144), start=True, stop=True)
                last.then_inc(c.fills(b), 1)

        def linear_v(c, s, arg):
            va = ar(s, LV, NT * (P + 1)).rearrange("p (t d) -> p t d", t=NT)
            v.memset(va[:, :, P:P + 1], 1.0)
            v.wait_ge(c.filled(0), c.fill(0))
            v.tensor_scalar(ar(s, LQ, T), bank(s, 0)[:, :], w("bq_lin"), None, ALU.add).then_inc(c.drains(0), 1)
            v.wait_ge(c.filled(1), c.fill(1))
            v.tensor_tensor(lin(s, LK), bank(s, 1)[:, :].rearrange("p (t d) -> p t d", t=NT), over_tokens(row("lin_bk")), ALU.add).then_inc(c.drains(1), 1)
            v.wait_ge(c.drained(0), c.fill(0))
            v.wait_ge(c.drained(1), c.fill(1))
            v.tensor_scalar(ar(s, LE, T), ar(s, LQ, T), 0.0, None, ALU.min)
            v.tensor_scalar(ar(s, LF, T), ar(s, LK, T), 0.0, None, ALU.min).then_inc(c.raises("negative"), 1)
            v.wait_ge(c.filled(2), c.fill(2))
            v.tensor_tensor(va[:, :, 0:P], bank(s, 2)[:, :].rearrange("p (t d) -> p t d", t=NT), over_tokens(row("lin_bv")), ALU.add).then_inc(c.drains(2), 1)
            v.wait_ge(c.sem("elu"), c.nth("elu"))
            v.scalar_tensor_tensor(ar(s, LQ, T), ar(s, LQ, T), 0.0, ar(s, LE, T), ALU.max, ALU.add)
            v.scalar_tensor_tensor(ar(s, LK, T), ar(s, LK, T), 0.0, ar(s, LF, T), ALU.max, ALU.add).then_inc(c.raises("features"), 1)
            yield
            v.wait_ge(c.filled(3), c.fill(3))
            c.link(v.tensor_copy(ar(s, LS + 144, 1), bank(s, 3)[:, P:P + 1]))
            v.tensor_scalar(ar(s, LS + P, H), const("block16"), ar(s, LS + 144, 1), None, ALU.mult)
            v.tensor_tensor(ar(s, LS, P), bank(s, 3)[:, 0:P], const("blocks"), ALU.mult).then_inc(c.drains(3), 1)
            v.wait_ge(c.drained(3), c.fill(3))
            v.memset(ar(s, LS + 145, 1), 0.0).then_inc(c.raises("kv"), 1)
            yield
            for b in range(2):
                v.wait_ge(c.filled(b), c.fill(b, 1))
                src = bank(s, b)[:, 0:288].rearrange("p (t k) -> p t k", t=2)
                rec = ar(s, REC, 2 * H).rearrange("p (t h) -> p t h", t=2)
                c.link(v.tensor_scalar(rec, src[:, :, P:P + H], 1e-6, None, ALU.add))
                c.link(v.reciprocal(rec, rec))
                ins = v.tensor_tensor(context(s)[:, 2 * b:2 * b + 2, :].rearrange("p t (h d) -> p t h d", h=H),
                                      src[:, :, 0:P].rearrange("p t (h d) -> p t h d", h=H),
                                      rec.unsqueeze(3).to_broadcast([P, 2, H, HD]), ALU.mult)
                ins.then_inc(c.drains(b), 1)
                v.wait_ge(c.drained(b), c.fill(b, 1))
            v.memset(ar(s, LS + 145, 1), 0.0).then_inc(c.raises("context"), 1)

        def linear_s(c, s, arg):
            a.wait_ge(c.sem("negative"), c.nth("negative"))
            a.activation(ar(s, LE, 2 * T), ar(s, LE, 2 * T), ACT.Exp).then_inc(c.raises("elu"), 1)

        def split_rows(c, s, src, at, name, drain=None):
            parts = three(s, at)
            order = (0, 1, 2) if at == QP else (2, 1, 0)
            split3(c, src, [parts[:, k, :] for k in order], ar(s, TMP, T), drain).then_inc(c.raises(name), 1)

        def stack_p(c, s, arg):
            g.wait_ge(c.sem("normed"), c.past("normed"))
            g.memset(ar(s, KS, HP * T // 2), ONES_WORD).then_inc(c.raises("ones"), 1)

        def stack_y(c, s, arg):
            half = P // 2
            for n, (parts_at, at, name) in enumerate(((QP, QS, "q_parts"), (KP, KS, "k_parts"))):
                if n:
                    yield
                nc.sync.wait_ge(c.sem(name), c.past(name))
                for par in range(2):
                    nc.sync.dma_start(parts_dram[s][n][par].rearrange("k p t -> p k t"),
                                             three(s, parts_at)[half * par:half * par + half, :, :]).then_inc(c.raises("parts_out", 16), 16)
                nc.sync.wait_ge(c.sem("parts_out"), c.nth("parts_out", 32 * (n + 1)))
                if n:
                    nc.sync.wait_ge(c.sem("ones"), c.nth("ones"))
                for par in range(2):
                    src = parts_dram[s][n][par].rearrange("k (r a) t -> (k r) a t", a=HP)
                    for first, run in RUNS:
                        lo = 64 * par + first * HD
                        skip = 0 if n == 0 else (3 - run) * HD
                        nc.sync.dma_start(stacks(s, at)[lo:lo + run * HD, :, :], src[skip:skip + run * HD, :, :]).then_inc(c.raises("stacked", 16), 16)

        RC, RSN, RR, KD, KDT, RS = PROBS, PROBS + T, PROBS, PROBS + 2 * T, PROBS + 3 * T, PROBS + 3 * T + 384
        value = lambda s: ar(s, VA, T).rearrange("p (t d) -> p t d", t=NT)
        chunks = lambda ap: ap.rearrange("p (c n) -> p c n", c=NT)

        def tables_y(c, s, arg):
            nc.sync.wait_ge(c.sem("normed"), c.past("normed"))
            for k in range(2):
                nc.sync.dma_start(ar(s, RC + T * k, T), tables[arg + k, :, :]).then_inc(c.raises("table", 16), 16)

        def rotary_t(c, s, names):
            for b, name in enumerate(names):
                pe.wait_ge(c.drained(b), c.fill_before(b))
                pe.matmul(bank(s, b)[:, :], w(name), WT[s][:, :], start=True, stop=True).then_inc(c.fills(b), 1)

        def rotary_v(c, s, biases):
            v.wait_ge(c.sem("table"), c.nth("table", 32))
            for n, dst in enumerate((QF, KF)):
                if n:
                    v.wait_ge(c.sem("rotated"), c.nth("rotated"))
                for k in range(2):
                    b = 2 * n + k
                    v.wait_ge(c.filled(b), c.fill(b))
                    out_ap, table = ar(s, TMP + T * k, T), ar(s, RC + T * k, T)
                    if biases:
                        ins = v.scalar_tensor_tensor(out_ap, bank(s, b)[:, :], w(biases[b]), table, ALU.add, ALU.mult)
                    else:
                        ins = v.tensor_tensor(out_ap, bank(s, b)[:, :], table, ALU.mult)
                    ins.then_inc(c.drains(b), 1)
                    v.wait_ge(c.drained(b), c.fill(b))
                v.tensor_tensor(ar(s, dst, T), ar(s, TMP, T), ar(s, TMP2, T), ALU.add).then_inc(c.raises("rotated"), 1)

        def ret_in_t(c, s, arg):
            pe.wait_ge(c.drained(0), c.fill_past(0))
            rotary_t(c, s, ("ret_Wq", "ret_Wq_rot", "ret_Wk", "ret_Wk_rot"))
            for b, name in ((0, "ret_Wv"), (1, "ret_Wg")):
                pe.wait_ge(c.drained(b), c.fill_before(b, 1))
                for t in range(NT):
                    last = pe.matmul(bank(s, b)[:, t * P:(t + 1) * P], WT[s][:, t * P:(t + 1) * P], w(name), start=True, stop=True)
                last.then_inc(c.fills(b), 1)
            yield
            pe.wait_ge(c.sem("k_decayed"), c.nth("k_decayed"))
            pe.wait_ge(c.drained(2), c.fill_before(2, 1))
            for t in range(NT - 1):
                last = pe.matmul(bank(s, 2)[:, t * P:(t + 1) * P], ar(s, KD + t * P, P), I, is_transpose=True, start=True, stop=True)
            last.then_inc(c.fills(2), 1)
            pe.wait_ge(c.drained(0), c.fill(0, 1))
            pe.wait_ge(c.drained(2), c.fill(2, 1))
            pe.wait_ge(c.drained(3), c.fill_before(3, 1))
            for t in range(NT - 1):
                last = pe.matmul(bank(s, 3)[:, t * P:(t + 1) * P], ar(s, KDT + t * P, P), value(s)[:, t, :], start=True, stop=True)
            last.then_inc(c.fills(3), 1)

        def ret_in_s(c, s, arg):
            a.wait_ge(c.filled(0), c.fill(0, 1))
            a.copy(flat(value(s)), bank(s, 0)[:, :]).then_inc(c.drains(0), 1)
            a.wait_ge(c.filled(1), c.fill(1, 1))
            a.copy(ar(s, CT, T), bank(s, 1)[:, :]).then_inc(c.raises("gate"), 1)
            a.activation(ar(s, CN, T), bank(s, 1)[:, :], ACT.Tanh, scale=0.5).then_inc(c.drains(1), 1)
            yield
            a.wait_ge(c.filled(2), c.fill(2, 1))
            a.copy(ar(s, KDT, 384), bank(s, 2)[:, 0:384]).then_inc(c.drains(2), 1)

        def ret_in_v(c, s, arg):
            rotary_v(c, s, None)
            v.wait_ge(c.sem("rotated"), c.nth("rotated", 2))
            v.tensor_tensor(chunks(ar(s, KD, T)), chunks(ar(s, KF, T)), over_tokens(const("k_decay")), ALU.mult).then_inc(c.raises("k_decayed"), 1)
            split_rows(c, s, ar(s, QF, T), QP, "q_parts")
            yield
            v.wait_ge(c.sem("q_parts"), c.nth("q_parts"))
            split_rows(c, s, ar(s, KF, T), KP, "k_parts")
            v.wait_ge(c.sem("gate"), c.nth("gate"))
            v.wait_ge(c.drained(1), c.fill(1, 1))
            c.link(v.scalar_tensor_tensor(ar(s, CT, T), ar(s, CN, T), 1.0, ar(s, CT, T), ALU.add, ALU.mult))
            v.wait_ge(c.sem("k_parts"), c.nth("k_parts"))
            v.tensor_tensor(chunks(ar(s, TMP, T)), chunks(ar(s, QF, T)), over_tokens(const("q_decay")), ALU.mult).then_inc(c.raises("q_decayed"), 1)
            v.wait_ge(c.filled(3), c.fill(3, 1))
            for k in range(3):
                src = bank(s, 3)[:, k * P:(k + 1) * P]
                dst = ar(s, RS + k * P, P)
                ins = v.tensor_tensor(dst, src, const("blocks"), ALU.mult)
                if k == 2:
                    ins.then_inc(c.drains(3), 1)
                    v.wait_ge(c.drained(3), c.fill(3, 1))
                else:
                    c.link(ins)
                if k:
                    ins = v.scalar_tensor_tensor(dst, ar(s, RS + (k - 1) * P, P), const("gamma_chunk"), dst, ALU.mult, ALU.add)
                    if k < 2:
                        c.link(ins)
                    else:
                        ins.then_inc(c.raises("entering"), 1)

        def ret_head_t(c, s, h):
            if h == 0:
                pe.wait_ge(c.sem("stacked"), c.past("stacked"))
                pe.wait_ge(c.sem("q_decayed"), c.past("q_decayed"))
                pe.wait_ge(c.sem("entering"), c.past("entering"))
                pe.wait_ge(c.drained(2), c.fill_before(2))
                for t in range(1, NT):
                    pe.matmul(bank(s, 2)[:, t * P:(t + 1) * P], ar(s, TMP + t * P, P), ar(s, RS + (t - 1) * P, P),
                              start=t == 1, stop=True, skip_group_check=True)
            r = head_rows(h, NSTACK)
            pe.wait_ge(c.drained(0), c.fill_before(0))
            for t in range(NT):
                last = pe.matmul(bank(s, 0)[:, t * P:(t + 1) * P], stacks(s, KS)[r, h // 2, t * P:(t + 1) * P],
                                 stacks(s, QS)[r, h // 2, t * P:(t + 1) * P], start=True, stop=True)
            last.then_inc(c.fills(0), 1)
            if h:
                ret_values(c, s, h - 1)

        def ret_values(c, s, h):
            pe.wait_ge(c.drained(0), c.fill_past(0))
            for t in range(NT):
                last = pe.matmul(bank(s, 2)[:, t * P + h * HD:t * P + (h + 1) * HD], ar(s, RR + T * (h % 2) + t * P, P),
                                 value(s)[:, t, h * HD:(h + 1) * HD], start=False,
                                 stop=True, skip_group_check=True)
            if h == H - 1:
                last.then_inc(c.fills(2), 1)
            else:
                last.then_inc(c.raises("retained"), 1)

        def ret_head_v(c, s, h):
            if h >= 2:
                v.wait_ge(c.sem("retained"), c.past("retained", 0))
            v.wait_ge(c.filled(0), c.fill(0))
            v.tensor_tensor(chunks(ar(s, RR + T * (h % 2), T)), chunks(bank(s, 0)[:, :]),
                                    over_tokens(const("decay", h * P, P)), ALU.mult).then_inc(c.drains(0), 1)

        def ret_out_t(c, s, arg):
            ret_values(c, s, H - 1)

        def ret_out_v(c, s, arg):
            groups = lambda ap: ap.rearrange("p (n d) -> p n d", d=HD)
            wide = lambda ap: ap.unsqueeze(2).to_broadcast([P, NT * H, HD])
            mean, sq = ar(s, NM, NT * H), ar(s, TMP2, T)
            o = ar(s, CN, T)
            v.wait_ge(c.filled(2), c.fill(2))
            c.link(v.tensor_reduce(mean, groups(bank(s, 2)[:, :]), AXX, ALU.add))
            c.link(v.tensor_scalar(mean, mean, 1.0 / HD, None, ALU.mult))
            v.tensor_tensor(groups(o), groups(bank(s, 2)[:, :]), wide(mean), ALU.subtract).then_inc(c.drains(2), 1)
            v.wait_ge(c.drained(2), c.fill(2))
            c.link(v.tensor_tensor(sq, o, o, ALU.mult))
            c.link(v.tensor_reduce(mean, groups(sq), AXX, ALU.add))
            v.tensor_scalar(mean, mean, 1.0 / HD, 1e-5, ALU.mult, ALU.add).then_inc(c.raises("var"), 1)
            yield
            v.wait_ge(c.sem("rstd"), c.nth("rstd"))
            c.link(v.tensor_tensor(groups(o), groups(o), wide(ar(s, NMP, NT * H)), ALU.mult))
            for ins in ((row("gn_w"), ALU.mult), (row("gn_b"), ALU.add)):
                c.link(v.tensor_tensor(context(s), context(s), over_tokens(ins[0]), ins[1]))
            v.tensor_tensor(o, o, ar(s, CT, T), ALU.mult).then_inc(c.raises("context"), 1)

        def ret_out_p(c, s, arg):
            g.wait_ge(c.sem("var"), c.nth("var"))
            g.tensor_tensor(ar(s, NMP, NT * H), ar(s, NM, NT * H), mhalf64[:, :], ALU.pow).then_inc(c.raises("rstd"), 1)

        def query_tiles(causal, kt):
            return kt * P if causal else 0

        def row_max_t(c, s, arg):
            h, causal = arg
            if h == 0:
                pe.wait_ge(c.sem("stacked"), c.past("stacked"))
            r = head_rows(h, NSTACK)
            for qt in range(NT):
                n = (qt + 1) * P if causal else T
                pe.wait_ge(c.drained(qt), c.fill_before(qt))
                last = pe.matmul(bank(s, qt)[:, 0:n], stacks(s, QS)[r, h // 2, qt * P:(qt + 1) * P],
                                 stacks(s, KS)[r, h // 2, 0:n], start=True, stop=not causal)
                if causal:
                    last = pe.matmul(bank(s, qt)[:, qt * P:n], identb[:, :], maskb[:, 0, :], start=False, stop=True)
                last.then_inc(c.fills(qt), 1)
                if qt == 1:
                    yield

        def row_max_v(c, s, arg):
            h, causal = arg
            for qt in range(NT):
                n = (qt + 1) * P if causal else T
                v.wait_ge(c.filled(qt), c.fill(qt))
                v.tensor_reduce(minus_max(s)[:, qt, h:h + 1], bank(s, qt)[:, 0:n], AXX, ALU.max, negate=True).then_inc(c.drains(qt), 1)
                if qt == 1:
                    yield

        def max_rows_v(c, s, arg):
            for b in range(4):
                v.wait_ge(c.drained(b), c.fill_past(b))
            split3(c, minus_max(s), [max_parts(s)[:, :, k, :] for k in range(3)],
                          ar(s, NMR, NT * H).rearrange("p (t h) -> p t h", t=NT)).then_inc(c.raises("max_parts"), 1)

        def max_rows_t(c, s, arg):
            pe.wait_ge(c.sem("max_parts"), c.nth("max_parts"))
            pe.wait_ge(c.drained(0), c.fill_before(0))
            for t in range(NT):
                last = pe.matmul(bank(s, 0)[0:3 * H, t * P // 2:(t + 1) * P // 2].bitcast(BF16),
                                 max_parts(s)[:, t, :, :].rearrange("p k h -> p (k h)"), identb[:, :],
                                 is_transpose=True, start=True, stop=True)
            last.then_inc(c.fills(0), 1)

        def max_rows_s(c, s, arg):
            a.wait_ge(c.filled(0), c.fill(0))
            a.copy(maxT(s), bank(s, 0)[0:3 * H, 0:T // 2].bitcast(BF16)).then_inc(c.drains(0), 1)

        def max_rows_y(c, s, arg):
            nc.sync.wait_ge(c.drained(0), c.fill(0))
            nc.sync.dma_start(max_dram[s], maxT(s)).then_inc(c.raises("max_out", 16), 16)
            nc.sync.wait_ge(c.sem("max_out"), c.nth("max_out", 16))
            src = max_dram[s].rearrange("(k a h) t -> h k a t", k=3, a=HP)
            for par in range(2):
                lo = 64 * par + NSTACK
                nc.sync.dma_start(stacks(s, QS)[lo:lo + 3, :, :], src[par, :, :, :]).then_inc(c.raises("max_stacked", 16), 16)

        gathered = lambda s, g: ar(s, TMP + T * (g % 2), T)[0:GROUP_ROWS, :]

        def attend_t(c, s, arg):
            h, causal = arg
            if h == 0:
                pe.wait_ge(c.sem("max_stacked"), c.past("max_stacked"))
            r = head_rows(h, NMAX)
            for kt in range(NT):
                q0 = query_tiles(causal, kt)
                b = kt % 2
                pe.wait_ge(c.drained(b), c.fill_before(b, kt // 2))
                last = pe.matmul(bank(s, b)[:, 0:T - q0], stacks(s, KS)[r, h // 2, kt * P:(kt + 1) * P],
                                 stacks(s, QS)[r, h // 2, q0:T], start=True, stop=not causal)
                if causal:
                    last = pe.matmul(bank(s, b)[:, 0:P], identb[:, :], maskb[:, 1, :], start=False, stop=True)
                last.then_inc(c.fills(b), 1)
                if kt >= 2:
                    pe.wait_ge(c.drained(kt - 2), c.fill(kt - 2))
                    attend_values(c, s, h, kt - 2, causal)
                elif h:
                    pe.wait_ge(c.drained(kt), c.fill_past(kt))
                    attend_values(c, s, h - 1, kt + 2, causal)
                if h > 1 and h % 4 == 1 and kt == 1:
                    turn_group(c, s, h // 4 - 1, True)
                if kt == 1:
                    yield

        def attend_values(c, s, h, kt, causal):
            b = 2 + h // 4 % 2
            if h % 4 == 0 and kt == 0:
                pe.wait_ge(c.drained(b), c.fill_before(b))
                pe.matmul(bank(s, b)[:, :], zerob[0:1, :], identb[0:1, 0:1].to_broadcast([1, T]), start=True, stop=True)
            q0 = query_tiles(causal, kt)
            at = 32 * (h % 4)
            pe.matmul(bank(s, b)[at:at + HD + 1, q0:T], vaug(s)[:, kt, h, :], prob(s, kt)[:, 0:T - q0],
                             start=False, stop=True, skip_group_check=True).then_inc(c.raises("multiplied"), 1)

        def turn_group(c, s, g, past):
            if past:
                pe.wait_ge(c.sem("gathered"), c.past("gathered"))
            else:
                pe.wait_ge(c.sem("gathered"), c.nth("gathered"))
            for t in range(NT):
                last = pe.matmul(bank(s, 2 + g % 2)[:, t * P:t * P + GROUP_ROWS], gathered(s, g)[:, t * P:(t + 1) * P],
                                 I[0:GROUP_ROWS, 0:GROUP_ROWS], is_transpose=True, start=True, stop=True)
            last.then_inc(c.fills(2 + g % 2), 1)

        def gather_s(c, s, g):
            a.wait_ge(c.sem("multiplied"), c.nth("multiplied", 2))
            if g >= 2:
                a.wait_ge(c.filled(2 + g % 2), c.fill_past(2 + g % 2))
            a.copy(gathered(s, g), bank(s, 2 + g % 2)[0:GROUP_ROWS, :]).then_inc(c.raises("gathered"), 1)

        def divide_v(c, s, g):
            v.wait_ge(c.filled(2 + g % 2), c.fill(2 + g % 2))
            src = bank(s, 2 + g % 2)[:, :].rearrange("p (t h d) -> p t h d", t=NT, h=4)
            rec = ar(s, REC + 4 * NT * g, 4 * NT).rearrange("p (t h) -> p t h", t=NT)
            c.link(v.reciprocal(rec, src[:, :, :, HD]))
            v.tensor_tensor(context(s)[:, :, 32 * g:32 * g + 32].rearrange("p t (h d) -> p t h d", h=4),
                                    src[:, :, :, 0:HD], rec.unsqueeze(3).to_broadcast([P, NT, 4, HD]), ALU.mult).then_inc(c.drains(2 + g % 2), 1)

        def attend_s(c, s, arg):
            h, causal = arg
            for kt in range(NT):
                n = T - query_tiles(causal, kt)
                a.wait_ge(c.filled(kt % 2), c.fill(kt % 2, kt // 2))
                if h and kt < 2:
                    a.wait_ge(c.sem("multiplied"), c.past("multiplied", 1 - kt))
                elif h:
                    a.wait_ge(c.sem("multiplied"), c.nth("multiplied", kt - 1))
                a.activation(prob(s, kt)[:, 0:n], bank(s, kt % 2)[:, 0:n], ACT.Exp, scale=SCORE_SCALE).then_inc(c.drains(kt % 2), 1)
                if kt == 1:
                    yield
            if h and h % 4 == 0:
                gather_s(c, s, h // 4 - 1)

        def attend_v(c, s, arg):
            h, causal = arg
            divide_v(c, s, h // 4 - 1)

        def attended_t(c, s, causal):
            for kt in range(2, NT):
                pe.wait_ge(c.drained(kt - 2), c.fill_past(kt - 2))
                attend_values(c, s, H - 1, kt, causal)
            turn_group(c, s, H // 4 - 1, False)

        def attended_s(c, s, causal):
            gather_s(c, s, H // 4 - 1)

        def attended_v(c, s, arg):
            divide_v(c, s, H // 4 - 1)
            v.wait_ge(c.drained(3), c.fill(3))
            v.memset(ar(s, REC + 64, 1), 0.0).then_inc(c.raises("context"), 1)

        def attn_in_t(c, s, arg):
            pe.wait_ge(c.drained(0), c.fill_past(0))
            for b, name in ((0, "f_Wq"), (1, "f_Wk")):
                pe.wait_ge(c.drained(b), c.fill_before(b))
                pe.matmul(bank(s, b)[:, :], w(name), WT[s][:, :], start=True, stop=True).then_inc(c.fills(b), 1)
            pe.wait_ge(c.drained(2), c.fill_before(2))
            for t in range(NT):
                last = pe.matmul(bank(s, 2)[:, t * P:(t + 1) * P], WT[s][:, t * P:(t + 1) * P], w("f_Wv"), start=True, stop=True)
            last.then_inc(c.fills(2), 1)

        def split_heads(ap):
            return ap.rearrange("p (t h d) -> p t h d", t=NT, h=H)

        def attn_in_v(c, s, arg):
            v.wait_ge(c.filled(0), c.fill(0))
            split_rows(c, s, bank(s, 0)[:, :], QP, "q_parts", (0, 0))
            v.wait_ge(c.sem("q_parts"), c.nth("q_parts"))
            v.wait_ge(c.filled(1), c.fill(1))
            split_rows(c, s, bank(s, 1)[:, :], KP, "k_parts", (1, 0))
            v.memset(vaug(s)[:, :, :, HD:HD + 1], 1.0)
            v.wait_ge(c.filled(2), c.fill(2))
            v.tensor_copy(vaug(s)[:, :, :, 0:HD], split_heads(bank(s, 2)[:, :])).then_inc(c.drains(2), 1)

        HB1, OT1, ACC1, O1 = 0, 4096, 4608, 5120
        h1 = lambda s, e, j: ar(s, HB1 + 2048 * (e % 2) + T * j, T)
        acc1 = lambda s: ar(s, ACC1, T).rearrange("p (t d) -> p t d", t=NT)
        o1 = lambda s: ar(s, O1, T).rearrange("p (t d) -> p t d", t=NT)

        def moe1_in_v(c, s, arg):
            v.wait_ge(c.drained(3), c.fill_past(3))
            c.link(norm_vector(c, s, W[s], o1(s), 1e-6))
            c.link(v.tensor_tensor(o1(s), o1(s), over_tokens(row("f_ln1g")), ALU.mult))
            v.tensor_tensor(o1(s), o1(s), over_tokens(row("f_ln1b")), ALU.add).then_inc(c.raises("normed"), 1)
            yield
            v.wait_ge(c.filled(1), c.fill(1))
            router_v(c, s, bank(s, 1)[:, 0:NT * E].rearrange("p (t e) -> p t e", t=NT), 1, 0, True)

        def moe1_in_p(c, s, arg):
            norm_pool(c, s)

        def moe1_out_p(c, s, arg):
            yield
            norm_pool(c, s)

        def moe1_in_t(c, s, arg):
            pe.wait_ge(c.sem("normed"), c.nth("normed"))
            pe.wait_ge(c.drained(0), c.fill_before(0))
            turn(c, s, o1(s), 0, identity=I)
            yield
            pe.wait_ge(c.drained(0), c.fill(0))
            pe.wait_ge(c.drained(1), c.fill_before(1))
            for t in range(NT):
                last = pe.matmul(bank(s, 1)[:, t * E:(t + 1) * E], ar(s, OT1 + t * P, P), w("f_Wr"), start=True, stop=True)
            last.then_inc(c.fills(1), 1)
            yield
            turn_weights(c, s, 3, 0)

        def moe1_in_s(c, s, arg):
            a.wait_ge(c.filled(0), c.fill(0))
            a.copy(ar(s, OT1, T), bank(s, 0)[:, :]).then_inc(c.drains(0), 1)
            yield
            router_s(c, s, 1, 0, True)
            yield
            a.wait_ge(c.filled(3), c.fill(3))
            a.copy(weightT(s), bank(s, 3)[0:E, :]).then_inc(c.drains(3), 1)

        def moe1_t(c, s, e):
            for j in range(4):
                pe.wait_ge(c.drained(j % 2), c.fill_before(j % 2, j // 2))
                pe.matmul(bank(s, j % 2)[:, :], w("We1", e * H1 + j * P, P), ar(s, OT1, T), start=True, stop=True).then_inc(c.fills(j % 2), 1)
            if e:
                yield
                moe1_second(c, s, e - 1)

        def moe1_second(c, s, e):
            pe.wait_ge(c.drained(1), c.fill_past(1))
            pe.wait_ge(c.drained(2), c.fill_before(2))
            for t in range(NT):
                for j in range(4):
                    last = pe.matmul(bank(s, 2)[:, t * P:(t + 1) * P], h1(s, e, j)[:, t * P:(t + 1) * P],
                                     w("We2", (e * 4 + j) * P, P), start=j == 0, stop=j == 3)
            last.then_inc(c.fills(2), 1)

        def moe1_s(c, s, e):
            if e >= 2:
                a.wait_ge(c.filled(2), c.fill_past(2))
            for j in range(4):
                a.wait_ge(c.filled(j % 2), c.fill(j % 2, j // 2))
                a.activation(h1(s, e, j), bank(s, j % 2)[:, :], ACT.Gelu, bias=w("be1", e * 4 + j, 1)).then_inc(c.drains(j % 2), 1)

        def moe1_v(c, s, e):
            if e:
                yield
                moe1_add(c, s, e - 1)

        def moe1_add(c, s, e):
            v.wait_ge(c.filled(2), c.fill(2))
            if e:
                v.wait_ge(c.drained(2), c.fill_past(2))
            for t in range(NT):
                last = v.scalar_tensor_tensor(acc1(s)[:, t, :], bank(s, 2)[:, t * P:(t + 1) * P], weight(s)[:, t, e:e + 1],
                                              o1(s)[:, t, :] if e == 0 else acc1(s)[:, t, :], ALU.mult, ALU.add)
            last.then_inc(c.drains(2), 1)

        def moe1_out_t(c, s, arg):
            moe1_second(c, s, E - 1)
            pe.wait_ge(c.drained(3), c.fill_before(3))
            for t in range(NT):
                last = pe.matmul(bank(s, 3)[:, t * P:(t + 1) * P], weightT(s)[:, t * P:(t + 1) * P], w("f_b2")[0:E, :],
                                 start=True, stop=True)
            last.then_inc(c.fills(3), 1)

        def moe1_out_v(c, s, arg):
            moe1_add(c, s, E - 1)
            v.wait_ge(c.drained(2), c.fill(2))
            v.wait_ge(c.filled(3), c.fill(3))
            v.tensor_tensor(flat(acc1(s)), flat(acc1(s)), bank(s, 3)[:, :], ALU.add).then_inc(c.drains(3), 1)
            v.wait_ge(c.drained(3), c.fill(3))
            yield
            finish_norm_v(c, s, acc1(s), ar(s, 5632, T).rearrange("p (t d) -> p t d", t=NT), 1e-6, row("f_ln2g"), row("f_ln2b"))

        LATENT = ("bqr", "bqr_rot", "bkr", "bkr_rot")

        def lat_in_t(c, s, arg):
            pe.wait_ge(c.drained(0), c.fill_past(0))
            rotary_t(c, s, ("lat_wqr", "lat_wqr_rot", "lat_wkr", "lat_wkr_rot"))
            yield
            pe.wait_ge(c.drained(0), c.fill_before(0, 1))
            pe.matmul(bank(s, 0)[0:32, :], w("lat_wkv"), WT[s][:, :], start=True, stop=True).then_inc(c.fills(0), 1)
            yield
            pe.wait_ge(c.drained(0), c.fill(0, 1))
            pe.wait_ge(c.drained(1), c.fill_before(1, 1))
            for t in range(NT):
                last = pe.matmul(bank(s, 1)[:, t * P:(t + 1) * P], ar(s, CT + t * P, P)[0:32, :], w("lat_wv")[0:32, :],
                                 start=True, stop=True)
            last.then_inc(c.fills(1), 1)

        def lat_in_s(c, s, arg):
            yield
            for k, at in enumerate((QF, KF)):
                a.wait_ge(c.sem("rotated"), c.nth("rotated", k + 1))
                a.activation(ar(s, at, T), ar(s, at, T), ACT.Gelu).then_inc(c.raises("activated"), 1)
                if k == 0:
                    a.wait_ge(c.filled(0), c.fill(0, 1))
                    a.activation(ar(s, CT, T)[0:32, :], bank(s, 0)[0:32, :], ACT.Gelu, bias=w("bkv")[0:32, :]).then_inc(c.drains(0), 1)

        def lat_in_v(c, s, arg):
            rotary_v(c, s, LATENT)
            yield
            yield
            v.memset(vaug(s)[:, :, :, HD:HD + 1], 1.0)
            v.wait_ge(c.filled(1), c.fill(1, 1))
            bias = row("lat_bv").rearrange("p (h d) -> p h d", h=H)
            v.tensor_tensor(vaug(s)[:, :, :, 0:HD], split_heads(bank(s, 1)[:, :]),
                                    bias.unsqueeze(1).to_broadcast([P, NT, H, HD]), ALU.add).then_inc(c.drains(1), 1)
            v.wait_ge(c.sem("rotated"), c.nth("rotated", 2))
            v.wait_ge(c.sem("activated"), c.nth("activated", 1))
            split_rows(c, s, ar(s, QF, T), QP, "q_parts")
            v.wait_ge(c.sem("q_parts"), c.nth("q_parts"))
            v.wait_ge(c.sem("activated"), c.nth("activated", 2))
            split_rows(c, s, ar(s, KF, T), KP, "k_parts")

        VECTOR = {"norm": norm_v, "mamba_in": mamba_in_v, "mamba_dir": mamba_dir_v, "scan": scan_v, "scan_first": scan_v,
                  "mamba_out": mamba_out_v, "combine": combine_v}
        POOL = {"norm": norm_p, "mamba_in": mamba_in_p, "scan": scan_p, "scan_first": scan_p}
        TENSOR = {"norm": norm_t, "mamba_in": mamba_in_t, "mamba_dir": mamba_dir_t, "scan": scan_t, "scan_first": scan_t,
                  "mamba_out": mamba_out_t, "combine": combine_t}
        SCALAR = {"norm": norm_s, "mamba_in": mamba_in_s, "mamba_dir": mamba_dir_s, "scan": scan_s, "scan_first": scan_s, "combine": combine_s}
        VECTOR.update({"moe0_in": moe0_in_v, "moe0": moe0_v, "moe0_first": moe0_v, "moe0_out": moe0_out_v})
        POOL.update({"moe0_in": moe0_in_p, "moe0_out": moe0_out_p})
        TENSOR.update({"moe0_in": moe0_in_t, "moe0": moe0_t, "moe0_first": moe0_t, "moe0_out": moe0_out_t})
        SCALAR.update({"moe0_in": moe0_in_s, "moe0": moe0_s, "moe0_first": moe0_s})
        VECTOR.update({"project": project_v, "linear": linear_v, "ret_in": ret_in_v, "ret_head_first": ret_head_v,
                       "ret_head": ret_head_v, "ret_out": ret_out_v})
        POOL.update({"stack": stack_p, "ret_out": ret_out_p})
        TENSOR.update({"project": project_t, "linear": linear_t, "ret_in": ret_in_t, "ret_head_first": ret_head_t,
                       "ret_head": ret_head_t, "ret_out": ret_out_t})
        SCALAR.update({"project": project_s, "linear": linear_s, "ret_in": ret_in_s})
        VECTOR.update({"attn_in": attn_in_v, "lat_in": lat_in_v, "row_max": row_max_v, "max_rows": max_rows_v,
                       "attended": attended_v, "moe1_in": moe1_in_v, "moe1": moe1_v, "moe1_out": moe1_out_v})
        POOL.update({"moe1_in": moe1_in_p, "moe1_out": moe1_out_p})
        TENSOR.update({"attn_in": attn_in_t, "lat_in": lat_in_t, "row_max": row_max_t, "max_rows": max_rows_t,
                       "attended": attended_t, "moe1_in": moe1_in_t,
                       "moe1_first": moe1_t, "moe1": moe1_t, "moe1_out": moe1_out_t})
        SCALAR.update({"lat_in": lat_in_s, "max_rows": max_rows_s,
                       "moe1_in": moe1_in_s, "moe1_first": moe1_s, "moe1": moe1_s})
        SYNC = {"lat_in": lambda c, s, arg: tables_y(c, s, 2), "max_rows": max_rows_y, "stack": stack_y, "ret_in": lambda c, s, arg: tables_y(c, s, 0)}
        attend = {kind: attend_t for kind in ("attend_first", "attend_gather", "attend_turn2", "attend_turn3", "attend")}
        TENSOR.update(attend)
        SCALAR.update({kind: attend_s for kind in attend})
        SCALAR["attended"] = attended_s
        VECTOR.update({"attend_turn2": attend_v, "attend_turn3": attend_v})

        setup = setup_sems
        PAIRS = x.shape[0]
        WEIGHT_LOADS = 3 * 16

        ones = arena[0][:, 64:64 + P]
        b1_sq, sq_sum = arena[0][:, 16:32], arena[0][:, 32:40]
        b1_sum = arena[0][:, 40:48]
        w1T = arena[0][:, 256:512]

        block = stack.enter_context(nc.Block())

        @block.sync
        def _(sp):
            sp.dma_start(Ct[:, :], consts).then_inc(setup["weights_loaded"], 16)
            sp.dma_start(Wt[:, :], wts).then_inc(setup["weights_loaded"], 16)
            sp.dma_start(Rt[:, :], rows.to_broadcast([P, R_WIDTH])).then_inc(setup["weights_loaded"], 16)
            def transfers(part, pair, following):
                def load(c, s, arg):
                    sp.dma_start(X[s][:, :, :], x[following if s else pair, s, :, :].rearrange("(t p) d -> p t d", p=P)).then_inc(c.raises("x_loaded", 16), 16)

                def store(c, s, arg):
                    residual_ready(c)
                    sp.dma_start(out[pair, s, :, :].rearrange("(t p) d -> p t d", p=P), X[s][:, :, :]).then_inc(c.raises("x_stored", 16), 16)
                    sp.wait_ge(c.sem("x_stored"), c.nth("x_stored", 16))

                def rest(c, s, arg):
                    residual_ready(c)

                run(sp, None, {"load": load, "store": store, "rest": rest, **SYNC}, part)

            transfers("enter", None, 0)
            leave(sp, clears=True)
            with sp.Fori(0, PAIRS - 1) as pair:
                transfers("pair", pair, pair + 1)
                leave(sp, clears=True)
            transfers("last", PAIRS - 1, None)

        @block.gpsimd
        def _(pool):
            pool.memset(mhalf64[:, :], -0.5).then_inc(setup["mhalf_ready"], 1)
            pool.wait_ge(setup["mhalf_ready"], 1)
            run(pool, chains["gpsimd"], POOL, "enter")
            leave(pool)
            with pool.Fori(0, PAIRS - 1):
                run(pool, chains["gpsimd"], POOL, "pair")
                leave(pool)
            run(pool, chains["gpsimd"], POOL, "last")

        @block.scalar
        def _(act):
            act.wait_ge(setup["weights_loaded"], WEIGHT_LOADS)
            act.activation(w("A"), w("A"), ACT.Exp).then_inc(setup["A_exp"], 1)
            act.wait_ge(setup["halved"], 1)
            run(act, chains["scalar"], SCALAR, "enter")
            leave(act)
            with act.Fori(0, PAIRS - 1):
                run(act, chains["scalar"], SCALAR, "pair")
                leave(act)
            run(act, chains["scalar"], SCALAR, "last")

        @block.vector
        def _(dve):
            c = Cursor(prog, dve, None, 0, 0, setup_chain)
            dve.wait_ge(setup["weights_loaded"], WEIGHT_LOADS)
            for src, dst in ((w("b_in"), half_bin[:, :]), (w("bg"), half_bg[:, :]), (w("conv_w"), w("conv_w")),
                             (w("conv_b"), w("conv_b"))):
                v.tensor_scalar(dst, src, 0.5, None, ALU.mult)
            v.tensor_copy(identb[:, :], I)
            v.memset(zerob[:, :], 0.0)
            v.memset(ones, 1.0)
            v.tensor_reduce(b1_sum, w("b1").rearrange("p (e j) -> p e j", j=2), AXX, ALU.add).then_inc(setup["consts_ready"], 1)
            v.tensor_copy(selb[:, :], const("sel32")[0:96, :])
            v.tensor_copy(sel8b[:, :], const("sel8")[0:3 * E, :])
            v.tensor_copy(maskb[:, 0, :], const("mask_q"))
            v.tensor_copy(maskb[:, 1, :], const("mask_k"))
            dve.wait_ge(setup["A_exp"], 1)
            v.tensor_scalar(w("A"), w("A"), -1.0, None, ALU.mult).then_inc(setup["halved"], 1)
            dve.wait_ge(setup["halved"], 1)
            w1 = w("w1").rearrange("p (e n) -> p e n", e=E)
            mean = arena[0][:, 0:E]
            c.link(v.tensor_reduce(mean, w1, AXX, ALU.add))
            c.link(v.tensor_scalar(mean, mean, 1.0 / H0, None, ALU.mult))
            v.tensor_tensor(w1, w1, mean.unsqueeze(2).to_broadcast([P, E, H0]), ALU.subtract).then_inc(setup["centred"], 1)
            dve.wait_ge(setup["w1_turned"], 1)
            v.scalar_tensor_tensor(w("b1").rearrange("p (e j) -> p e j", j=2), banks[0][0][:, 0:E].unsqueeze(2).to_broadcast([P, E, 2]), -1.0 / H0,
                                   w("b1").rearrange("p (e j) -> p e j", j=2), ALU.mult, ALU.add).then_inc(setup["centred"], 1)
            dve.wait_ge(setup["centred"], 2)
            c.link(v.tensor_tensor(b1_sq, w("b1"), w("b1"), ALU.mult))
            v.tensor_reduce(sq_sum, b1_sq.rearrange("p (e j) -> p e j", j=2), AXX, ALU.add).then_inc(setup["sq_ready"], 1)
            for e in range(E):
                dve.wait_ge(setup["w1_turned"], 2 + e)
                if e:
                    dve.wait_ge(setup["gram"], e)
                v.tensor_copy(w1T, banks[0][1][:, 0:2 * P]).then_inc(setup["w1T_ready"], 1)
                dve.wait_ge(setup["gram"], e + 1)
                v.tensor_scalar(G[:, e, :], banks[0][2][:, 0:P], 1.0 / H0, None, ALU.mult)
                v.tensor_scalar(w("v2", e, 1), banks[0][3][:, 0:1], 2.0 / H0, None, ALU.mult).then_inc(setup["gram_ready"], 1)
            dve.wait_ge(setup["w1_turned"], 2 + E)
            v.tensor_scalar(ce[:, :], banks[0][0][:, 0:E], 1.0 / H0, 1e-5, ALU.mult, ALU.add).then_inc(setup["gram_ready"], 1)
            dve.wait_ge(setup["gram_ready"], E + 1)
            run(dve, chains["vector"], VECTOR, "enter")
            leave(dve)
            with dve.Fori(0, PAIRS - 1):
                run(dve, chains["vector"], VECTOR, "pair")
                leave(dve)
            run(dve, chains["vector"], VECTOR, "last")

        @block.tensor
        def _(ten):
            ten.wait_ge(setup["weights_loaded"], WEIGHT_LOADS)
            ten.wait_ge(setup["halved"], 1)
            ten.wait_ge(setup["consts_ready"], 1)
            pe.matmul(banks[0][0][:, 0:E], ones, b1_sum, start=True, stop=True).then_inc(setup["w1_turned"], 1)
            ten.wait_ge(setup["centred"], 2)
            for e in range(E):
                if e:
                    ten.wait_ge(setup["w1T_ready"], e)
                for j in range(2):
                    last = pe.matmul(banks[0][1][:, j * P:(j + 1) * P], w("w1", e * H0 + j * P, P), I, is_transpose=True,
                                     start=True, stop=True)
                last.then_inc(setup["w1_turned"], 1)
                ten.wait_ge(setup["w1T_ready"], e + 1)
                if e:
                    ten.wait_ge(setup["gram_ready"], e)
                for j in range(2):
                    pe.matmul(banks[0][2][:, 0:P], w1T[:, j * P:(j + 1) * P], w1T[:, j * P:(j + 1) * P], start=j == 0, stop=j == 1)
                for j in range(2):
                    last = pe.matmul(banks[0][3][:, 0:1], w1T[:, j * P:(j + 1) * P], w("b1", e * 2 + j, 1), start=j == 0, stop=j == 1)
                last.then_inc(setup["gram"], 1)
            ten.wait_ge(setup["sq_ready"], 1)
            pe.matmul(banks[0][0][:, 0:E], ones, sq_sum, start=True, stop=True).then_inc(setup["w1_turned"], 1)
            ten.wait_ge(setup["gram_ready"], E + 1)
            run(ten, None, TENSOR, "enter")
            leave(ten)
            with ten.Fori(0, PAIRS - 1):
                run(ten, None, TENSOR, "pair")
                leave(ten)
            run(ten, None, TENSOR, "last")

        prog.check()


def _pack(np, sections, parts):
    out = []
    for name, width in sections:
        a = parts[name]
        a = a.reshape(a.shape[0], -1)
        assert a.shape[1] == width, (name, a.shape, width)
        if a.shape[0] < P:
            a = np.concatenate([a, np.zeros((P - a.shape[0], width), a.dtype)], 0)
        out.append(a)
    return np.ascontiguousarray(np.concatenate(out, 1))


def _head_order(np):
    return np.arange(P).reshape(HP, 2, HD).transpose(1, 2, 0).reshape(-1)


def _constants(np):
    f = np.float32
    p, q = np.arange(P)[:, None], np.arange(P)[None, :]
    gamma = 1.0 - 2.0 ** (-5.0 - np.arange(H))
    order = _head_order(np)
    head, of_value = order // HD, np.arange(P) // HD
    c = {
        "ident": (p == q), "anti": (p + q == P - 1),
        "sel32": np.arange(P)[:, None] % 32 == np.arange(32)[None, :],
        "sel8": np.arange(P)[:, None] % 8 == np.arange(8)[None, :],
        "mask_q": np.where(q > p, MASKED, 0.0), "mask_k": np.where(p > q, MASKED, 0.0),
        "blocks": head[:, None] == of_value[None, :], "block16": head[:, None] == np.arange(H)[None, :],
        "earlier": np.broadcast_to((np.arange(E)[None, :] < np.arange(E)[:, None]).reshape(1, -1), (P, E * E)),
        "gamma_chunk": (gamma[head] ** P)[:, None],
        "k_decay": gamma[head][:, None] ** (P - q), "q_decay": gamma[head][:, None] ** q * SCORE_SCALE,
        "decay": np.where((q >= p)[:, None, :], gamma[None, :, None] ** np.maximum(q - p, 0)[:, None, :], 0.0) * SCORE_SCALE,
    }
    packed = _pack(np, CONSTS, {k: np.asarray(v, dtype=f) for k, v in c.items()})

    def rope(width, features):
        inv = (1.0 / f(10000.0) ** (np.arange(0, width, 2, dtype=f) / f(width))).astype(f)
        freqs = (np.arange(T, dtype=f)[:, None] * inv[None, :]).astype(f)
        emb = np.concatenate([freqs, freqs], -1)
        cos, sin = np.cos(emb).astype(f), np.sin(emb).astype(f)
        sin = sin * np.where(np.arange(width) < width // 2, f(-1), f(1))[None, :]
        return np.tile(cos, (1, features // width)).T, np.tile(sin, (1, features // width)).T

    tables = np.stack([*rope(HD, P), *rope(P, P)]).astype(f)
    return packed, np.ascontiguousarray(tables[:, order, :])


def _weights(np, i):
    def halves(a):
        return a.reshape(2, P, -1).transpose(1, 0, 2)

    def per_dir(name, rows):
        a = i["L0_attn_a_" + name]
        return np.stack([a[d].reshape(-1, P).T for d in range(2)], 1) if rows else a

    A = "L0_attn_a_"
    order = _head_order(np)
    rot8 = np.concatenate([np.roll(np.arange(HD * h, HD * h + HD), HD // 2) for h in range(H)])
    rot8, rot = rot8[order], np.roll(np.arange(P), P // 2)[order]
    col = lambda a: a.reshape(-1, P).T
    both = lambda a, fn: np.stack([fn(a[d]) for d in range(2)], 1)
    F0, F1, R, L, N = "L0_ffn_", "L1_ffn_", "L1_attn_a_", "L1_attn_b_", "L0_attn_b_"
    return {
        "ln_w": i[A + "ln_w"].T, "ln_b": i[A + "ln_b"].T, "b_in": both(i[A + "b_in"], col),
        "conv_w": both(i[A + "conv_w"], halves), "conv_b": both(i[A + "conv_b"], col),
        "b_dt": both(i[A + "b_dt"], col), "A": both(i[A + "A_log"], halves), "D": both(i[A + "D"], col),
        "b_out": i[A + "b_out"].T, "bg": col(i[A + "bg"]), "bv": col(i[A + "bv"]), "bq_lin": col(i[N + "bq"])[order],
        "b1": i[F0 + "b1"].reshape(-1, P).T, "g1": i[F0 + "ln1_g"].reshape(-1, P).T,
        "be_ln1": i[F0 + "ln1_b"].reshape(-1, P).T, "be1": i[F1 + "be1"].reshape(-1, P).T,
        "bqr": col(i[L + "bqr"])[order], "bqr_rot": col(i[L + "bqr"])[rot], "bkr": col(i[L + "bkr"])[order],
        "bkr_rot": col(i[L + "bkr"])[rot], "bkv": i[L + "bkv"].reshape(-1, 1),
        "W_in": both(i[A + "W_in"], lambda a: a), "W_x": both(i[A + "W_xproj"], halves),
        "W_dt": both(i[A + "W_dt"], lambda a: a), "W_out": both(i[A + "W_out"], halves),
        "Wg": halves(i[A + "Wg"]), "Wv": halves(i[A + "Wv"]),
        "gate_w": i[F0 + "gate_w"], "v2": np.zeros((P, E), np.float32),
        "w1": i[F0 + "w1"].transpose(1, 0, 2), "w2": i[F0 + "w2"].reshape(E, 2, P, P).transpose(2, 0, 1, 3),
        "b2": i[F0 + "b2"],
        "lin_Wq": i[N + "Wq"].T[:, order], "lin_Wk": i[N + "Wk"].T[:, order], "lin_Wv": i[N + "Wv"].T, "lin_Wo": i[N + "Wo"].T,
        "ret_Wq": i[R + "Wq"].T[:, order], "ret_Wq_rot": i[R + "Wq"].T[:, rot8], "ret_Wk": i[R + "Wk"].T[:, order],
        "ret_Wk_rot": i[R + "Wk"].T[:, rot8], "ret_Wv": i[R + "Wv"].T, "ret_Wg": i[R + "Wg"].T,
        "ret_Wo": i[R + "Wo"].T,
        "f_Wq": i[F1 + "Wq"][:, order], "f_Wk": i[F1 + "Wk"][:, order], "f_Wv": i[F1 + "Wv"], "f_Wo": i[F1 + "Wo"],
        "f_Wr": i[F1 + "Wr"], "f_b2": i[F1 + "be2"],
        "lat_wqr": i[L + "wqr"][:, order], "lat_wqr_rot": i[L + "wqr"][:, rot], "lat_wkr": i[L + "wkr"][:, order],
        "lat_wkr_rot": i[L + "wkr"][:, rot], "lat_wkv": i[L + "wkv"], "lat_wv": i[L + "wv"], "lat_wo": i[L + "wo"],
        "We1": i[F1 + "We1"].transpose(1, 0, 2), "We2": i[F1 + "We2"].reshape(E, 4, P, P).transpose(2, 0, 1, 3),
    }, {
        "lin_bk": i[N + "bk"].reshape(-1)[order], "lin_bv": i[N + "bv"], "lin_bo": i[N + "bo"], "ln_g": i[F0 + "ln_g"], "ln_be": i[F0 + "ln_b"],
        "gn_w": i[R + "gn_w"], "gn_b": i[R + "gn_b"], "f_bo": i[F1 + "bo"], "f_ln1g": i[F1 + "ln1_g"],
        "f_ln1b": i[F1 + "ln1_b"], "f_ln2g": i[F1 + "ln2_g"], "f_ln2b": i[F1 + "ln2_b"],
        "lat_bv": i[L + "bv"], "lat_bo": i[L + "bo"],
    }


def kernel(**inputs):
    import numpy as np
    import concourse.bacc as bacc
    from concourse.bass_utils import run_bass_kernel_spmd

    i = {k: np.asarray(v) for k, v in inputs.items()}
    weights, rows = _weights(np, i)
    consts, tables = _constants(np)
    x = i["L0_attn_a_x"]
    arrays = {
        "x": np.ascontiguousarray(x.reshape(x.shape[0] // SLOTS, SLOTS, T, P)),
        "wts": _pack(np, WEIGHTS, weights),
        "rows": np.ascontiguousarray(np.concatenate([rows[n].reshape(1, -1) for n, _ in ROWS], 1)),
        "consts": consts, "tables": tables,
    }
    nc = bacc.Bacc("TRN2", target_bir_lowering=False, num_devices=1)
    ins = [nc.dram_tensor("in_" + n, a.shape, FP32, kind="ExternalInput").ap() for n, a in arrays.items()]
    out = nc.dram_tensor("out", arrays["x"].shape, FP32, kind="ExternalOutput").ap()
    network(nc, *ins, out)
    r = run_bass_kernel_spmd(nc, [{"in_" + n: a for n, a in arrays.items()}], core_ids=[0])
    return r.results[0]["out"].reshape(x.shape)
```
